# Optimizing a Trainium2 kernel written in Bass

```python
import numpy as np
import jax
import jax.numpy as jnp

def _softmax(x, axis=-1):
    return jax.nn.softmax(x, axis=axis)

def _gelu(x):
    return jax.nn.gelu(x, approximate=True)

def _silu(x):
    return jax.nn.silu(x)

def _sigmoid(x):
    return jax.nn.sigmoid(x)

def _layernorm(x, axis=-1, eps=1e-05):
    m = jnp.mean(x, axis=axis, keepdims=True)
    v = jnp.var(x, axis=axis, keepdims=True)
    return (x - m) / jnp.sqrt(v + eps)

def _scatter_add(tgt, idx, src, axis=0):
    return tgt.at[idx].add(src)

def _segment_sum(src, seg, n):
    return jax.ops.segment_sum(src, seg, n)
kernel_name = 'mk_flamingo_gated_d1_seqx_r4_54f71f'

def setup_inputs(seed: int=0):
    np.random.seed(seed)
    _w = jnp.asarray

    def _rec_inputs():
        import jax
        import jax.numpy as jnp
        _rk = jax.random.key(seed)
        x = 7.22e-05 + 1 * jax.random.normal(jax.random.fold_in(_rk, 1), (1, 2048, 256), jnp.float32)
        _lenS = 2048 - jax.random.randint(jax.random.fold_in(_rk, 7), (1,), 0, max(1, 2048 // 4) + 1, jnp.int32)
        _lenS2 = 1601 - jax.random.randint(jax.random.fold_in(_rk, 8), (1,), 0, max(1, 1601 // 4) + 1, jnp.int32)
        _ctx_1024P = jax.random.normal(jax.random.fold_in(_rk, 11), (1, 16, 256), jnp.float32)
        _ctx_1024c = jax.random.dirichlet(jax.random.fold_in(_rk, 511), 0.3 * jnp.ones((16,), jnp.float32), (1, 1601))
        _ctx_1024t = jnp.einsum('bsk,bkd->bsd', _ctx_1024c, _ctx_1024P)
        _ctx_1024t = _ctx_1024t * jax.lax.rsqrt(jnp.mean(jnp.square(_ctx_1024t)) + 1e-12) * 0.953939
        ctx_1024 = 4.13588e-05 + 0.999923 * (_ctx_1024t + 0.3 * jax.random.normal(jax.random.fold_in(_rk, 611), (1, 1601, 256), jnp.float32))
        _g = jax.random.normal(jax.random.fold_in(_rk, 9001), (2, 1), jnp.float32)
        _g = jnp.sign(_g) * jnp.maximum(jnp.abs(_g), 1.0) + (_g == 0) * 1.0
        g_xattn = _g[0]
        g_ffn = _g[1]
        return (x, ctx_1024, g_xattn, g_ffn)
    x, ctx_1024, g_xattn, g_ffn = _rec_inputs()

    def _L0_xattn_setup():
        import jax, jax.numpy as jnp
        import numpy as np
        D_MODEL = 256
        H = 16
        D_K = D_MODEL // H
        key = jax.random.key(seed)
        ks = jax.random.split(key, 7)
        B, S = (4, 512)
        q = jax.random.normal(ks[0], (B, S, D_MODEL), dtype=jnp.float32)
        k = jax.random.normal(ks[1], (B, S, D_MODEL), dtype=jnp.float32)
        v = jax.random.normal(ks[2], (B, S, D_MODEL), dtype=jnp.float32)
        scale = 1.0 / np.sqrt(D_MODEL)
        w_q = jax.random.normal(ks[3], (D_MODEL, D_MODEL), dtype=jnp.float32) * scale
        w_k = jax.random.normal(ks[4], (D_MODEL, D_MODEL), dtype=jnp.float32) * scale
        w_v = jax.random.normal(ks[5], (D_MODEL, D_MODEL), dtype=jnp.float32) * scale
        w_o = jax.random.normal(ks[6], (D_MODEL, D_MODEL), dtype=jnp.float32) * scale
        return {'q': q, 'k': k, 'v': v, 'w_q': w_q, 'w_k': w_k, 'w_v': w_v, 'w_o': w_o}
    _L0_xattn_all = _L0_xattn_setup()
    _L0_xattn_in = {k: v for k, v in _L0_xattn_all.items() if k in ('w_q', 'w_k', 'w_v', 'w_o')}
    del _L0_xattn_all

    def _L0_ffn_setup():
        import jax, jax.numpy as jnp
        import numpy as np
        H = 256
        I = 176
        E = 64
        TOP_K = 8
        NG = 8
        TOPK_GROUP = 4
        N_SHARED = 2
        ROUTED_SCALE = 2.5
        S_I = I * N_SHARED

        def _route(x, gate_w, gate_bias):
            T = x.shape[0]
            logits = x @ gate_w.T
            scores = jax.nn.sigmoid(logits)
            scores_for_choice = scores + gate_bias[None, :]
            grp = scores_for_choice.reshape(T, NG, E // NG)
            group_scores = jnp.sum(jax.lax.top_k(grp, 2)[0], axis=-1)
            _, gidx = jax.lax.top_k(group_scores, TOPK_GROUP)
            gmask = jnp.zeros((T, NG), dtype=scores.dtype).at[jnp.arange(T)[:, None], gidx].set(1.0)
            emask = jnp.repeat(gmask, E // NG, axis=1)
            masked = jnp.where(emask > 0, scores_for_choice, 0.0)
            _, topk_idx = jax.lax.top_k(masked, TOP_K)
            topk_w = jnp.take_along_axis(scores, topk_idx, axis=1)
            topk_w = topk_w / (jnp.sum(topk_w, axis=-1, keepdims=True) + 1e-20)
            topk_w = topk_w * ROUTED_SCALE
            rw = jnp.zeros((T, E), dtype=scores.dtype).at[jnp.arange(T)[:, None], topk_idx].add(topk_w)
            return rw

        def _mlp(x, gw, uw, dw):
            return jax.nn.silu(x @ gw.T) * (x @ uw.T) @ dw.T
        key = jax.random.key(seed)
        ks = jax.random.split(key, 10)
        sc = 0.02
        return {'hidden_states': jax.random.normal(ks[0], (1, 256, H), dtype=jnp.float32), 'gate_w': sc * jax.random.normal(ks[1], (E, H), dtype=jnp.float32), 'gate_bias': sc * jax.random.normal(ks[2], (E,), dtype=jnp.float32), 'Wg': sc * jax.random.normal(ks[3], (E, I, H), dtype=jnp.float32), 'Wu': sc * jax.random.normal(ks[4], (E, I, H), dtype=jnp.float32), 'Wd': sc * jax.random.normal(ks[5], (E, H, I), dtype=jnp.float32), 'Sg': sc * jax.random.normal(ks[6], (S_I, H), dtype=jnp.float32), 'Su': sc * jax.random.normal(ks[7], (S_I, H), dtype=jnp.float32), 'Sd': sc * jax.random.normal(ks[8], (H, S_I), dtype=jnp.float32)}
    _L0_ffn_all = _L0_ffn_setup()
    _L0_ffn_in = {k: v for k, v in _L0_ffn_all.items() if k in ('gate_w', 'gate_bias', 'Wg', 'Wu', 'Wd', 'Sg', 'Su', 'Sd')}
    del _L0_ffn_all
    return {'x': x, 'ctx_1024': ctx_1024, 'g_xattn': g_xattn, 'g_ffn': g_ffn, 'L0_xattn_w_q': _L0_xattn_in['w_q'], 'L0_xattn_w_k': _L0_xattn_in['w_k'], 'L0_xattn_w_v': _L0_xattn_in['w_v'], 'L0_xattn_w_o': _L0_xattn_in['w_o'], 'L0_ffn_gate_w': _L0_ffn_in['gate_w'], 'L0_ffn_gate_bias': _L0_ffn_in['gate_bias'], 'L0_ffn_Wg': _L0_ffn_in['Wg'], 'L0_ffn_Wu': _L0_ffn_in['Wu'], 'L0_ffn_Wd': _L0_ffn_in['Wd'], 'L0_ffn_Sg': _L0_ffn_in['Sg'], 'L0_ffn_Su': _L0_ffn_in['Su'], 'L0_ffn_Sd': _L0_ffn_in['Sd']}

def reference(x, ctx_1024, g_xattn, g_ffn, L0_xattn_w_q, L0_xattn_w_k, L0_xattn_w_v, L0_xattn_w_o, L0_ffn_gate_w, L0_ffn_gate_bias, L0_ffn_Wg, L0_ffn_Wu, L0_ffn_Wd, L0_ffn_Sg, L0_ffn_Su, L0_ffn_Sd):
    import jax
    import jax.numpy as jnp

    def _L0_xattn_ref(q, k, v, w_q, w_k, w_v, w_o):
        import jax, jax.numpy as jnp
        import numpy as np
        D_MODEL = 256
        H = 16
        D_K = D_MODEL // H
        B, S, _ = q.shape

        def proj(x, w):
            y = jnp.einsum('bsd,ed->bse', x, w)
            return y.reshape(B, -1, H, D_K).transpose(0, 2, 1, 3)
        query = proj(q, w_q)
        key_ = proj(k, w_k)
        value = proj(v, w_v)
        scores = jnp.einsum('bhqd,bhkd->bhqk', query, key_) / jnp.sqrt(jnp.float32(D_K))
        attn = jax.nn.softmax(scores, axis=-1)
        x = jnp.einsum('bhqk,bhkd->bhqd', attn, value)
        x = x.transpose(0, 2, 1, 3).reshape(B, S, H * D_K)
        return jnp.einsum('bsd,ed->bse', x, w_o)

    def _L0_ffn_ref(hidden_states, gate_w, gate_bias, Wg, Wu, Wd, Sg, Su, Sd):
        import jax, jax.numpy as jnp
        import numpy as np
        H = 256
        I = 176
        E = 64
        TOP_K = 8
        NG = 8
        TOPK_GROUP = 4
        N_SHARED = 2
        ROUTED_SCALE = 2.5
        S_I = I * N_SHARED

        def _route(x, gate_w, gate_bias):
            T = x.shape[0]
            logits = x @ gate_w.T
            scores = jax.nn.sigmoid(logits)
            scores_for_choice = scores + gate_bias[None, :]
            grp = scores_for_choice.reshape(T, NG, E // NG)
            group_scores = jnp.sum(jax.lax.top_k(grp, 2)[0], axis=-1)
            _, gidx = jax.lax.top_k(group_scores, TOPK_GROUP)
            gmask = jnp.zeros((T, NG), dtype=scores.dtype).at[jnp.arange(T)[:, None], gidx].set(1.0)
            emask = jnp.repeat(gmask, E // NG, axis=1)
            masked = jnp.where(emask > 0, scores_for_choice, 0.0)
            _, topk_idx = jax.lax.top_k(masked, TOP_K)
            topk_w = jnp.take_along_axis(scores, topk_idx, axis=1)
            topk_w = topk_w / (jnp.sum(topk_w, axis=-1, keepdims=True) + 1e-20)
            topk_w = topk_w * ROUTED_SCALE
            rw = jnp.zeros((T, E), dtype=scores.dtype).at[jnp.arange(T)[:, None], topk_idx].add(topk_w)
            return rw

        def _mlp(x, gw, uw, dw):
            return jax.nn.silu(x @ gw.T) * (x @ uw.T) @ dw.T
        B, S, _ = hidden_states.shape
        x = hidden_states.reshape(B * S, H)
        rw = _route(x, gate_w, gate_bias)
        expert_out = jax.vmap(lambda gw_, uw_, dw_: _mlp(x, gw_, uw_, dw_))(Wg, Wu, Wd)
        routed = jnp.einsum('eth,te->th', expert_out, rw)
        shared = _mlp(x, Sg, Su, Sd)
        out = (routed + shared).reshape(B, S, H)
        return out
    x = x + jnp.tanh(g_xattn[0]) * _L0_xattn_ref(_layernorm(x, axis=-1), ctx_1024, ctx_1024, L0_xattn_w_q, L0_xattn_w_k, L0_xattn_w_v, L0_xattn_w_o)
    x = x + jnp.tanh(g_ffn[0]) * _L0_ffn_ref(_layernorm(x, axis=-1), L0_ffn_gate_w, L0_ffn_gate_bias, L0_ffn_Wg, L0_ffn_Wu, L0_ffn_Wd, L0_ffn_Sg, L0_ffn_Su, L0_ffn_Sd)
    return x

_drawn_inputs = setup_inputs


def setup_inputs(seed=0):
    import zlib

    import numpy as np

    out = dict(_drawn_inputs(seed))
    spreads = {}
    factors = {'L0_ffn_gate_w': 5.597,
     'L0_ffn_gate_bias': 8.0,
     'L0_ffn_Wg': 5.288,
     'L0_ffn_Wu': 5.225,
     'L0_ffn_Wd': 5.228,
     'L0_ffn_Sg': 3.324,
     'L0_ffn_Su': 3.301,
     'L0_ffn_Sd': 3.288}
    for name, (base, spread) in spreads.items():
        noise = np.random.default_rng([zlib.crc32(name.encode()), seed]).standard_normal(out[name].shape)
        drawn = base * np.exp(spread * noise) if base else spread * noise
        out[name] = jnp.asarray(drawn.astype(out[name].dtype))
    for name, factor in factors.items():
        out[name] = (out[name] * factor).astype(out[name].dtype)
    return out
```

```python
import concourse.bass as bass
from concourse import mybir
from contextlib import ExitStack


def flamingo_gated_block(
    nc: bass.Bass,
    x_in: bass.AP,
    ctxT_in: bass.AP,
    wq_in: bass.AP,
    wkv_in: bass.AP,
    wo_in: bass.AP,
    router_in: bass.AP,
    bias_in: bass.AP,
    gates_in: bass.AP,
    wgu_in: bass.AP,
    wd_in: bass.AP,
    out: bass.AP,
):
    f32 = mybir.dt.float32
    bf16 = mybir.dt.bfloat16
    i32 = mybir.dt.int32
    u32 = mybir.dt.uint32
    ALU = mybir.AluOpType
    ACT = mybir.ActivationFunctionType
    AX = mybir.AxisListType
    RMAX = bass.bass_isa.ReduceOp.max
    ds = bass.ds

    P = 128
    S, D = x_in.shape
    KV = ctxT_in.shape[2]
    NH = 16
    DK = D // NH
    TT = S // P
    KC = -(-KV // P)
    KR = [min(P, KV - P * c) for c in range(KC)]
    QB = 512
    NB = S // QB
    TB = QB // P
    NG = NH // 4
    NT = 6
    AUG = NT * DK + 2
    EPS = 1e-5
    SHIFT_MAX = 40.0

    E = router_in.shape[2]
    K8 = 8
    I2 = wd_in.shape[1]
    IW = 2 * I2
    WGU = 2 * 2 * IW
    WD = 2 * D
    WSPLIT = 2 * (WGU + WD)
    DHI = 2 * WGU
    DLO = 2 * WGU + WD
    NSLOT = 8
    REGION = S + P
    T_MAX = K8 * S // P + E - 1
    NTAB = 200
    SCALE_OUT = 2.5

    dispatch = nc.dram_tensor("dispatch_rows", (E * REGION + 6 * P, 2 * D), bf16).ap()
    T_MIN = K8 * S // P
    T_PAIRS = (T_MAX + 1) // 2
    expert_out = nc.dram_tensor("expert_rows", (2 * T_PAIRS * P, D), f32).ap()

    ctx = ExitStack()
    with ctx:
        def sb(name, shape, dt):
            return ctx.enter_context(nc.sbuf_tensor(name, shape, dt))

        def sem(name):
            return ctx.enter_context(nc.semaphore(name))

        KT = sb("KT", [P, NH * KV + 16], bf16)
        QT = sb("QT", [P, NB * NH * QB], bf16)
        VA = sb("VA", [P, KC * NH * 32], f32)
        PR = sb("PR", [P, 3 * 4 * QB], f32)
        ACC = sb("ACC", [P, TT, D], f32)
        SCR = sb("SCR", [P, 3584], f32)
        wo = sb("wo", [P, NG, D], f32)
        gw = sb("gw", [P, 2, E], f32)
        bias = sb("bias", [P, E], f32)
        gates = sb("gates", [P, 2], f32)
        tg = sb("tg", [P, 2], f32)
        identf = sb("identf", [P, P], f32)
        identb = sb("identb", [P, P], bf16)
        before = sb("before", [P, P], bf16)
        upto = sb("upto", [E, E], f32)
        ones_b = sb("ones_b", [P, P], bf16)
        ones_f = sb("ones_f", [E, 1], f32)
        zrow = sb("zrow", [P, 2 * D], bf16)
        iota_e = sb("iota_e", [P, E], f32)
        base_e = sb("base_e", [P, E], f32)
        iota_t = sb("iota_t", [E, NTAB], f32)
        turn = sb("turn", [P, 1], f32)
        stats = sb("stats", [P, 6], f32)
        mv = sb("mv", [P, TT, 2], f32)
        rs = sb("rs", [P, TT], f32)
        rt = sb("rt", [P, TT], f32)
        ri = sb("ri", [P, TT], i32)
        ve = sb("ve", [P, TT], f32)
        kmax = sb("kmax", [P, NH], f32)
        knall = sb("knall", [P, NH], f32)
        NM = sb("NM", [P, TT, NH], f32)
        qn = sb("qn", [P, NH], f32)
        shmax = sb("shmax", [P, 2], f32)
        flag = sb("flag", [P, 1], i32)
        EX = sb("EX", [P, E], f32)
        SCO = sb("SCO", [P, E], f32)
        CF = sb("CF", [P, E], f32)
        G8 = sb("G8", [P, E], f32)
        GS = sb("GS", [P, 8], f32)
        T8 = sb("T8", [P, 8], f32)
        I8 = sb("I8", [P, 8], u32)
        F8 = sb("F8", [P, 8], f32)
        GM = sb("GM", [P, 8], f32)
        W8 = sb("W8", [P, 8], f32)
        W1 = sb("W1", [P, 2], f32)
        MK = sb("MK", [P, E], bf16)
        MSUM = sb("MSUM", [P, E], bf16)
        POS = sb("POS", [P, E], f32)
        IDX = sb("IDX", [P, TT, K8], u32)
        WK = sb("WK", [P, TT, K8], f32)
        cnt = sb("cnt", [E, 1], f32)
        cti = sb("cti", [E, 1], i32)
        ctf = sb("ctf", [E, 1], f32)
        cum = sb("cum", [E, 1], f32)

        SP4 = ctx.enter_context(nc.psum_tensor("SP4", [P, 4 * 512], f32))
        PVB = [ctx.enter_context(nc.psum_tensor(f"PVB{i}", [P, 512], f32)) for i in range(2)]
        M0 = ctx.enter_context(nc.psum_tensor("M0", [P, 512], f32))
        M1 = ctx.enter_context(nc.psum_tensor("M1", [P, 512], f32))
        BANKS = [SP4[:, 512 * i:512 * i + 512] for i in range(4)] + [PVB[0][:, :], PVB[1][:, :], M0[:, :], M1[:, :]]

        KTv = KT[:, 0:NH * KV].rearrange("p (h k) -> p h k", h=NH)
        QTv = QT[:, :].rearrange("p (b h q) -> p b h q", b=NB, h=NH)
        VAv = VA[:, :].rearrange("p (c h d) -> p c h d", c=KC, h=NH)
        PRv = PR[:, :].rearrange("p (s h q) -> p s h q", s=3, h=4)

        KN = QT[:, 0:2 * KC * NH].bitcast(f32).rearrange("p (c h) -> p c h", c=KC)

        def attnT(b, g):
            o = (b * NH + 4 * g) * QB
            return QT[:, o:o + 2 * QB].bitcast(f32)

        def h2T_cols(i):
            b, j = i // TB, i % TB
            o = b * NH * QB
            v = QT[:, o:o + NH * QB].rearrange("p (g r) -> p g r", g=4)
            return v[:, :, 2 * QB + P * j:2 * QB + P * (j + 1)]

        ctxT = PR[:, 0:2 * KV].rearrange("p (c k) -> p c k", c=2)
        wkv = PR[:, 2 * KV:2 * KV + 1024].rearrange("p (c n) -> p c n", c=2)
        wq = PR[:, 2 * KV + 1024:2 * KV + 1536].rearrange("p (c n) -> p c n", c=2)
        AW = NH * AUG
        AUGT = [SCR[:, j * (AW // 2):(j + 1) * (AW // 2)].bitcast(bf16).rearrange("p (h a) -> p h a", h=NH)
                for j in range(2)]
        SQ = SCR[:, AW:AW + D]
        R1 = [SCR[:, AW + D * (1 + j):AW + D * (2 + j)] for j in range(2)]
        QS = SCR[:, AW + 3 * D:AW + 4 * D]
        XN = SCR[:, AW + 4 * D:AW + 5 * D]
        XNT = SCR[:, AW + 5 * D:AW + 6 * D]
        CHOSEN = NM[:, 0:TT // 2, :].rearrange("p t (u k) -> p (t u) k", k=K8)
        IDX2 = NM[:, TT // 2:TT, :].bitcast(u32).rearrange("p t (u k) -> p (t u) k", k=K8)
        MROW = SCR[:, 0:NH]
        MHL = SCR[:, NH:2 * NH].bitcast(bf16).rearrange("p (h t) -> p h t", h=NH)

        OS = SCR[:, 0:512]
        RS = SCR[:, 512:1024]
        H2 = SCR[:, 1024:1280]
        H2T = SCR[:, 1280:1536]
        XR = [SCR[:, 1536 + D * j:1536 + D * (j + 1)].bitcast(bf16) for j in range(4)]
        TABF = SCR[0:1, 0:5 * NTAB]
        CTB = EX[0:E, :].bitcast(bf16)
        DELTA = POS[:, :]
        A8 = SCR[:, 2560:3072]
        PX = SCR[:, 3072:3584]

        def wslot(o, n):
            return KT[:, ds(o, n)]
        STG = [KT[:, NSLOT * WSPLIT + 2 * (WGU + WD) * j:NSLOT * WSPLIT + 2 * (WGU + WD) * (j + 1)].bitcast(f32)
               for j in range(2)]
        SW = [PR[:, (WSPLIT // 2) * s:(WSPLIT // 2) * (s + 1)].bitcast(bf16) for s in range(2)]
        RING = PR[:, WSPLIT:WSPLIT + K8 * D].rearrange("p (k n) -> p k n", k=K8)
        XG = [VA[:, 256 * j:256 * (j + 1)].bitcast(bf16) for j in range(2)]
        XT = [VA[:, 512 + 256 * j:512 + 256 * (j + 1)].bitcast(bf16) for j in range(2)]
        SIL = [VA[:, 1024 + IW * j:1024 + IW * (j + 1)] for j in range(2)]
        HF = [VA[:, 1376 + IW * j:1376 + IW * (j + 1)] for j in range(2)]
        HHL = [VA[:, 1728 + IW * j:1728 + IW * (j + 1)].bitcast(bf16).rearrange("p (t n) -> p t n", t=2) for j in range(2)]
        HT = [VA[:, 2080 + 256 * j:2080 + 256 * (j + 1)].bitcast(bf16) for j in range(2)]
        YB = [VA[:, 2592 + D * j:2592 + D * (j + 1)] for j in range(2)]
        TAB = VA[0:1, 3200:3200 + 5 * NTAB].bitcast(i32)
        XTP = [BANKS[j][:, 0:256].bitcast(bf16) for j in range(2)]
        GUP = [BANKS[2 + j] for j in range(2)]
        HTP = [BANKS[4 + j][:, 0:256].bitcast(bf16) for j in range(2)]
        YP = [BANKS[6 + j][:, 0:D] for j in range(2)]

        ctx_in = sem("ctx_in"); wkv_in_s = sem("wkv_loaded"); x_loaded = sem("x_loaded"); wq_loaded = sem("wq_loaded")
        small_loaded = sem("small_loaded")
        consts = sem("consts")
        gates_done = sem("gates_done")
        pe_kv = sem("pe_kv"); act_kh = sem("act_kh"); act_v = sem("act_v"); dve_r1 = sem("dve_r1"); act_km = sem("act_km")
        dve_ka = sem("dve_ka"); pe_kt = sem("pe_kt"); dve_kt = sem("dve_kt"); dve_kn = sem("dve_kn"); pool_kmax = sem("pool_kmax")
        dve_xn = sem("dve_xn"); pe_xt = sem("pe_xt"); dve_xt = sem("dve_xt"); pe_q = sem("pe_q"); act_qs = sem("act_qs")
        act_qh = sem("act_qh"); pool_r1 = sem("pool_r1"); act_qm = sem("act_qm"); pool_ql = sem("pool_ql"); dve_qn = sem("dve_qn")
        dve_m = sem("dve_m"); pe_qt = sem("pe_qt"); dve_qt = sem("dve_qt")
        dve_top = sem("dve_top"); pool_top = sem("pool_top"); dve_flag = sem("dve_flag")
        gen_s = sem("gen_s"); gen_m = sem("gen_m"); gen_split = sem("gen_split"); gen_t = sem("gen_t"); gen_qt = sem("gen_qt")
        gen_chain = sem("gen_chain")
        pe_qk = sem("pe_qk"); act_exp = sem("act_exp"); pe_pv = sem("pe_pv"); dve_pv = sem("dve_pv"); dve_attn = sem("dve_attn")
        pe_op = sem("pe_op"); dve_h2 = sem("dve_h2"); pool_xr = sem("pool_xr"); pe_h2t = sem("pe_h2t"); dve_h2t = sem("dve_h2t")
        dve_hl = sem("dve_hl"); pe_lg = sem("pe_lg"); act_sig = sem("act_sig"); dve_mk = sem("dve_mk"); pe_rank = sem("pe_rank")
        dve_msum = sem("dve_msum"); dve_idx = sem("dve_idx")
        scattered = [sem(f"scattered{j}") for j in range(4)]
        dummy_zero = sem("dummy_zero"); padded = sem("padded")
        pe_tab = sem("pe_tab"); dve_tab = sem("dve_tab")
        w_loaded = [sem(f"w_loaded{j}") for j in range(2)]
        w_split = sem("w_split")
        tiles_done = sem("tiles_done")
        sh_gu = sem("sh_gu"); sh_sil = sem("sh_sil"); sh_h = sem("sh_h"); sh_t = sem("sh_t"); sh_te = sem("sh_te"); sh_y = sem("sh_y"); sh_ye = sem("sh_ye")
        xg_loaded = [sem(f"xg_loaded{j}") for j in range(2)]
        e_t1 = sem("e_t1"); e_xt = sem("e_xt"); e_gu = sem("e_gu"); e_sil = sem("e_sil"); e_h = sem("e_h"); e_t2 = sem("e_t2")
        e_te = sem("e_te"); e_ye = sem("e_ye")
        y_stored = [sem(f"y_stored{j}") for j in range(2)]
        gathered = [sem(f"gathered{k}") for k in range(K8)]
        dve_comb = sem("dve_comb"); out_done = sem("out_done")
        chain = sem("vector_chain")
        pchain = sem("pool_chain"); chain_tab = sem("dve_tab_parts"); e_link = sem("hidden_chain"); rows_done = sem("rows_done"); rest_zero = sem("rest_zero"); dve_idx2 = sem("dve_idx2")

        N_SPLIT0 = 8
        ET, RT, WB, PADR, WAITC = (slice(NTAB * n, NTAB * (n + 1)) for n in range(5))

        block = ctx.enter_context(nc.Block())

        @block.sync
        def _(eng):
            eng.dma_start(ctxT, ctxT_in).then_inc(ctx_in, 16)
            eng.dma_start(wkv, wkv_in).then_inc(wkv_in_s, 16)
            eng.dma_start(ACC[:, :, :], x_in.rearrange("(t p) n -> p t n", p=P)).then_inc(x_loaded, 16)
            eng.dma_start(wq, wq_in).then_inc(wq_loaded, 16)
            eng.dma_start(gates[:, :], gates_in.broadcast_to((P, 2))).then_inc(small_loaded, 16)
            eng.dma_start(bias[:, :], bias_in.broadcast_to((P, E))).then_inc(small_loaded, 16)
            eng.dma_start(wo[:, :, :], wo_in).then_inc(small_loaded, 16)
            eng.dma_start(gw[:, :, :], router_in).then_inc(small_loaded, 16)
            eng.wait_ge(consts, 1)
            eng.dma_start(expert_out[T_MIN * P:, :].rearrange("(t p) n -> p t n", p=P),
                          zrow[:, :].bitcast(f32).rearrange("p (o n) -> p o n", o=1).broadcast_to((P, 2 * T_PAIRS - T_MIN, D)))\
               .then_inc(rest_zero, 16)
            for j in range(6):
                eng.dma_start(dispatch[E * REGION + P * j:E * REGION + P * (j + 1), :], zrow[:, :]).then_inc(dummy_zero, 16)
            eng.wait_ge(dve_tab, 1)
            with eng.Fori(0, E) as e:
                r = eng.value_load(TAB[0:1, ds(PADR.start + e, 1)], min_val=0, max_val=E * REGION - P)
                eng.dma_start(dispatch[ds(r, P), :], zrow[:, :]).then_inc(padded, 16)
            eng.wait_ge(padded, 16 * E)
            eng.wait_ge(rest_zero, 16)
            eng.wait_ge(dummy_zero, 16 * 6)
            for j in range(4):
                eng.wait_ge(scattered[j], 16 * K8 * TT // 4)

            def load(t, j, count=None):
                r = eng.value_load(TAB[0:1, ds(RT.start + t, 1)], min_val=0, max_val=E * REGION + 5 * P)
                eng.dma_start(XG[j], dispatch[ds(r, P), :]).then_inc(xg_loaded[j], 16)

            n = eng.value_load(TAB[0:1, ET.stop - 1:ET.stop], min_val=0, max_val=T_MAX)
            eng.wait_ge(pe_tab, 3)
            eng.wait_ge(dve_tab, 1)
            load(0, 0)
            load(1, 1)
            for t in (2, 3, 4):
                eng.wait_ge(e_t1, t - 1)
                load(t, t % 2)
            with eng.Fori(0, (T_MAX + 1) // 2) as i:
                with eng.If(i < n):
                    for j in range(2):
                        eng.wait_ge(e_t1, i * 2 + (4 + j))
                        load(i * 2 + (5 + j), (1 + j) % 2)

            for i in range(TT):
                eng.wait_ge(dve_comb, K8 * (i + 1))
                eng.dma_start(out[i * P:(i + 1) * P, :], ACC[:, i, :]).then_inc(out_done, 16)
            eng.wait_ge(out_done, 16 * TT)

        @block.gpsimd
        def _(eng):
            eng.memset(zrow[:, :], 0.0).then_inc(consts, 1)
            eng.memset(identf[:, :], 0.0)
            eng.memset(before[:, :], 1.0)
            eng.memset(ones_b[:, :], 1.0)
            eng.memset(ones_f[:, :], 1.0)
            eng.memset(upto[:, :], 1.0)
            eng.memset(MSUM[:, :], 0.0)
            eng.memset(turn[:, :], 0.0)
            eng.iota(iota_e[:, :], [[1, E]], base=0, channel_multiplier=0, allow_small_or_imprecise_dtypes=True)
            eng.iota(iota_t[:, :], [[1, NTAB]], base=0, channel_multiplier=0,
                     allow_small_or_imprecise_dtypes=True).then_inc(pchain, 1)
            eng.wait_ge(pchain, 1)
            eng.affine_select(out=identf[:, :], in_=identf[:, :], compare_op=ALU.not_equal, fill=1.0, base=0,
                              pattern=[[-1, P]], channel_multiplier=1)
            eng.affine_select(out=before[:, :], in_=before[:, :], compare_op=ALU.is_gt, fill=0.0, base=0,
                              pattern=[[1, P]], channel_multiplier=-1)
            eng.affine_select(out=upto[:, :], in_=upto[:, :], compare_op=ALU.is_ge, fill=0.0, base=0,
                              pattern=[[1, E]], channel_multiplier=-1)
            eng.tensor_scalar(base_e[:, :], iota_e[:, :], float(REGION), None, ALU.mult).then_inc(pchain, 1)
            eng.wait_ge(pchain, 2)
            eng.tensor_scalar(identb[:, :], identf[:, :], 1.0, None, ALU.mult).then_inc(consts, 1)
            for j in range(2):
                eng.memset(AUGT[j][:, :, NT * DK:AUG], 1.0)
            eng.memset(KN[:, :, :], 0.0)
            eng.memset(VAv[:, :, :, DK:2 * DK], 1.0).then_inc(consts, 1)

            eng.wait_ge(dve_kn, KC + 1)
            eng.partition_all_reduce(knall[:, :], kmax[:, :], P, RMAX).then_inc(pool_kmax, 1)
            for t in range(TT):
                eng.wait_ge(act_qh, t + 1)
                if t >= 1:
                    eng.wait_ge(act_qm, t)
                    eng.wait_ge(pool_ql, t)
                eng.tensor_tensor(R1[0], QS, AUGT[t % 2][:, :, 0:DK], ALU.subtract).then_inc(pool_r1, 1)
                eng.wait_ge(act_qm, t + 1)
                eng.tensor_tensor(AUGT[t % 2][:, :, 5 * DK:6 * DK], R1[0].rearrange("p (h d) -> p h d", h=NH),
                                  AUGT[t % 2][:, :, 3 * DK:4 * DK], ALU.subtract).then_inc(pool_ql, 1)
            eng.wait_ge(dve_top, 1)
            eng.partition_all_reduce(shmax[:, 1:2], shmax[:, 0:1], P, RMAX).then_inc(pool_top, 1)

            def rows(i):
                eng.wait_ge(dve_h2, i + 1)
                if i >= 4:
                    eng.wait_ge(scattered[i % 4], 16 * K8 * (i // 4))
                eng.tensor_scalar(XR[i % 4][:, 0:D], H2, 1.0, None, ALU.mult).then_inc(pool_xr, 1)
                eng.wait_ge(pool_xr, 2 * i + 1)
                eng.tensor_tensor(XR[i % 4][:, D:2 * D], H2, XR[i % 4][:, 0:D], ALU.subtract).then_inc(pool_xr, 1)

            def scatter(i):
                eng.wait_ge(pool_xr, 2 * i + 2)
                eng.wait_ge(dve_idx, i + 1)
                for k in range(K8):
                    eng.indirect_dma_start(out=dispatch, out_offset=bass.IndirectOffsetOnAxis(ap=IDX[:, i, k:k + 1], axis=0),
                                           in_=XR[i % 4], in_offset=None).then_inc(scattered[i % 4], 16)

            for i in range(TT):
                if i < TT - TB:
                    rows(i)
                    scatter(i)
                else:
                    rows(i)
            def load_w(e, j):
                eng.dma_start(STG[j][:, 0:WGU], wgu_in[ds(e, 1), :, :].rearrange("o p n -> p (o n)")).then_inc(w_loaded[j], 16)
                eng.dma_start(STG[j][0:I2, WGU:WGU + WD], wd_in[ds(e, 1), :, :].rearrange("o p n -> p (o n)")).then_inc(w_loaded[j], 16)

            def split_hi(j, hi_gu, hi_d):
                eng.tensor_scalar(hi_gu, STG[j][:, 0:WGU], 1.0, None, ALU.mult).then_inc(w_split, 1)
                eng.tensor_scalar(hi_d, STG[j][0:I2, WGU:WGU + WD], 1.0, None, ALU.mult).then_inc(w_split, 1)

            def split_lo(j, hi_gu, hi_d, lo_gu, lo_d):
                eng.tensor_tensor(lo_gu, STG[j][:, 0:WGU], hi_gu, ALU.subtract).then_inc(w_split, 1)
                eng.tensor_tensor(lo_d, STG[j][0:I2, WGU:WGU + WD], hi_d, ALU.subtract).then_inc(w_split, 1)

            eng.wait_ge(pe_qk, 2 * NB * NG * KC)
            for s in range(2):
                load_w(E + s, s)
            for i in range(TT - TB, TT):
                scatter(i)
            eng.wait_ge(pe_pv, NB * NG * KC)
            for s in range(2):
                eng.wait_ge(w_loaded[s], 32)
                hg, hd = SW[s][:, 0:WGU], SW[s][0:I2, DHI:DLO]
                split_hi(s, hg, hd)
                eng.wait_ge(w_split, 4 * s + 2)
                split_lo(s, hg, hd, SW[s][:, WGU:2 * WGU], SW[s][0:I2, DLO:DLO + WD])
                eng.wait_ge(w_split, 4 * s + 4)
                load_w(s, s)
            eng.wait_ge(dve_tab, 1)

            def expert(i, j, more):
                w = eng.value_load(TAB[0:1, ds(i * NSLOT + (WAITC.start + j), 1)], min_val=1, max_val=T_MAX + 1)
                eng.wait_ge(w_loaded[j % 2], i * (16 * NSLOT) + 32 * (j // 2 + 2))
                eng.wait_ge(tiles_done, w)
                o = j * WSPLIT
                eng.tensor_tensor(turn[:, :], turn[:, :], turn[:, :], ALU.add).then_inc(w_split, 1)
                hg, hd = KT[:, o:o + WGU], KT[0:I2, o + DHI:o + DLO]
                split_hi(j % 2, hg, hd)
                eng.wait_ge(w_split, i * (5 * NSLOT) + (N_SPLIT0 + 5 * j + 3))
                split_lo(j % 2, hg, hd, KT[:, o + WGU:o + 2 * WGU], KT[0:I2, o + DLO:o + DLO + WD])
                if more:
                    eng.wait_ge(w_split, i * (5 * NSLOT) + (N_SPLIT0 + 5 * j + 5))
                    load_w(i * NSLOT + (j + 2), j % 2)

            with eng.Fori(0, E // NSLOT - 1) as i:
                for j in range(NSLOT):
                    expert(i, j, True)
            for j in range(NSLOT):
                expert(E // NSLOT - 1, j, j < NSLOT - 2)

            eng.wait_ge(dve_idx2, TT)
            eng.wait_ge(rows_done, 1)
            for i in range(TT):
                for k in range(K8):
                    if i >= 1:
                        eng.wait_ge(dve_comb, K8 * (i - 1) + k + 1)
                    eng.indirect_dma_start(out=RING[:, k, :], out_offset=None, in_=expert_out,
                                           in_offset=bass.IndirectOffsetOnAxis(ap=IDX2[:, i, k:k + 1], axis=0)).then_inc(gathered[k], 16)

        @block.scalar
        def _(eng):
            eng.wait_ge(small_loaded, 64)
            eng.activation(tg[:, :], gates[:, :], ACT.Tanh).then_inc(gates_done, 1)

            def heads3(t, lo, hi, step=1):
                return t.rearrange("p h (n d) -> p h n d", d=DK)[:, :, lo:hi:step, :]

            def key_first(c):
                r, kv = KR[c], BANKS[c % 2]
                eng.wait_ge(pe_kv, c + 1)
                if c >= 2:
                    eng.wait_ge(pe_kt, 2 * (c - 1))
                src = kv[0:r, 0:D].rearrange("p (h o d) -> p h o d", h=NH, o=1).broadcast_to((r, NH, 3, DK))
                eng.activation(heads3(AUGT[c % 2][0:r, :, 0:NT * DK], 1, NT, 2), src, ACT.Copy).then_inc(act_kh, 1)
                if c >= 1:
                    eng.wait_ge(dve_kn, c)
                eng.activation(SQ[0:r, :], kv[0:r, 0:D], ACT.Square).then_inc(act_v, 1)
                eng.activation(VAv[0:r, c, :, 0:DK], kv[0:r, D:2 * D].rearrange("p (h d) -> p h d", h=NH),
                               ACT.Copy).then_inc(act_v, 1)

            def key_second(c):
                r = KR[c]
                eng.wait_ge(dve_r1, c + 1)
                src = R1[c % 2][0:r, :].rearrange("p (h o d) -> p h o d", h=NH, o=1).broadcast_to((r, NH, 2, DK))
                eng.activation(heads3(AUGT[c % 2][0:r, :, 0:NT * DK], 2, 5, 2), src, ACT.Copy).then_inc(act_km, 1)

            eng.wait_ge(consts, 3)
            key_first(0)
            for c in range(1, KC):
                key_first(c)
                key_second(c - 1)
            key_second(KC - 1)

            eng.wait_ge(dve_ka, KC)
            for t in range(TT):
                qa = AUGT[t % 2][:, :, 0:NT * DK]
                eng.wait_ge(pe_q, t + 1)
                if t == 0:
                    eng.wait_ge(pe_kt, 2 * KC)
                if t >= 1:
                    eng.wait_ge(pool_ql, t)
                    eng.wait_ge(act_qm, t)
                eng.activation(QS, PVB[1][:, 0:D], ACT.Copy, scale=1.0 / DK ** 0.5).then_inc(act_qs, 1)
                eng.wait_ge(act_qs, t + 1)
                if t >= 2:
                    eng.wait_ge(pe_qt, 2 * (t - 1))
                src = QS.rearrange("p (h o d) -> p h o d", h=NH, o=1).broadcast_to((P, NH, 3, DK))
                eng.activation(heads3(qa, 0, 3), src, ACT.Copy).then_inc(act_qh, 1)
                if t >= 1:
                    eng.wait_ge(dve_qn, t)
                eng.activation(SQ, QS, ACT.Square).then_inc(act_v, 1)
                eng.wait_ge(pool_r1, t + 1)
                src = R1[0].rearrange("p (h o d) -> p h o d", h=NH, o=1).broadcast_to((P, NH, 2, DK))
                eng.activation(heads3(qa, 3, 5), src, ACT.Copy).then_inc(act_qm, 1)

            def sigmoid_exp(i):
                eng.wait_ge(pe_lg, i + 1)
                if i >= 1:
                    eng.wait_ge(dve_mk, i)
                eng.activation(EX[:, :], M1[:, 0:E], ACT.Exp, scale=-1.0).then_inc(act_sig, 1)

            for n in range(NB * NG * KC):
                b, c = n // (NG * KC), n % KC
                r = KR[c]
                for p in range(2):
                    eng.wait_ge(pe_qk, 2 * n + p + 1)
                    if n >= 3:
                        eng.wait_ge(pe_pv, n - 2)
                    eng.activation(PRv[0:r, n % 3, 2 * p:2 * p + 2, :],
                                   SP4[0:r, 1024 * p:1024 * p + 1024].rearrange("p (h q) -> p h q", h=2),
                                   ACT.Exp).then_inc(act_exp, 1)
                m = n % (NG * KC)
                if b >= 1 and m % 8 == 2 and 10 <= m < 10 + 8 * TB:
                    sigmoid_exp((b - 1) * TB + (m - 10) // 8)
            for i in range(TT - TB, TT):
                sigmoid_exp(i)

            def sh_silu(cnt_gu, s):
                eng.wait_ge(sh_gu, cnt_gu)
                eng.activation(SIL[s], GUP[s][:, 0:IW], ACT.Silu).then_inc(sh_sil, 1)

            def sh_evac(cnt_t, s):
                eng.wait_ge(sh_t, cnt_t)
                eng.activation(HT[s][0:I2, :], HTP[s][0:I2, :], ACT.Copy).then_inc(sh_te, 1)

            for i in range(TT):
                for s in range(2):
                    if i >= 1:
                        eng.wait_ge(sh_h, 2 * (i - 1) + s + 1)
                    sh_silu(2 * i + s + 1, s)
                if i >= 1:
                    if i >= 2:
                        eng.wait_ge(sh_y, i - 1)
                    for s in range(2):
                        sh_evac(2 * (i - 1) + s + 1, s)
            eng.wait_ge(sh_y, TT - 1)
            for s in range(2):
                sh_evac(2 * (TT - 1) + s + 1, s)

            def silu(t, j):
                eng.wait_ge(e_gu, t + 1)
                eng.activation(SIL[j], GUP[j][:, 0:IW], ACT.Silu).then_inc(e_sil, 1)

            def ht_evac(t, j):
                eng.wait_ge(e_t2, t + 1)
                eng.activation(HT[j][0:I2, :], HTP[j][0:I2, :], ACT.Copy).then_inc(e_te, 1)

            def y_out(t, j, first=False):
                eng.wait_ge(tiles_done, t + 2)
                if not first:
                    eng.wait_ge(y_stored[j], t * 8 - 8 * j)
                eng.activation(YB[j], YP[j], ACT.Copy).then_inc(e_ye, 1)
                eng.wait_ge(e_ye, t + 1)
                eng.dma_start(expert_out[ds(t * P, P), :], YB[j]).then_inc(y_stored[j], 16)

            eng.wait_ge(dve_tab, 1)
            eng.wait_ge(sh_y, TT)
            silu(0, 0)
            silu(1, 1)
            ht_evac(0, 0)
            n = eng.value_load(TAB[0:1, ET.stop - 1:ET.stop], min_val=0, max_val=T_MAX)
            for j in range(2):
                eng.wait_ge(e_h, j + 1)
                silu(2 + j, j)
                eng.wait_ge(tiles_done, j + 1)
                ht_evac(1 + j, (1 + j) % 2)
                y_out(j, j, first=True)
            with eng.Fori(1, (T_MAX + 1) // 2) as i:
                with eng.If(i < n):
                    for j in range(2):
                        eng.wait_ge(e_h, i * 2 + (j + 1))
                        silu(i * 2 + (2 + j), j)
                        eng.wait_ge(tiles_done, i * 2 + (j + 1))
                        ht_evac(i * 2 + (1 + j), (1 + j) % 2)
                        y_out(i * 2 + j, j)
            for j in range(2):
                eng.wait_ge(y_stored[j], n * 16)
            eng.activation(tg[:, 0:1], tg[:, 0:1], ACT.Copy).then_inc(rows_done, 1)

        @block.tensor
        def _(eng):
            def mm(o, l, r, start, stop, **kw):
                return eng.matmul(o, l, r, start=start, stop=stop, **kw)

            def kv_rows(c):
                r = KR[c]
                if c >= 2:
                    eng.wait_ge(act_v, 2 * (c - 1))
                    eng.wait_ge(dve_r1, c - 1)
                for k in range(2):
                    i = mm(BANKS[c % 2][0:r, :], ctxT[:, k, c * P:c * P + r], wkv[:, k, :], k == 0, k == 1)
                i.then_inc(pe_kv, 1)

            def kv_transposes(c):
                r = KR[c]
                eng.wait_ge(dve_ka, c + 1)
                for g in range(2):
                    n = 2 * c + g
                    if n >= 2:
                        eng.wait_ge(dve_kt, n - 1)
                    bank = BANKS[2 + n % 2].bitcast(bf16).rearrange("p (h q) -> p h q", h=8)
                    for h in range(8):
                        i = eng.transpose(bank[0:AUG, h, 0:r], AUGT[c % 2][0:r, 8 * g + h, :], identb[0:r, 0:r])
                    i.then_inc(pe_kt, 1)

            eng.wait_ge(consts, 3)
            eng.wait_ge(ctx_in, 16)
            eng.wait_ge(wkv_in_s, 16)
            kv_rows(0)
            for c in range(1, KC):
                kv_rows(c)
                kv_transposes(c - 1)
            kv_transposes(KC - 1)

            def q_transposes(t):
                eng.wait_ge(dve_m, t + 1)
                eng.wait_ge(pool_ql, t + 1)
                for g in range(2):
                    n = 2 * t + g
                    eng.wait_ge(dve_kt, 2 * KC)
                    if n >= 2:
                        eng.wait_ge(dve_qt, n - 1)
                    bank = BANKS[2 + n % 2].bitcast(bf16).rearrange("p (h q) -> p h q", h=8)
                    for h in range(8):
                        i = eng.transpose(bank[0:AUG, h, :], AUGT[t % 2][:, 8 * g + h, :], identb[:, :])
                    i.then_inc(pe_qt, 1)

            eng.wait_ge(wq_loaded, 16)
            for t in range(TT):
                eng.wait_ge(dve_xn, t + 1)
                for k in range(2):
                    if t >= 1:
                        eng.wait_ge(dve_xt, t)
                    i = eng.transpose(PVB[0][:, P * k:P * (k + 1)], XN[:, P * k:P * (k + 1)], identf[:, :])
                i.then_inc(pe_xt, 1)
                eng.wait_ge(dve_xt, t + 1)
                if t >= 1:
                    eng.wait_ge(act_qs, t)
                for k in range(2):
                    i = mm(PVB[1][:, 0:D], XNT[:, P * k:P * (k + 1)], wq[:, k, :], k == 0, k == 1)
                i.then_inc(pe_q, 1)
                if t >= 1:
                    q_transposes(t - 1)
            q_transposes(TT - 1)

            eng.wait_ge(dve_flag, 1)
            general = eng.value_load(flag[0:1, 0:1], min_val=0, max_val=1)
            with eng.If(general > 0):
                eng.wait_ge(dve_qt, 2 * TT)
                with eng.Fori(0, NB) as b:
                    for j in range(TB):
                        for h in range(NH):
                            if not (j == 0 and h == 0):
                                eng.wait_ge(gen_m, b * (TB * NH) + (j * NH + h))
                            for c in range(4):
                                w = min(512, KV - 512 * c)
                                i = mm(SP4[:, 512 * c:512 * c + w],
                                       QT[0:NT * DK, ds(b * (NH * QB) + (h * QB + j * P), P)],
                                       KTv[0:NT * DK, h, 512 * c:512 * c + w], True, True)
                            i.then_inc(gen_s, 1)
                        eng.wait_ge(gen_split, b * TB + (j + 1))
                        for h in range(NH):
                            bank = BANKS[6 + h // 8].bitcast(bf16)
                            i = eng.transpose(bank[NT * DK:AUG, P * (h % 8):P * (h % 8 + 1)], MHL[:, h, :], identb[:, :])
                        i.then_inc(gen_t, 1)
                        eng.wait_ge(gen_qt, b * TB + (j + 1))
                        eng.wait_ge(gen_m, b * (TB * NH) + (j + 1) * NH)
            eng.nop()

            def scores(n, p):
                b, g, c = n // (NG * KC), n // KC % NG, n % KC
                r = KR[c]
                if n >= 1:
                    eng.wait_ge(act_exp, 2 * (n - 1) + p + 1)
                for u in range(2):
                    h = 4 * g + 2 * p + u
                    i = mm(SP4[0:r, 512 * (2 * p + u):512 * (2 * p + u + 1)], KTv[0:AUG, h, c * P:c * P + r],
                           QTv[0:AUG, b, h, :], True, True)
                i.then_inc(pe_qk, 1)

            def attend(n):
                b, g, c = n // (NG * KC), n // KC % NG, n % KC
                q, r = n // KC, KR[c]
                eng.wait_ge(act_exp, 2 * n + 2)
                if c == 0 and q >= 2:
                    eng.wait_ge(dve_pv, q - 1)
                for u in range(4):
                    i = mm(PVB[q % 2][32 * u:32 * u + 32, :], VAv[0:r, c, 4 * g + u, :], PRv[0:r, n % 3, u, :],
                           c == 0, c == KC - 1)
                i.then_inc(pe_pv, 1)

            def out_proj(i):
                b, j = i // TB, i % TB
                eng.wait_ge(dve_attn, NG * (b + 1))
                if i >= 1:
                    eng.wait_ge(dve_h2t, i)
                for g in range(NG):
                    x = mm(M0[:, 0:D], attnT(b, g)[:, P * j:P * (j + 1)], wo[:, g, :], g == 0, g == NG - 1)
                x.then_inc(pe_op, 1)

            def h2_transpose(i):
                eng.wait_ge(dve_h2, i + 1)
                for k in range(2):
                    x = eng.transpose(M0[:, D + P * k:D + P * (k + 1)], H2[:, P * k:P * (k + 1)], identf[:, :])
                x.then_inc(pe_h2t, 1)

            def router(i):
                eng.wait_ge(dve_h2t, i + 1)
                if i >= 1:
                    eng.wait_ge(dve_idx, i)
                for k in range(2):
                    x = mm(M1[:, 0:E], H2T[:, P * k:P * (k + 1)], gw[:, k, :], k == 0, k == 1)
                x.then_inc(pe_lg, 1)

            def ranks(i):
                eng.wait_ge(dve_mk, i + 1)
                if i >= 1:
                    eng.wait_ge(dve_msum, i)
                mm(M1[:, E:2 * E], before[:, :], MK[:, :], True, False)
                mm(M1[:, E:2 * E], ones_b[:, :], MSUM[:, :], False, True).then_inc(pe_rank, 1)

            eng.wait_ge(dve_qt, 2 * TT)
            scores(0, 0)
            scores(0, 1)
            STEPS = NB * NG * KC
            for n in range(STEPS):
                if n + 1 < STEPS:
                    scores(n + 1, 0)
                if n >= 1:
                    attend(n - 1)
                if n + 1 < STEPS:
                    scores(n + 1, 1)
                b, m = n // (NG * KC), n % (NG * KC)
                if b >= 1:
                    for j in range(TB):
                        i = (b - 1) * TB + j
                        if m == 3 + 8 * j:
                            out_proj(i)
                        if m == 7 + 8 * j:
                            h2_transpose(i)
                        if m == 9 + 8 * j:
                            router(i)
                        if m == 15 + 8 * j:
                            ranks(i)
            attend(STEPS - 1)
            for i in range(TT - TB, TT):
                out_proj(i)
                h2_transpose(i)
                router(i)
                ranks(i)

            eng.wait_ge(dve_msum, TT)
            mm(M0[0:E, 0:1], MSUM[:, :], ones_b[:, 0:1], True, True).then_inc(pe_tab, 1)
            eng.wait_ge(chain_tab, 1)
            mm(M0[0:E, 8:9], upto[:, :], ctf[:, :], True, True)
            mm(M0[:, 384:384 + E], CTB, before[0:E, 0:E], True, True)
            mm(M0[0:1, 64:64 + E], cnt[:, :], identf[0:E, 0:E], True, True).then_inc(pe_tab, 1)
            eng.wait_ge(chain_tab, 2)
            CMP = A8[0:E, 0:NTAB]
            mm(M1[0:1, 0:NTAB], ones_f[:, :], CMP, True, True)
            mm(M1[0:1, 256:256 + NTAB], ctf[:, :], CMP, True, True)
            mm(M0[0:1, 256:256 + E], cum[:, :], identf[0:E, 0:E], True, True).then_inc(pe_tab, 1)

            def gate_up(o, xs, w, wlo):
                mm(o, xs(0), w(0), True, False)
                mm(o, xs(0), wlo(0), False, False)
                mm(o, xs(1), w(1), False, False)
                mm(o, xs(1), wlo(1), False, False)
                mm(o, xs(2), w(0), False, False)
                return mm(o, xs(3), w(1), False, True)

            def down(o, ht, w, wlo, first=True, last=True):
                mm(o, ht(0), w(0), first, False)
                mm(o, ht(0), wlo(0), False, False)
                mm(o, ht(1), w(1), False, False)
                mm(o, ht(1), wlo(1), False, False)
                mm(o, ht(2), w(0), False, False)
                return mm(o, ht(3), w(1), False, last)

            def h_transposes(j):
                for q in range(4):
                    x = eng.transpose(HTP[j][0:I2, P * q:P * (q + 1)],
                                      HHL[j][:, q // 2, I2 * (q % 2):I2 * (q % 2 + 1)], identb[:, :])
                return x

            def htv(j):
                return lambda q: HT[j][0:I2, P * q:P * (q + 1)]

            eng.wait_ge(w_split, N_SPLIT0)
            eng.wait_ge(dve_tab, 1)
            eng.wait_ge(dve_hl, TT)

            def sh_down(i):
                for s in range(2):
                    eng.wait_ge(sh_h, 2 * i + s + 1)
                    if i >= 1:
                        eng.wait_ge(sh_te, 2 * (i - 1) + s + 1)
                    h_transposes(s).then_inc(sh_t, 1)
                if i >= 1:
                    eng.wait_ge(sh_ye, i)
                for s in range(2):
                    eng.wait_ge(sh_te, 2 * i + s + 1)
                    w = SW[s]
                    x = down(YP[0], htv(s), lambda k: w[0:I2, DHI + D * k:DHI + D * (k + 1)],
                             lambda k: w[0:I2, DLO + D * k:DLO + D * (k + 1)], s == 0, s == 1)
                x.then_inc(sh_y, 1)

            for i in range(TT):
                for s in range(2):
                    if i >= 1:
                        eng.wait_ge(sh_h, 2 * (i - 1) + s + 1)
                    w = SW[s]
                    h2 = h2T_cols(i)
                    gate_up(GUP[s][:, 0:2 * IW], lambda q: h2[:, q, :], lambda k: w[:, 2 * IW * k:2 * IW * (k + 1)],
                            lambda k: w[:, WGU + 2 * IW * k:WGU + 2 * IW * (k + 1)]).then_inc(sh_gu, 1)
                if i >= 1:
                    sh_down(i - 1)
            sh_down(TT - 1)
            eng.wait_ge(sh_ye, TT)
            eng.transpose(HTP[0][0:I2, 0:P], HHL[0][:, 0, 0:I2], identb[:, :]).then_inc(tiles_done, 1)

            def t1(t, j, cnt_x):
                eng.wait_ge(xg_loaded[j], cnt_x)
                for q in range(4):
                    x = eng.transpose(XTP[j][:, P * q:P * (q + 1)], XG[j][:, P * q:P * (q + 1)], identb[:, :])
                x.then_inc(e_t1, 1)

            def gu(t, j, w):
                er = eng.value_load(TAB[0:1, ds(ET.start + t, 1)], min_val=0, max_val=5 * E + N_SPLIT0)
                eng.wait_ge(e_xt, t + 1)
                eng.wait_ge(w_split, er)
                x = XT[j]
                gate_up(GUP[j][:, 0:2 * IW], lambda q: x[:, P * q:P * (q + 1)], lambda k: wslot(w + 2 * IW * k, 2 * IW),
                        lambda k: wslot(w + (WGU + 2 * IW * k), 2 * IW)).then_inc(e_gu, 1)

            def t2(t, j):
                eng.wait_ge(e_h, t + 1)
                h_transposes(j).then_inc(e_t2, 1)

            def dn(t, j, w):
                eng.wait_ge(e_te, t + 1)
                down(YP[j], htv(j), lambda k: KT[0:I2, ds(w + (DHI + D * k), D)],
                     lambda k: KT[0:I2, ds(w + (DLO + D * k), D)]).then_inc(tiles_done, 1)

            def slot_of(t):
                return eng.value_load(TAB[0:1, ds(WB.start + t, 1)], min_val=0, max_val=(NSLOT - 1) * WSPLIT)

            n = eng.value_load(TAB[0:1, ET.stop - 1:ET.stop], min_val=0, max_val=T_MAX)
            t1(0, 0, 16)
            t1(1, 1, 16)
            gu(0, 0, slot_of(0))
            eng.wait_ge(e_xt, 1)
            t1(2, 0, 32)
            gu(1, 1, slot_of(1))
            t2(0, 0)
            with eng.Fori(0, (T_MAX + 1) // 2) as i:
                with eng.If(i < n):
                    wg = [slot_of(i * 2 + (2 + j)) for j in range(2)]
                    wd = [slot_of(i * 2 + j) for j in range(2)]
                    for j in range(2):
                        eng.wait_ge(e_xt, i * 2 + (2 + j))
                        t1(None, 1 - j, i * 16 + (32 + 16 * j))
                        eng.wait_ge(e_h, i * 2 + (1 + j))
                        gu(i * 2 + (2 + j), j, wg[j])
                        t2(i * 2 + (1 + j), 1 - j)
                        dn(i * 2 + j, j, wd[j])

        @block.vector
        def _(eng):
            links = [0]

            def link(x):
                links[0] += 1
                x.then_inc(chain, 1)
                eng.wait_ge(chain, links[0])

            def rsqrt(y, v, t, iv, n):
                link(eng.tensor_scalar(iv, v.bitcast(i32), 1, None, ALU.logical_shift_right))
                link(eng.tensor_scalar(y.bitcast(i32), iv, -1.0, float(0x5F3759DF), ALU.mult, ALU.add))
                for _ in range(4):
                    link(eng.tensor_tensor(t, y, y, ALU.mult))
                    link(eng.tensor_tensor(t, t, v, ALU.mult))
                    link(eng.tensor_scalar(t, t, -0.5, 1.5, ALU.mult, ALU.add))
                    link(eng.tensor_tensor(y, y, t, ALU.mult))

            eng.wait_ge(x_loaded, 16)
            for t in range(TT):
                link(eng.bn_stats(stats[:, :], ACC[:, t, :]))
                link(eng.bn_aggr(mv[:, t, :], stats[:, :]))
            link(eng.tensor_scalar(ve[:, :], mv[:, :, 1], EPS, None, ALU.add))
            rsqrt(rs[:, :], ve[:, :], rt[:, :], ri[:, :], TT)

            def kt_evac(c):
                r = KR[c]
                for g in range(2):
                    n = 2 * c + g
                    eng.wait_ge(pe_kt, n + 1)
                    bank = BANKS[2 + n % 2].bitcast(bf16).rearrange("p (h q) -> p h q", h=8)
                    eng.tensor_copy(KTv[0:AUG, 8 * g:8 * g + 8, c * P:c * P + r], bank[0:AUG, :, 0:r]).then_inc(dve_kt, 1)

            for c in range(KC):
                r = KR[c]
                ka = AUGT[c % 2][0:r]
                eng.wait_ge(act_v, 2 * c + 2)
                eng.tensor_tensor(R1[c % 2][0:r, :].rearrange("p (h d) -> p h d", h=NH),
                                  BANKS[c % 2][0:r, 0:D].rearrange("p (h d) -> p h d", h=NH),
                                  ka[:, :, DK:2 * DK], ALU.subtract).then_inc(dve_r1, 1)
                eng.tensor_reduce(KN[0:r, c, :], SQ[0:r, :].rearrange("p (h d) -> p h d", h=NH), AX.X,
                                  ALU.add).then_inc(dve_kn, 1)
                eng.wait_ge(act_km, c + 1)
                eng.wait_ge(dve_r1, c + 1)
                eng.tensor_tensor(ka[:, :, 0:DK], R1[c % 2][0:r, :].rearrange("p (h d) -> p h d", h=NH),
                                  ka[:, :, 2 * DK:3 * DK], ALU.subtract).then_inc(dve_ka, 1)
                if c >= 1:
                    kt_evac(c - 1)
            eng.wait_ge(dve_kn, KC)
            eng.tensor_reduce(kmax[:, :], KN[:, :, :].rearrange("p c h -> p h c"), AX.X, ALU.max).then_inc(dve_kn, 1)
            kt_evac(KC - 1)

            def qt_evac(t):
                for g in range(2):
                    n = 2 * t + g
                    eng.wait_ge(pe_qt, n + 1)
                    bank = BANKS[2 + n % 2].bitcast(bf16).rearrange("p (h q) -> p h q", h=8)
                    eng.tensor_copy(QTv[0:AUG, t // TB, 8 * g:8 * g + 8, P * (t % TB):P * (t % TB + 1)],
                                    bank[0:AUG, :, :]).then_inc(dve_qt, 1)

            eng.wait_ge(pool_kmax, 1)
            link(eng.tensor_scalar(knall[:, :], knall[:, :], -0.5 / DK ** 0.5, None, ALU.mult))
            for t in range(TT):
                if t >= 1:
                    eng.wait_ge(pe_xt, t)
                eng.tensor_scalar(XN, ACC[:, t, :], mv[:, t, 0:1], rs[:, t:t + 1], ALU.subtract,
                                  ALU.mult).then_inc(dve_xn, 1)
                eng.wait_ge(pe_xt, t + 1)
                if t >= 1:
                    eng.wait_ge(pe_q, t)
                eng.tensor_copy(XNT, PVB[0][:, 0:D]).then_inc(dve_xt, 1)
                if t >= 1:
                    qt_evac(t - 1)
                eng.wait_ge(act_v, 2 * KC + t + 1)
                eng.tensor_reduce(qn[:, :], SQ.rearrange("p (h d) -> p h d", h=NH), AX.X, ALU.add).then_inc(dve_qn, 1)
                eng.wait_ge(dve_qn, t + 1)
                link(eng.scalar_tensor_tensor(out=NM[:, t, :], in0=qn[:, :], scalar=-0.5 * DK ** 0.5, in1=knall[:, :],
                                              op0=ALU.mult, op1=ALU.add))
                if t == 0:
                    eng.wait_ge(pe_kt, 2 * KC)
                if t >= 2:
                    eng.wait_ge(pe_qt, 2 * (t - 1))
                qa = AUGT[t % 2]
                link(eng.tensor_copy(qa[:, :, NT * DK], NM[:, t, :]))
                eng.tensor_tensor(qa[:, :, NT * DK + 1], NM[:, t, :], qa[:, :, NT * DK], ALU.subtract).then_inc(dve_m, 1)
            qt_evac(TT - 1)
            link(eng.tensor_reduce(shmax[:, 1:2], NM[:, :, :].rearrange("p t h -> p (t h)"), AX.X, ALU.min))
            eng.tensor_scalar(shmax[:, 0:1], shmax[:, 1:2], -1.0, None, ALU.mult).then_inc(dve_top, 1)
            eng.wait_ge(pool_top, 1)
            eng.tensor_scalar(flag[:, :], shmax[:, 1:2], SHIFT_MAX, None, ALU.is_gt).then_inc(dve_flag, 1)
            eng.wait_ge(dve_flag, 1)
            general = eng.value_load(flag[0:1, 0:1], min_val=0, max_val=1)
            with eng.If(general > 0):
                with eng.Fori(0, NB) as b:
                    for j in range(TB):
                        for h in range(NH):
                            eng.wait_ge(gen_s, b * (TB * NH) + (j * NH + h + 1))
                            eng.tensor_reduce(MROW[:, h:h + 1], SP4[:, 0:KV], AX.X, ALU.max).then_inc(gen_m, 1)
                        eng.wait_ge(gen_m, b * (TB * NH) + (j + 1) * NH)
                        eng.tensor_scalar(MROW, MROW, -1.0, None, ALU.mult).then_inc(gen_chain, 1)
                        eng.wait_ge(gen_chain, b * (2 * TB) + (2 * j + 1))
                        eng.tensor_copy(MHL[:, :, 0], MROW).then_inc(gen_chain, 1)
                        eng.wait_ge(gen_chain, b * (2 * TB) + (2 * j + 2))
                        eng.tensor_tensor(MHL[:, :, 1], MROW, MHL[:, :, 0], ALU.subtract).then_inc(gen_split, 1)
                        eng.wait_ge(gen_t, b * TB + (j + 1))
                        for g in range(2):
                            bank = BANKS[6 + g].bitcast(bf16)
                            x = eng.tensor_copy(QT[NT * DK:AUG, ds(b * (NH * QB) + 8 * g * QB, 8 * QB)]
                                                .rearrange("p (h q) -> p h q", h=8)[:, :, P * j:P * (j + 1)],
                                                bank[NT * DK:AUG, :].rearrange("p (h q) -> p h q", h=8))
                        x.then_inc(gen_qt, 1)
            eng.nop()

            def normalise(q):
                b, g = q // NG, q % NG
                eng.wait_ge(pe_pv, KC * (q + 1))
                eng.wait_ge(dve_attn, q) if q else None
                eng.tensor_copy(OS, PVB[q % 2][:, :]).then_inc(dve_pv, 1)
                eng.wait_ge(dve_pv, q + 1)
                link(eng.stream_shuffle(RS, OS, [DK] * 32))
                link(eng.reciprocal(RS, RS))
                eng.tensor_tensor(attnT(b, g), OS, RS, ALU.mult).then_inc(dve_attn, 1)

            def residual(i):
                eng.wait_ge(pe_op, i + 1)
                link(eng.scalar_tensor_tensor(out=ACC[:, i, :], in0=M0[:, 0:D], scalar=tg[:, 0:1], in1=ACC[:, i, :],
                                              op0=ALU.mult, op1=ALU.add))
                link(eng.bn_stats(stats[:, :], ACC[:, i, :]))
                link(eng.bn_aggr(mv[:, 0, :], stats[:, :]))
                link(eng.tensor_scalar(ve[:, 0:1], mv[:, 0, 1:2], EPS, None, ALU.add))
                rsqrt(rs[:, 0:1], ve[:, 0:1], rt[:, 0:1], ri[:, 0:1], 1)
                if i >= 1:
                    eng.wait_ge(pool_xr, 2 * i)
                    eng.wait_ge(pe_h2t, i)
                eng.tensor_scalar(H2, ACC[:, i, :], mv[:, 0, 0:1], rs[:, 0:1], ALU.subtract, ALU.mult).then_inc(dve_h2, 1)
                eng.wait_ge(dve_h2, i + 1)

            def h2_parts(i):
                eng.wait_ge(pe_h2t, i + 1)
                if i >= 1:
                    eng.wait_ge(pe_lg, i)
                eng.tensor_copy(H2T, M0[:, D:2 * D]).then_inc(dve_h2t, 1)
                eng.wait_ge(dve_h2t, i + 1)
                h2 = h2T_cols(i)
                src = H2T.rearrange("p (c q) -> p c q", c=2)
                link(eng.tensor_copy(h2[:, 0:2, :], src))
                eng.tensor_tensor(h2[:, 2:4, :], src, h2[:, 0:2, :], ALU.subtract).then_inc(dve_hl, 1)
                eng.wait_ge(dve_hl, i + 1)

            A8v = A8.rearrange("p (k e) -> p k e", k=K8)
            PXv = PX.rearrange("p (k e) -> p k e", k=K8)

            def choose(i):
                eng.wait_ge(act_sig, i + 1)
                link(eng.tensor_scalar(CF[:, :], EX[:, :], 1.0, None, ALU.add))
                link(eng.reciprocal(SCO[:, :], CF[:, :]))
                link(eng.tensor_tensor(CF[:, :], SCO[:, :], bias[:, :], ALU.add))
                for g in range(8):
                    x = eng.max(G8[:, 8 * g:8 * g + 8], CF[:, 8 * g:8 * g + 8])
                link(x)
                g8 = G8[:, :].rearrange("p (g k) -> p g k", k=8)
                link(eng.tensor_tensor(GS[:, :], g8[:, :, 0], g8[:, :, 1], ALU.add))
                link(eng.max(T8[:, :], GS[:, :]))
                link(eng.max_index(I8[:, :], T8[:, :], GS[:, :]))
                link(eng.tensor_copy(F8[:, :], I8[:, :]))
                a4 = A8[:, 0:32].rearrange("p (g j) -> p g j", j=4)
                link(eng.tensor_tensor(a4, iota_e[:, 0:8].rearrange("p (g o) -> p g o", o=1).broadcast_to((P, 8, 4)),
                                       F8[:, 0:4].rearrange("p (o j) -> p o j", o=1).broadcast_to((P, 8, 4)), ALU.is_equal))
                link(eng.tensor_reduce(GM[:, :], a4, AX.X, ALU.add))
                cf = CF[:, :].rearrange("p (g k) -> p g k", k=8)
                link(eng.tensor_tensor(cf, cf, GM[:, :].rearrange("p (g o) -> p g o", o=1).broadcast_to((P, 8, 8)), ALU.mult))
                link(eng.tensor_scalar(CF[:, :], CF[:, :], 0.0, None, ALU.add))
                link(eng.max(T8[:, :], CF[:, :]))
                link(eng.max_index(I8[:, :], T8[:, :], CF[:, :]))
                link(eng.tensor_copy(F8[:, :], I8[:, :]))
                link(eng.tensor_copy(CHOSEN[:, i, :], F8[:, :]))
                link(eng.tensor_tensor(A8v, iota_e[:, :].rearrange("p (o e) -> p o e", o=1).broadcast_to((P, K8, E)),
                                       F8[:, :].rearrange("p (k o) -> p k o", o=1).broadcast_to((P, K8, E)), ALU.is_equal))
                if i >= 1:
                    eng.wait_ge(pe_rank, i)
                with nc.allow_low_precision("ones and zeros"):
                    eng.tensor_reduce(MK[:, :], A8v.rearrange("p k e -> p e k"), AX.X, ALU.add).then_inc(dve_mk, 1)
                eng.wait_ge(dve_mk, i + 1)

            def place(i):
                eng.wait_ge(pe_rank, i + 1)
                link(eng.tensor_tensor(POS[:, :], M1[:, E:2 * E], base_e[:, :], ALU.add))
                eng.tensor_tensor(MSUM[:, :], MSUM[:, :], MK[:, :], ALU.add).then_inc(dve_msum, 1)
                eng.wait_ge(dve_msum, i + 1)
                link(eng.tensor_tensor(PXv, A8v, POS[:, :].rearrange("p (o e) -> p o e", o=1).broadcast_to((P, K8, E)), ALU.mult))
                link(eng.tensor_reduce(W8[:, :], PXv, AX.X, ALU.add))
                eng.tensor_copy(IDX[:, i, :], W8[:, :]).then_inc(dve_idx, 1)
                eng.wait_ge(dve_idx, i + 1)
                link(eng.tensor_tensor(PXv, A8v, SCO[:, :].rearrange("p (o e) -> p o e", o=1).broadcast_to((P, K8, E)), ALU.mult))
                link(eng.tensor_reduce(W8[:, :], PXv, AX.X, ALU.add))
                link(eng.tensor_reduce(W1[:, 0:1], W8[:, :], AX.X, ALU.add))
                link(eng.tensor_scalar(W1[:, 0:1], W1[:, 0:1], 1e-20, None, ALU.add))
                link(eng.reciprocal(W1[:, 1:2], W1[:, 0:1]))
                link(eng.tensor_scalar(W8[:, :], W8[:, :], W1[:, 1:2], SCALE_OUT, ALU.mult, ALU.mult))
                link(eng.tensor_scalar(WK[:, i, :], W8[:, :], tg[:, 1:2], None, ALU.mult))

            eng.wait_ge(gates_done, 1)
            eng.wait_ge(pe_qt, 2 * TT)
            eng.wait_ge(pool_ql, TT)
            for b in range(NB):
                i = (b - 1) * TB
                if b >= 1:
                    residual(i)
                    h2_parts(i)
                    choose(i)
                    residual(i + 1)
                normalise(b * NG)
                if b >= 1:
                    place(i)
                    h2_parts(i + 1)
                    choose(i + 1)
                    residual(i + 2)
                    place(i + 1)
                    h2_parts(i + 2)
                    choose(i + 2)
                normalise(b * NG + 1)
                if b >= 1:
                    residual(i + 3)
                    place(i + 2)
                    h2_parts(i + 3)
                    choose(i + 3)
                normalise(b * NG + 2)
                if b >= 1:
                    place(i + 3)
                normalise(b * NG + 3)
            for i in range(TT - TB, TT):
                residual(i)
                h2_parts(i)
                choose(i)
                place(i)

            eng.wait_ge(pe_tab, 1)
            link(eng.tensor_copy(cnt[:, :], M0[0:E, 0:1]))
            link(eng.tensor_scalar(cti[:, :], cnt[:, :], float(P - 1), None, ALU.add))
            link(eng.tensor_scalar(cti[:, :], cti[:, :], 7, None, ALU.logical_shift_right))
            link(eng.tensor_copy(ctf[:, :], cti[:, :]))
            eng.tensor_scalar(CTB, ones_b[0:E, :], ctf[:, 0:1], None, ALU.mult).then_inc(chain_tab, 1)
            eng.wait_ge(pe_tab, 2)
            link(eng.tensor_copy(cum[:, :], M0[0:E, 8:9]))
            link(eng.scalar_tensor_tensor(out=DELTA, in0=M0[:, 384:384 + E], scalar=float(P), in1=base_e[:, :],
                                          op0=ALU.mult, op1=ALU.subtract))
            link(eng.tensor_tensor(TAB[0:1, PADR.start:PADR.start + E], M0[0:1, 64:64 + E], base_e[0:1, :], ALU.add))
            eng.tensor_scalar(A8[0:E, 0:NTAB], iota_t[:, :], cum[:, 0:1], None, ALU.is_ge).then_inc(chain_tab, 1)
            eng.wait_ge(pe_tab, 3)
            tf = TABF
            link(eng.tensor_copy(tf[0:1, ET], M1[0:1, 0:NTAB]))
            link(eng.scalar_tensor_tensor(out=tf[0:1, RT], in0=M1[0:1, 256:256 + NTAB], scalar=-1.0, in1=iota_t[0:1, :],
                                          op0=ALU.mult, op1=ALU.add))
            link(eng.tensor_scalar(tf[0:1, WB], tf[0:1, ET], float(REGION), None, ALU.mult))
            link(eng.scalar_tensor_tensor(out=TAB[0:1, RT], in0=tf[0:1, RT], scalar=float(P), in1=tf[0:1, WB],
                                          op0=ALU.mult, op1=ALU.add))
            link(eng.tensor_scalar(TAB[0:1, WB], tf[0:1, ET], float(E - 1), None, ALU.min))
            link(eng.tensor_scalar(TAB[0:1, WB], TAB[0:1, WB], NSLOT - 1, None, ALU.bitwise_and))
            link(eng.tensor_scalar(TAB[0:1, WB], TAB[0:1, WB], float(WSPLIT), None, ALU.mult))
            link(eng.tensor_scalar(tf[0:1, ET], tf[0:1, ET], float(E - 1), None, ALU.min))
            link(eng.tensor_scalar(TAB[0:1, ET], tf[0:1, ET], 5.0, float(N_SPLIT0 + 5), ALU.mult, ALU.add))
            link(eng.tensor_scalar(tf[0:1, 0:1], M1[0:1, 255 + NTAB:256 + NTAB], 1.0, None, ALU.add))
            link(eng.tensor_copy(TAB[0:1, ET.stop - 1:ET.stop], tf[0:1, 0:1]))
            link(eng.tensor_scalar(TAB[0:1, ET.stop - 1:ET.stop], TAB[0:1, ET.stop - 1:ET.stop], 1, None, ALU.logical_shift_right))
            link(eng.memset(TAB[0:1, WAITC.start:WAITC.start + NSLOT], 1))
            eng.tensor_scalar(TAB[0:1, WAITC.start + NSLOT:WAITC.start + E], M0[0:1, 256:256 + E - NSLOT], 1.0, None,
                              ALU.add).then_inc(dve_tab, 1)
            eng.wait_ge(dve_tab, 1)

            def hidden(j):
                return eng.tensor_tensor(HF[j], SIL[j], GUP[j][:, IW:2 * IW], ALU.mult)

            def result_rows(i):
                link(eng.tensor_tensor(A8v, iota_e[:, :].rearrange("p (o e) -> p o e", o=1).broadcast_to((P, K8, E)),
                                       CHOSEN[:, i, :].rearrange("p (k o) -> p k o", o=1).broadcast_to((P, K8, E)), ALU.is_equal))
                link(eng.tensor_tensor(PXv, A8v, DELTA.rearrange("p (o e) -> p o e", o=1).broadcast_to((P, K8, E)), ALU.mult))
                link(eng.tensor_reduce(W8[:, :], PXv, AX.X, ALU.add))
                eng.tensor_tensor(IDX2[:, i, :], IDX[:, i, :], W8[:, :], ALU.add).then_inc(dve_idx2, 1)
                eng.wait_ge(dve_idx2, i + 1)

            for i in range(TT):
                result_rows(i)
                for s in range(2):
                    eng.wait_ge(sh_sil, 2 * i + s + 1)
                    link(hidden(s))
                    if i >= 1:
                        eng.wait_ge(sh_t, 2 * (i - 1) + s + 1)
                    link(eng.tensor_copy(HHL[s][:, 0, :], HF[s]))
                    eng.tensor_tensor(HHL[s][:, 1, :], HF[s], HHL[s][:, 0, :], ALU.subtract).then_inc(sh_h, 1)
                if i >= 1:
                    eng.wait_ge(sh_y, i)
                    eng.scalar_tensor_tensor(out=ACC[:, i - 1, :], in0=YP[0], scalar=tg[:, 1:2], in1=ACC[:, i - 1, :],
                                             op0=ALU.mult, op1=ALU.add).then_inc(sh_ye, 1)
            eng.wait_ge(sh_y, TT)
            eng.scalar_tensor_tensor(out=ACC[:, TT - 1, :], in0=YP[0], scalar=tg[:, 1:2], in1=ACC[:, TT - 1, :],
                                     op0=ALU.mult, op1=ALU.add).then_inc(sh_ye, 1)

            def xt_evac(t, j):
                eng.wait_ge(e_t1, t + 1)
                eng.tensor_copy(XT[j], XTP[j]).then_inc(e_xt, 1)

            def h_split(t, j, link_to):
                eng.wait_ge(e_sil, t + 1)
                hidden(j).then_inc(e_link, 1)
                eng.wait_ge(e_link, link_to)
                eng.tensor_copy(HHL[j][:, 0, :], HF[j]).then_inc(e_link, 1)
                eng.wait_ge(e_link, link_to + 1)
                eng.tensor_tensor(HHL[j][:, 1, :], HF[j], HHL[j][:, 0, :], ALU.subtract).then_inc(e_h, 1)

            n = eng.value_load(TAB[0:1, ET.stop - 1:ET.stop], min_val=0, max_val=T_MAX)
            xt_evac(0, 0)
            xt_evac(1, 1)
            h_split(0, 0, 1)
            eng.wait_ge(e_gu, 1)
            xt_evac(2, 0)
            h_split(1, 1, 3)
            with eng.Fori(0, (T_MAX + 1) // 2) as i:
                with eng.If(i < n):
                    for j in range(2):
                        eng.wait_ge(e_gu, i * 2 + (2 + j))
                        xt_evac(i * 2 + (3 + j), 1 - j)
                        eng.wait_ge(e_t2, i * 2 + (1 + j))
                        h_split(i * 2 + (2 + j), j, i * 4 + (5 + 2 * j))

            for i in range(TT):
                for k in range(K8):
                    eng.wait_ge(gathered[k], 16 * (i + 1))
                    if k >= 1 or i >= 1:
                        eng.wait_ge(dve_comb, K8 * i + k)
                    eng.scalar_tensor_tensor(out=ACC[:, i, :], in0=RING[:, k, :], scalar=WK[:, i, k:k + 1],
                                             in1=ACC[:, i, :], op0=ALU.mult, op1=ALU.add).then_inc(dve_comb, 1)


def kernel(x, ctx_1024, g_xattn, g_ffn, L0_xattn_w_q, L0_xattn_w_k, L0_xattn_w_v, L0_xattn_w_o, L0_ffn_gate_w,
           L0_ffn_gate_bias, L0_ffn_Wg, L0_ffn_Wu, L0_ffn_Wd, L0_ffn_Sg, L0_ffn_Su, L0_ffn_Sd):
    import numpy as np
    import concourse.bacc as bacc
    from concourse.bass_utils import run_bass_kernel_spmd

    a = np.asarray
    S, D = x.shape[1], x.shape[2]
    E, IW = L0_ffn_Wg.shape[0], L0_ffn_Wg.shape[1]
    I2 = IW // 2

    def chunks(w):
        w = a(w)
        return w.reshape(w.shape[0] // 128, 128, w.shape[1]).transpose(1, 0, 2)

    wo = np.zeros((4, 4, 32, D), np.float32)
    wo[:, :, 0:16, :] = a(L0_xattn_w_o).T.reshape(4, 4, 16, D)
    gate = np.concatenate([a(L0_ffn_Wg), a(L0_ffn_Sg).reshape(2, IW, D)])
    up = np.concatenate([a(L0_ffn_Wu), a(L0_ffn_Su).reshape(2, IW, D)])
    gu = np.concatenate([gate, up], axis=1)
    wgu = gu.transpose(0, 2, 1).reshape(E + 2, 2, 128, 2 * IW).transpose(0, 2, 1, 3).reshape(E + 2, 128, 4 * IW)
    down = np.concatenate([a(L0_ffn_Wd), a(L0_ffn_Sd).reshape(D, 2, IW).transpose(1, 0, 2)])
    wd = down.transpose(0, 2, 1).reshape(E + 2, 2, I2, D).transpose(0, 2, 1, 3).reshape(E + 2, I2, 2 * D)
    arrays = {
        "x": a(x).reshape(S, D),
        "ctxT": chunks(a(ctx_1024)[0].T),
        "wq": chunks(a(L0_xattn_w_q).T),
        "wkv": chunks(np.concatenate([a(L0_xattn_w_k), a(L0_xattn_w_v)]).T),
        "wo": wo.reshape(4, 128, D).transpose(1, 0, 2),
        "router": chunks(a(L0_ffn_gate_w).T),
        "bias": a(L0_ffn_gate_bias).reshape(1, E),
        "gates": np.concatenate([a(g_xattn).reshape(1), a(g_ffn).reshape(1)]).reshape(1, 2),
        "wgu": wgu,
        "wd": wd,
    }
    arrays = {"in_" + k: np.ascontiguousarray(v) for k, v in arrays.items()}
    nc = bacc.Bacc("TRN2", target_bir_lowering=False, num_devices=1)
    args = [nc.dram_tensor(k, v.shape, mybir.dt.from_np(v.dtype), kind="ExternalInput").ap() for k, v in arrays.items()]
    args.append(nc.dram_tensor("out", (S, D), mybir.dt.float32, kind="ExternalOutput").ap())
    flamingo_gated_block(nc, *args)
    r = run_bass_kernel_spmd(nc, [arrays], core_ids=[0])
    return r.results[0]["out"].reshape(x.shape)
```

```python
import concourse.bass as bass
from concourse import mybir
from contextlib import ExitStack


def flamingo_gated_block(
    nc: bass.Bass,
    x_in: bass.AP,
    ctxT_in: bass.AP,
    wq_in: bass.AP,
    wkv_in: bass.AP,
    wo_in: bass.AP,
    router_in: bass.AP,
    bias_in: bass.AP,
    gates_in: bass.AP,
    w_in: bass.AP,
    out: bass.AP,
):
    f32 = mybir.dt.float32
    bf16 = mybir.dt.bfloat16
    i32 = mybir.dt.int32
    u32 = mybir.dt.uint32
    ALU = mybir.AluOpType
    ACT = mybir.ActivationFunctionType
    AX = mybir.AxisListType
    RMAX = bass.bass_isa.ReduceOp.max
    ds = bass.ds

    P = 128
    S, D = x_in.shape
    KV = ctxT_in.shape[2]
    NH = 16
    DK = D // NH
    TT = S // P
    KC = -(-KV // P)
    KR = [min(P, KV - P * c) for c in range(KC)]
    QB = 512
    NB = S // QB
    TB = QB // P
    NG = NH // 4
    NT = 6
    AUG = NT * DK + 2
    EPS = 1e-5
    SHIFT_MAX = 40.0

    E = router_in.shape[2]
    K8 = 8
    WALL = w_in.shape[2]
    WGU = WALL - 2 * D
    IW = WGU // 4
    I2 = IW // 2
    WSPLIT = 2 * WALL
    DHI = WGU
    DLO = WALL + WGU
    NSTG = 4
    NSLOT = 8
    REGION = S + P
    T_MAX = K8 * S // P + E - 1
    NTAB = 200
    SCALE_OUT = 2.5

    dispatch = nc.dram_tensor("dispatch_rows", (E * REGION + P, 2 * D), bf16).ap()
    T_MIN = K8 * S // P
    U = 4
    STEPS_MAX = -(-T_MAX // U)
    expert_out = nc.dram_tensor("expert_rows", (U * STEPS_MAX * P, D), f32).ap()

    ctx = ExitStack()
    with ctx:
        def sb(name, shape, dt):
            return ctx.enter_context(nc.sbuf_tensor(name, shape, dt))

        def sem(name):
            return ctx.enter_context(nc.semaphore(name))

        KT = sb("KT", [P, NH * KV + 16], bf16)
        QT = sb("QT", [P, NB * NH * QB], bf16)
        VA = sb("VA", [P, KC * NH * 32], f32)
        PR = sb("PR", [P, 3 * 4 * QB], f32)
        ACC = sb("ACC", [P, TT, D], f32)
        SCR = sb("SCR", [P, 3584], f32)
        wo = sb("wo", [P, NG, D], f32)
        gw = sb("gw", [P, 2, E], f32)
        bias = sb("bias", [P, E], f32)
        gates = sb("gates", [P, 2], f32)
        tg = sb("tg", [P, 2], f32)
        identf = sb("identf", [P, P], f32)
        identb = sb("identb", [P, P], bf16)
        before = sb("before", [P, P], bf16)
        upto = sb("upto", [E, E], f32)
        ones_b = sb("ones_b", [P, P], bf16)
        ones_f = sb("ones_f", [E, 1], f32)
        zrow = sb("zrow", [P, 2 * D], bf16)
        iota_e = sb("iota_e", [P, E], f32)
        base_e = sb("base_e", [P, E], f32)
        iota_t = sb("iota_t", [E, NTAB], f32)
        turn = sb("turn", [P, 1 + NSLOT], f32)
        stats = sb("stats", [P, 6], f32)
        mv = sb("mv", [P, TT, 2], f32)
        rs = sb("rs", [P, TT], f32)
        rt = sb("rt", [P, TT], f32)
        ri = sb("ri", [P, TT], i32)
        ve = sb("ve", [P, TT], f32)
        kmax = sb("kmax", [P, NH], f32)
        knall = sb("knall", [P, NH], f32)
        NM = sb("NM", [P, TT, NH], f32)
        qn = sb("qn", [P, NH], f32)
        shmax = sb("shmax", [P, 2], f32)
        flag = sb("flag", [P, 1], i32)
        EX = sb("EX", [P, E], f32)
        SCO = sb("SCO", [P, E], f32)
        CF = sb("CF", [P, E], f32)
        G8 = sb("G8", [P, E], f32)
        GS = sb("GS", [P, 8], f32)
        T8 = sb("T8", [P, 8], f32)
        I8 = sb("I8", [P, 8], u32)
        F8 = sb("F8", [P, 8], f32)
        GM = sb("GM", [P, 8], f32)
        W8 = sb("W8", [P, 8], f32)
        W1 = sb("W1", [P, 2], f32)
        MK = sb("MK", [P, E], bf16)
        MSUM = sb("MSUM", [P, E], bf16)
        POS = sb("POS", [P, E], f32)
        IDX = sb("IDX", [P, TT, K8], u32)
        WK = sb("WK", [P, TT, K8], f32)
        cnt = sb("cnt", [E, 1], f32)
        cti = sb("cti", [E, 1], i32)
        ctf = sb("ctf", [E, 1], f32)
        cum = sb("cum", [E, 1], f32)

        SP4 = ctx.enter_context(nc.psum_tensor("SP4", [P, 4 * 512], f32))
        PVB = [ctx.enter_context(nc.psum_tensor(f"PVB{i}", [P, 512], f32)) for i in range(2)]
        M0 = ctx.enter_context(nc.psum_tensor("M0", [P, 512], f32))
        M1 = ctx.enter_context(nc.psum_tensor("M1", [P, 512], f32))
        BANKS = [SP4[:, 512 * i:512 * i + 512] for i in range(4)] + [PVB[0][:, :], PVB[1][:, :], M0[:, :], M1[:, :]]

        KTv = KT[:, 0:NH * KV].rearrange("p (h k) -> p h k", h=NH)
        QTv = QT[:, :].rearrange("p (b h q) -> p b h q", b=NB, h=NH)
        VAv = VA[:, :].rearrange("p (c h d) -> p c h d", c=KC, h=NH)
        PRv = PR[:, :].rearrange("p (s h q) -> p s h q", s=3, h=4)

        KN = QT[:, 0:2 * KC * NH].bitcast(f32).rearrange("p (c h) -> p c h", c=KC)

        def attnT(b, g):
            o = (b * NH + 4 * g) * QB
            return QT[:, o:o + 2 * QB].bitcast(f32)

        def h2T_cols(i):
            b, j = i // TB, i % TB
            o = b * NH * QB
            v = QT[:, o:o + NH * QB].rearrange("p (g r) -> p g r", g=4)
            return v[:, :, 2 * QB + P * j:2 * QB + P * (j + 1)]

        ctxT = PR[:, 0:2 * KV].rearrange("p (c k) -> p c k", c=2)
        wkv = PR[:, 2 * KV:2 * KV + 1024].rearrange("p (c n) -> p c n", c=2)
        wq = PR[:, 2 * KV + 1024:2 * KV + 1536].rearrange("p (c n) -> p c n", c=2)
        AW = NH * AUG
        AUGT = [SCR[:, j * (AW // 2):(j + 1) * (AW // 2)].bitcast(bf16).rearrange("p (h a) -> p h a", h=NH)
                for j in range(2)]
        o = 2 * KV + 1536
        AUGT.append(PR[:, o:o + AW // 2].bitcast(bf16).rearrange("p (h a) -> p h a", h=NH))
        SQ = SCR[:, AW:AW + D]
        R1 = [SCR[:, AW + D * (1 + j):AW + D * (2 + j)] for j in range(2)]
        QS = [SCR[:, AW + 3 * D:AW + 4 * D], PR[:, o + AW // 2:o + AW // 2 + D]]
        XN = SCR[:, AW + 4 * D:AW + 5 * D]
        XNT = SCR[:, AW + 5 * D:AW + 6 * D]
        CHOSEN = NM[:, 0:TT // 2, :].rearrange("p t (u k) -> p (t u) k", k=K8)
        IDX2 = NM[:, TT // 2:TT, :].bitcast(u32).rearrange("p t (u k) -> p (t u) k", k=K8)
        MROW = SCR[:, 0:NH]
        MHL = SCR[:, NH:2 * NH].bitcast(bf16).rearrange("p (h t) -> p h t", h=NH)

        OS = SCR[:, 0:512]
        RS = SCR[:, 512:1024]
        H2 = SCR[:, 1024:1280]
        H2T = SCR[:, 1280:1536]
        XR = [SCR[:, 1536 + D * j:1536 + D * (j + 1)].bitcast(bf16) for j in range(4)]
        TABF = SCR[0:1, 0:5 * NTAB]
        CTB = EX[0:E, :].bitcast(bf16)
        DELTA = POS[:, :]
        A8 = SCR[:, 2560:3072]
        PX = SCR[:, 3072:3584]

        def wslot(o, n):
            return KT[:, ds(o, n)]
        STG = [KT[:, (NSLOT + j) * WSPLIT:(NSLOT + j + 1) * WSPLIT].bitcast(f32) for j in range(2)] \
            + [VA[:, 4224 + WALL * j:4224 + WALL * (j + 1)] for j in range(2)]
        SW = [PR[:, (WSPLIT // 2) * s:(WSPLIT // 2) * (s + 1)].bitcast(bf16) for s in range(2)]
        RING = PR[:, WSPLIT:WSPLIT + K8 * D].rearrange("p (k n) -> p k n", k=K8)
        XG = [VA[:, D * j:D * (j + 1)].bitcast(bf16) for j in range(2)] \
            + [PR[:, 5280 + D * j:5280 + D * (j + 1)].bitcast(bf16) for j in range(2)]
        XT = [VA[:, 512 + 256 * j:512 + 256 * (j + 1)].bitcast(bf16) for j in range(2)]
        SIL = [VA[:, 1024 + IW * j:1024 + IW * (j + 1)] for j in range(2)]
        HF = [VA[:, 1376 + IW * j:1376 + IW * (j + 1)] for j in range(2)]
        HHL = [VA[:, 1728 + IW * j:1728 + IW * (j + 1)].bitcast(bf16).rearrange("p (t n) -> p t n", t=2) for j in range(2)]
        HT = [VA[:, 2080 + 256 * j:2080 + 256 * (j + 1)].bitcast(bf16) for j in range(2)]
        YB = [VA[:, 2592 + D * j:2592 + D * (j + 1)] for j in range(2)]
        TAB = VA[0:1, 3200:3200 + 5 * NTAB].bitcast(i32)
        PACK = PR[0:1, WSPLIT + K8 * D:WSPLIT + K8 * D + NTAB].bitcast(i32)
        XTP = [BANKS[j][:, 0:256].bitcast(bf16) for j in range(2)]
        GUP = [BANKS[2 + j] for j in range(2)]
        HTP = [BANKS[4 + j][:, 0:256].bitcast(bf16) for j in range(2)]
        YP = [BANKS[6 + j][:, 0:D] for j in range(2)]

        ctx_in = sem("ctx_in"); wkv_in_s = sem("wkv_loaded"); x_loaded = sem("x_loaded"); wq_loaded = sem("wq_loaded")
        small_loaded = sem("small_loaded")
        consts = sem("consts")
        gates_done = sem("gates_done")
        pe_kv = sem("pe_kv"); act_kh = sem("act_kh"); act_v = sem("act_v"); dve_r1 = sem("dve_r1"); act_km = sem("act_km")
        dve_ka = sem("dve_ka"); pe_kt = sem("pe_kt"); dve_kt = sem("dve_kt"); dve_kn = sem("dve_kn"); pool_kmax = sem("pool_kmax")
        dve_xn = sem("dve_xn"); pe_xt = sem("pe_xt"); dve_xt = sem("dve_xt"); pe_q = sem("pe_q"); act_qs = sem("act_qs")
        act_qh = sem("act_qh"); pool_r1 = sem("pool_r1"); act_qm = sem("act_qm"); pool_ql = sem("pool_ql"); dve_qn = sem("dve_qn")
        dve_m = sem("dve_m"); pe_qt = sem("pe_qt"); dve_qt = sem("dve_qt")
        dve_top = sem("dve_top"); pool_top = sem("pool_top"); dve_flag = sem("dve_flag")
        gen_s = sem("gen_s"); gen_m = sem("gen_m"); gen_split = sem("gen_split"); gen_t = sem("gen_t"); gen_qt = sem("gen_qt")
        gen_chain = sem("gen_chain")
        pe_qk = sem("pe_qk"); act_exp = sem("act_exp"); pe_pv = sem("pe_pv"); dve_pv = sem("dve_pv"); dve_attn = sem("dve_attn")
        pe_op = sem("pe_op"); dve_h2 = sem("dve_h2"); pool_xr = sem("pool_xr"); pe_h2t = sem("pe_h2t"); dve_h2t = sem("dve_h2t")
        dve_hl = sem("dve_hl"); pe_lg = sem("pe_lg"); act_sig = sem("act_sig"); dve_mk = sem("dve_mk"); pe_rank = sem("pe_rank")
        dve_msum = sem("dve_msum"); dve_idx = sem("dve_idx")
        scattered = [sem(f"scattered{j}") for j in range(4)]
        dummy_zero = sem("dummy_zero"); padded = sem("padded")
        pe_tab = sem("pe_tab"); dve_tab = sem("dve_tab")
        w_loaded = [sem(f"w_loaded{j}") for j in range(NSTG)]
        w_first = [sem(f"w_first{j}") for j in range(2)]
        w_split = sem("w_split")
        tiles_done = sem("tiles_done")
        sh_gu = sem("sh_gu"); sh_sil = sem("sh_sil"); sh_h = sem("sh_h"); sh_t = sem("sh_t"); sh_te = sem("sh_te"); sh_y = sem("sh_y"); sh_ye = sem("sh_ye")
        xg_loaded = [sem(f"xg_loaded{j}") for j in range(U)]
        e_t1 = sem("e_t1"); e_xt = sem("e_xt"); e_gu = sem("e_gu"); e_sil = sem("e_sil"); e_h = sem("e_h"); e_t2 = sem("e_t2")
        e_te = sem("e_te"); e_ye = sem("e_ye")
        y_stored = [sem(f"y_stored{j}") for j in range(2)]
        gathered = [sem(f"gathered{k}") for k in range(K8)]
        dve_comb = sem("dve_comb"); out_done = sem("out_done")
        chain = sem("vector_chain")
        pchain = sem("pool_chain"); chain_tab = sem("dve_tab_parts"); e_link = sem("hidden_chain"); rows_done = sem("rows_done"); rest_zero = sem("rest_zero"); dve_idx2 = sem("dve_idx2")

        N_SPLIT0 = 2
        ET, RT, WB, PADR, WAITC = (slice(NTAB * n, NTAB * (n + 1)) for n in range(5))
        def registers(eng, ap, most):
            return nc.values_load_multi_w_load_instructions(ap, engines=[eng.engine], min_val=0, max_val=most)[1]

        block = ctx.enter_context(nc.Block())

        @block.sync
        def _(eng):
            eng.dma_start(ctxT, ctxT_in).then_inc(ctx_in, 16)
            eng.dma_start(wkv, wkv_in).then_inc(wkv_in_s, 16)
            eng.dma_start(ACC[:, :, :], x_in.rearrange("(t p) n -> p t n", p=P)).then_inc(x_loaded, 16)
            eng.dma_start(wq, wq_in).then_inc(wq_loaded, 16)
            eng.dma_start(gates[:, :], gates_in.broadcast_to((P, 2))).then_inc(small_loaded, 16)
            eng.dma_start(bias[:, :], bias_in.broadcast_to((P, E))).then_inc(small_loaded, 16)
            eng.dma_start(wo[:, :, :], wo_in).then_inc(small_loaded, 16)
            eng.dma_start(gw[:, :, :], router_in).then_inc(small_loaded, 16)
            eng.wait_ge(consts, 1)
            eng.dma_start(expert_out[T_MIN * P:, :].rearrange("(t p) n -> p t n", p=P),
                          zrow[:, :].bitcast(f32).rearrange("p (o n) -> p o n", o=1).broadcast_to((P, U * STEPS_MAX - T_MIN, D)))\
               .then_inc(rest_zero, 16)
            eng.dma_start(dispatch[E * REGION:E * REGION + P, :], zrow[:, :]).then_inc(dummy_zero, 16)
            eng.wait_ge(dve_tab, 1)
            with eng.Fori(0, E) as e:
                r = eng.value_load(TAB[0:1, ds(PADR.start + e, 1)], min_val=0, max_val=E * REGION - P)
                eng.dma_start(dispatch[ds(r, P), :], zrow[:, :]).then_inc(padded, 16)
            eng.wait_ge(padded, 16 * E)
            eng.wait_ge(rest_zero, 16)
            eng.wait_ge(dummy_zero, 16)
            for j in range(4):
                eng.wait_ge(scattered[j], 16 * K8 * TT // 4)

            def load(t4, first_time=False):
                first = registers(eng, TAB[0:1, ds(t4 * U + RT.start, U)], E * REGION)
                for j in range(U):
                    if not first_time:
                        eng.wait_ge(e_t1, t4 * U + (j + 1 - U))
                    eng.dma_start(XG[j], dispatch[ds(first[j], P), :]).then_inc(xg_loaded[j], 16)

            n = eng.value_load(TAB[0:1, ET.stop - 1:ET.stop], min_val=T_MIN // U, max_val=STEPS_MAX)
            eng.wait_ge(pe_tab, 3)
            eng.wait_ge(dve_tab, 1)
            load(0, first_time=True)
            with eng.Fori(0, n) as i:
                load(i + 1)

            for i in range(TT):
                eng.wait_ge(dve_comb, K8 * (i + 1))
                eng.dma_start(out[i * P:(i + 1) * P, :], ACC[:, i, :]).then_inc(out_done, 16)
            eng.wait_ge(out_done, 16 * TT)

        @block.gpsimd
        def _(eng):
            eng.memset(zrow[:, :], 0.0).then_inc(consts, 1)
            eng.memset(identf[:, :], 0.0)
            eng.memset(before[:, :], 1.0)
            eng.memset(ones_b[:, :], 1.0)
            eng.memset(ones_f[:, :], 1.0)
            eng.memset(upto[:, :], 1.0)
            eng.memset(MSUM[:, :], 0.0)
            eng.memset(turn[:, :], 0.0)
            eng.iota(iota_e[:, :], [[1, E]], base=0, channel_multiplier=0, allow_small_or_imprecise_dtypes=True)
            eng.iota(iota_t[:, :], [[1, NTAB]], base=0, channel_multiplier=0,
                     allow_small_or_imprecise_dtypes=True).then_inc(pchain, 1)
            eng.wait_ge(pchain, 1)
            eng.affine_select(out=identf[:, :], in_=identf[:, :], compare_op=ALU.not_equal, fill=1.0, base=0,
                              pattern=[[-1, P]], channel_multiplier=1)
            eng.affine_select(out=before[:, :], in_=before[:, :], compare_op=ALU.is_gt, fill=0.0, base=0,
                              pattern=[[1, P]], channel_multiplier=-1)
            eng.affine_select(out=upto[:, :], in_=upto[:, :], compare_op=ALU.is_ge, fill=0.0, base=0,
                              pattern=[[1, E]], channel_multiplier=-1)
            eng.tensor_scalar(base_e[:, :], iota_e[:, :], float(REGION), None, ALU.mult).then_inc(pchain, 1)
            eng.wait_ge(pchain, 2)
            eng.tensor_scalar(identb[:, :], identf[:, :], 1.0, None, ALU.mult).then_inc(consts, 1)
            for j in range(3):
                eng.memset(AUGT[j][:, :, NT * DK:AUG], 1.0)
            eng.memset(KN[:, :, :], 0.0)
            eng.memset(VAv[:, :, :, DK:2 * DK], 1.0).then_inc(consts, 1)

            eng.wait_ge(dve_kn, KC + 1)
            eng.partition_all_reduce(knall[:, :], kmax[:, :], P, RMAX).then_inc(pool_kmax, 1)
            def second_split(t):
                eng.wait_ge(act_qh, t + 1)
                if t >= 2:
                    eng.wait_ge(act_qm, t - 1)
                    eng.wait_ge(pool_ql, t - 1)
                eng.tensor_tensor(R1[t % 2], QS[t % 2], AUGT[t % 3][:, :, 0:DK], ALU.subtract).then_inc(pool_r1, 1)

            def third_split(t):
                eng.wait_ge(act_qm, t + 1)
                eng.tensor_tensor(AUGT[t % 3][:, :, 5 * DK:6 * DK], R1[t % 2].rearrange("p (h d) -> p h d", h=NH),
                                  AUGT[t % 3][:, :, 3 * DK:4 * DK], ALU.subtract).then_inc(pool_ql, 1)

            second_split(0)
            for t in range(1, TT):
                second_split(t)
                third_split(t - 1)
            third_split(TT - 1)
            eng.wait_ge(dve_top, 1)
            eng.partition_all_reduce(shmax[:, 1:2], shmax[:, 0:1], P, RMAX).then_inc(pool_top, 1)

            def rows(i):
                eng.wait_ge(dve_h2, i + 1)
                if i >= 4:
                    eng.wait_ge(scattered[i % 4], 16 * K8 * (i // 4))
                eng.tensor_scalar(XR[i % 4][:, 0:D], H2, 1.0, None, ALU.mult).then_inc(pool_xr, 1)
                eng.wait_ge(pool_xr, 2 * i + 1)
                eng.tensor_tensor(XR[i % 4][:, D:2 * D], H2, XR[i % 4][:, 0:D], ALU.subtract).then_inc(pool_xr, 1)

            def scatter(i):
                eng.wait_ge(pool_xr, 2 * i + 2)
                eng.wait_ge(dve_idx, i + 1)
                for k in range(K8):
                    eng.indirect_dma_start(out=dispatch, out_offset=bass.IndirectOffsetOnAxis(ap=IDX[:, i, k:k + 1], axis=0),
                                           in_=XR[i % 4], in_offset=None).then_inc(scattered[i % 4], 16)

            for i in range(TT):
                if i < TT - TB:
                    rows(i)
                    scatter(i)
                else:
                    rows(i)
            def load_w(e, st):
                eng.dma_start(STG[st], w_in[ds(e, 1), :, :].rearrange("o p n -> p (o n)")).then_inc(w_loaded[st], 16)

            def first_part(st, par, hi):
                eng.dma_start(hi, STG[st]).then_inc(w_first[par], 16)

            def second_part(st, hi, lo):
                eng.tensor_tensor(lo, STG[st], hi, ALU.subtract).then_inc(w_split, 1)

            eng.wait_ge(pe_qk, 2 * NB * NG * KC)
            for s in range(2):
                load_w(E + s, s)
            for i in range(TT - TB, TT):
                scatter(i)
            eng.wait_ge(pe_pv, NB * NG * KC)
            for s in range(2):
                load_w(s, 2 + s)
            for s in range(2):
                eng.wait_ge(w_loaded[s], 16)
                first_part(s, s, SW[s][:, 0:WALL])
            for s in range(2):
                eng.wait_ge(w_first[s], 16)
                second_part(s, SW[s][:, 0:WALL], SW[s][:, WALL:2 * WALL])
                eng.wait_ge(w_split, s + 1)
                load_w(2 + s, s)
            eng.wait_ge(dve_tab, 1)

            def slot(j):
                return KT[:, j * WSPLIT:j * WSPLIT + WALL], KT[:, j * WSPLIT + WALL:(j + 1) * WSPLIT]

            def expert_first(i, j):
                w = eng.value_load(TAB[0:1, ds(i * NSLOT + (WAITC.start + j), 1)], min_val=1, max_val=T_MAX + 1)
                eng.wait_ge(w_loaded[(j + 2) % NSTG], i * (16 * NSLOT // NSTG) + 16 * ((j + 2) // NSTG + 1))
                eng.wait_ge(tiles_done, w)
                eng.tensor_tensor(turn[:, j + 1:j + 2], turn[:, 0:1], turn[:, 0:1], ALU.add)
                first_part((j + 2) % NSTG, j % 2, slot(j)[0])

            def expert_second(i, j, more):
                eng.wait_ge(w_first[j % 2], i * (16 * NSLOT // 2) + 16 * (j // 2 + 2))
                second_part((j + 2) % NSTG, *slot(j))
                if more:
                    eng.wait_ge(w_split, i * NSLOT + (N_SPLIT0 + j + 1))
                    load_w(i * NSLOT + (j + NSTG), (j + 2) % NSTG)

            expert_first(0, 0)
            with eng.Fori(0, E // NSLOT - 1) as i:
                for j in range(NSLOT):
                    if j < NSLOT - 1:
                        expert_first(i, j + 1)
                    else:
                        expert_first(i + 1, 0)
                    expert_second(i, j, True)
            for j in range(NSLOT):
                if j < NSLOT - 1:
                    expert_first(E // NSLOT - 1, j + 1)
                expert_second(E // NSLOT - 1, j, j < NSLOT - NSTG)

            eng.wait_ge(dve_idx2, TT)
            eng.wait_ge(rows_done, 1)
            for i in range(TT):
                for k in range(K8):
                    if i >= 1:
                        eng.wait_ge(dve_comb, K8 * (i - 1) + k + 1)
                    eng.indirect_dma_start(out=RING[:, k, :], out_offset=None, in_=expert_out,
                                           in_offset=bass.IndirectOffsetOnAxis(ap=IDX2[:, i, k:k + 1], axis=0)).then_inc(gathered[k], 16)

        @block.scalar
        def _(eng):
            eng.wait_ge(small_loaded, 64)
            eng.activation(tg[:, :], gates[:, :], ACT.Tanh).then_inc(gates_done, 1)

            def heads3(t, lo, hi, step=1):
                return t.rearrange("p h (n d) -> p h n d", d=DK)[:, :, lo:hi:step, :]

            def key_first(c):
                r, kv = KR[c], BANKS[c % 2]
                eng.wait_ge(pe_kv, c + 1)
                if c >= 3:
                    eng.wait_ge(pe_kt, 2 * (c - 2))
                src = kv[0:r, 0:D].rearrange("p (h o d) -> p h o d", h=NH, o=1).broadcast_to((r, NH, 3, DK))
                eng.activation(heads3(AUGT[c % 3][0:r, :, 0:NT * DK], 1, NT, 2), src, ACT.Copy).then_inc(act_kh, 1)
                if c >= 1:
                    eng.wait_ge(dve_kn, c)
                eng.activation(SQ[0:r, :], kv[0:r, 0:D], ACT.Square).then_inc(act_v, 1)
                eng.activation(VAv[0:r, c, :, 0:DK], kv[0:r, D:2 * D].rearrange("p (h d) -> p h d", h=NH),
                               ACT.Copy).then_inc(act_v, 1)

            def key_second(c):
                r = KR[c]
                eng.wait_ge(dve_r1, c + 1)
                src = R1[c % 2][0:r, :].rearrange("p (h o d) -> p h o d", h=NH, o=1).broadcast_to((r, NH, 2, DK))
                eng.activation(heads3(AUGT[c % 3][0:r, :, 0:NT * DK], 2, 5, 2), src, ACT.Copy).then_inc(act_km, 1)

            eng.wait_ge(consts, 3)
            key_first(0)
            for c in range(1, KC):
                key_first(c)
                key_second(c - 1)
            key_second(KC - 1)

            eng.wait_ge(dve_ka, KC)

            def query_first(t):
                qa = AUGT[t % 3][:, :, 0:NT * DK]
                qs = QS[t % 2]
                eng.wait_ge(pe_q, t + 1)
                if t >= 2:
                    eng.wait_ge(pool_r1, t - 1)
                    eng.wait_ge(dve_qn, t - 1)
                eng.activation(qs, PVB[1][:, 0:D], ACT.Copy, scale=1.0 / DK ** 0.5).then_inc(act_qs, 1)
                eng.wait_ge(act_qs, t + 1)
                if t == 0:
                    eng.wait_ge(pe_kt, 2 * KC)
                if t >= 3:
                    eng.wait_ge(pe_qt, 2 * (t - 2))
                src = qs.rearrange("p (h o d) -> p h o d", h=NH, o=1).broadcast_to((P, NH, 3, DK))
                eng.activation(heads3(qa, 0, 3), src, ACT.Copy).then_inc(act_qh, 1)
                if t >= 1:
                    eng.wait_ge(dve_qn, t)
                eng.activation(SQ, qs, ACT.Square).then_inc(act_v, 1)

            def query_second(t):
                eng.wait_ge(pool_r1, t + 1)
                src = R1[t % 2].rearrange("p (h o d) -> p h o d", h=NH, o=1).broadcast_to((P, NH, 2, DK))
                eng.activation(heads3(AUGT[t % 3][:, :, 0:NT * DK], 3, 5), src, ACT.Copy).then_inc(act_qm, 1)

            query_first(0)
            for t in range(1, TT):
                query_first(t)
                query_second(t - 1)
            query_second(TT - 1)

            def sigmoid_exp(i):
                eng.wait_ge(pe_lg, i + 1)
                if i >= 1:
                    eng.wait_ge(dve_mk, i)
                eng.activation(EX[:, :], M1[:, 0:E], ACT.Exp, scale=-1.0).then_inc(act_sig, 1)

            for n in range(NB * NG * KC):
                b, c = n // (NG * KC), n % KC
                r = KR[c]
                for p in range(2):
                    eng.wait_ge(pe_qk, 2 * n + p + 1)
                    if n >= 3:
                        eng.wait_ge(pe_pv, n - 2)
                    eng.activation(PRv[0:r, n % 3, 2 * p:2 * p + 2, :],
                                   SP4[0:r, 1024 * p:1024 * p + 1024].rearrange("p (h q) -> p h q", h=2),
                                   ACT.Exp).then_inc(act_exp, 1)
                m = n % (NG * KC)
                if b >= 1 and m % 8 == 2 and 10 <= m < 10 + 8 * TB:
                    sigmoid_exp((b - 1) * TB + (m - 10) // 8)
            for i in range(TT - TB, TT):
                sigmoid_exp(i)

            def sh_silu(cnt_gu, s):
                eng.wait_ge(sh_gu, cnt_gu)
                eng.activation(SIL[s], GUP[s][:, 0:IW], ACT.Silu).then_inc(sh_sil, 1)

            def sh_evac(cnt_t, s):
                eng.wait_ge(sh_t, cnt_t)
                eng.activation(HT[s][0:I2, :], HTP[s][0:I2, :], ACT.Copy).then_inc(sh_te, 1)

            for i in range(TT):
                for s in range(2):
                    if i >= 1:
                        eng.wait_ge(sh_h, 2 * (i - 1) + s + 1)
                    sh_silu(2 * i + s + 1, s)
                if i >= 1:
                    if i >= 2:
                        eng.wait_ge(sh_y, i - 1)
                    for s in range(2):
                        sh_evac(2 * (i - 1) + s + 1, s)
            eng.wait_ge(sh_y, TT - 1)
            for s in range(2):
                sh_evac(2 * (TT - 1) + s + 1, s)

            def silu(t, j):
                eng.wait_ge(e_gu, t + 1)
                eng.activation(SIL[j], GUP[j][:, 0:IW], ACT.Silu).then_inc(e_sil, 1)

            def ht_evac(t, j):
                eng.wait_ge(e_t2, t + 1)
                eng.activation(HT[j][0:I2, :], HTP[j][0:I2, :], ACT.Copy).then_inc(e_te, 1)

            def y_out(t, j, first=False):
                eng.wait_ge(tiles_done, t + 2)
                if not first:
                    eng.wait_ge(y_stored[j], t * 8 - 8 * j)
                eng.activation(YB[j], YP[j], ACT.Copy).then_inc(e_ye, 1)
                eng.wait_ge(e_ye, t + 1)
                eng.dma_start(expert_out[ds(t * P, P), :], YB[j]).then_inc(y_stored[j], 16)

            eng.wait_ge(dve_tab, 1)
            eng.wait_ge(sh_y, TT)
            silu(0, 0)
            silu(1, 1)
            ht_evac(0, 0)
            n = eng.value_load(TAB[0:1, ET.stop - 1:ET.stop], min_val=T_MIN // U, max_val=STEPS_MAX)
            for t in range(U):
                eng.wait_ge(e_h, t + 1)
                silu(2 + t, t % 2)
                eng.wait_ge(tiles_done, t + 1)
                ht_evac(1 + t, (1 + t) % 2)
                y_out(t, t % 2, first=t < 2)
            with eng.Fori(1, n) as i:
                for j in range(U):
                    eng.wait_ge(e_h, i * U + (j + 1))
                    silu(i * U + (2 + j), j % 2)
                    eng.wait_ge(tiles_done, i * U + (j + 1))
                    ht_evac(i * U + (1 + j), (1 + j) % 2)
                    y_out(i * U + j, j % 2)
            for j in range(2):
                eng.wait_ge(y_stored[j], n * (16 * U // 2))
            eng.activation(tg[:, 0:1], tg[:, 0:1], ACT.Copy).then_inc(rows_done, 1)

        @block.tensor
        def _(eng):
            def mm(o, l, r, start, stop, **kw):
                return eng.matmul(o, l, r, start=start, stop=stop, **kw)

            def kv_rows(c):
                r = KR[c]
                if c >= 2:
                    eng.wait_ge(act_v, 2 * (c - 1))
                    eng.wait_ge(dve_r1, c - 1)
                for k in range(2):
                    i = mm(BANKS[c % 2][0:r, :], ctxT[:, k, c * P:c * P + r], wkv[:, k, :], k == 0, k == 1)
                i.then_inc(pe_kv, 1)

            def kv_transposes(c):
                r = KR[c]
                eng.wait_ge(dve_ka, c + 1)
                for g in range(2):
                    n = 2 * c + g
                    if n >= 2:
                        eng.wait_ge(dve_kt, n - 1)
                    bank = BANKS[2 + n % 2].bitcast(bf16).rearrange("p (h q) -> p h q", h=8)
                    for h in range(8):
                        i = eng.transpose(bank[0:AUG, h, 0:r], AUGT[c % 3][0:r, 8 * g + h, :], identb[0:r, 0:r])
                    i.then_inc(pe_kt, 1)

            eng.wait_ge(consts, 3)
            eng.wait_ge(ctx_in, 16)
            eng.wait_ge(wkv_in_s, 16)
            kv_rows(0)
            kv_rows(1)
            for c in range(KC):
                if c + 2 < KC:
                    kv_rows(c + 2)
                kv_transposes(c)

            def q_transposes(t):
                eng.wait_ge(dve_m, t + 1)
                eng.wait_ge(pool_ql, t + 1)
                for g in range(2):
                    n = 2 * t + g
                    eng.wait_ge(dve_kt, 2 * KC)
                    if n >= 2:
                        eng.wait_ge(dve_qt, n - 1)
                    bank = BANKS[2 + n % 2].bitcast(bf16).rearrange("p (h q) -> p h q", h=8)
                    for h in range(8):
                        i = eng.transpose(bank[0:AUG, h, :], AUGT[t % 3][:, 8 * g + h, :], identb[:, :])
                    i.then_inc(pe_qt, 1)

            def q_rows(t):
                eng.wait_ge(dve_xn, t + 1)
                if t >= 1:
                    eng.wait_ge(dve_xt, t)
                for k in range(2):
                    i = eng.transpose(PVB[0][:, P * k:P * (k + 1)], XN[:, P * k:P * (k + 1)], identf[:, :])
                i.then_inc(pe_xt, 1)
                eng.wait_ge(dve_xt, t + 1)
                if t >= 1:
                    eng.wait_ge(act_qs, t)
                for k in range(2):
                    i = mm(PVB[1][:, 0:D], XNT[:, P * k:P * (k + 1)], wq[:, k, :], k == 0, k == 1)
                i.then_inc(pe_q, 1)

            eng.wait_ge(wq_loaded, 16)
            q_rows(0)
            q_rows(1)
            for t in range(TT):
                if t + 2 < TT:
                    q_rows(t + 2)
                q_transposes(t)

            eng.wait_ge(dve_flag, 1)
            general = eng.value_load(flag[0:1, 0:1], min_val=0, max_val=1)
            with eng.If(general > 0):
                eng.wait_ge(dve_qt, 2 * TT)
                with eng.Fori(0, NB) as b:
                    for j in range(TB):
                        for h in range(NH):
                            if not (j == 0 and h == 0):
                                eng.wait_ge(gen_m, b * (TB * NH) + (j * NH + h))
                            for c in range(4):
                                w = min(512, KV - 512 * c)
                                i = mm(SP4[:, 512 * c:512 * c + w],
                                       QT[0:NT * DK, ds(b * (NH * QB) + (h * QB + j * P), P)],
                                       KTv[0:NT * DK, h, 512 * c:512 * c + w], True, True)
                            i.then_inc(gen_s, 1)
                        eng.wait_ge(gen_split, b * TB + (j + 1))
                        for h in range(NH):
                            bank = BANKS[6 + h // 8].bitcast(bf16)
                            i = eng.transpose(bank[NT * DK:AUG, P * (h % 8):P * (h % 8 + 1)], MHL[:, h, :], identb[:, :])
                        i.then_inc(gen_t, 1)
                        eng.wait_ge(gen_qt, b * TB + (j + 1))
                        eng.wait_ge(gen_m, b * (TB * NH) + (j + 1) * NH)
            eng.nop()

            def scores(n, p):
                b, g, c = n // (NG * KC), n // KC % NG, n % KC
                r = KR[c]
                if n >= 1:
                    eng.wait_ge(act_exp, 2 * (n - 1) + p + 1)
                for u in range(2):
                    h = 4 * g + 2 * p + u
                    i = mm(SP4[0:r, 512 * (2 * p + u):512 * (2 * p + u + 1)], KTv[0:AUG, h, c * P:c * P + r],
                           QTv[0:AUG, b, h, :], True, True)
                i.then_inc(pe_qk, 1)

            def attend(n):
                b, g, c = n // (NG * KC), n // KC % NG, n % KC
                q, r = n // KC, KR[c]
                eng.wait_ge(act_exp, 2 * n + 2)
                if c == 0 and q >= 2:
                    eng.wait_ge(dve_pv, q - 1)
                for u in range(4):
                    i = mm(PVB[q % 2][32 * u:32 * u + 32, :], VAv[0:r, c, 4 * g + u, :], PRv[0:r, n % 3, u, :],
                           c == 0, c == KC - 1)
                i.then_inc(pe_pv, 1)

            def out_proj(i):
                b, j = i // TB, i % TB
                eng.wait_ge(dve_attn, NG * (b + 1))
                if i >= 1:
                    eng.wait_ge(dve_h2t, i)
                for g in range(NG):
                    x = mm(M0[:, 0:D], attnT(b, g)[:, P * j:P * (j + 1)], wo[:, g, :], g == 0, g == NG - 1)
                x.then_inc(pe_op, 1)

            def h2_transpose(i):
                eng.wait_ge(dve_h2, i + 1)
                for k in range(2):
                    x = eng.transpose(M0[:, D + P * k:D + P * (k + 1)], H2[:, P * k:P * (k + 1)], identf[:, :])
                x.then_inc(pe_h2t, 1)

            def router(i):
                eng.wait_ge(dve_h2t, i + 1)
                if i >= 1:
                    eng.wait_ge(dve_idx, i)
                for k in range(2):
                    x = mm(M1[:, 0:E], H2T[:, P * k:P * (k + 1)], gw[:, k, :], k == 0, k == 1)
                x.then_inc(pe_lg, 1)

            def ranks(i):
                eng.wait_ge(dve_mk, i + 1)
                if i >= 1:
                    eng.wait_ge(dve_msum, i)
                mm(M1[:, E:2 * E], before[:, :], MK[:, :], True, False)
                mm(M1[:, E:2 * E], ones_b[:, :], MSUM[:, :], False, True).then_inc(pe_rank, 1)

            eng.wait_ge(dve_qt, 2 * TT)
            scores(0, 0)
            scores(0, 1)
            STEPS = NB * NG * KC
            for n in range(STEPS):
                if n + 1 < STEPS:
                    scores(n + 1, 0)
                if n >= 1:
                    attend(n - 1)
                if n + 1 < STEPS:
                    scores(n + 1, 1)
                b, m = n // (NG * KC), n % (NG * KC)
                if b >= 1:
                    for j in range(TB):
                        i = (b - 1) * TB + j
                        if m == 3 + 8 * j:
                            out_proj(i)
                        if m == 7 + 8 * j:
                            h2_transpose(i)
                        if m == 9 + 8 * j:
                            router(i)
                        if m == 15 + 8 * j:
                            ranks(i)
            attend(STEPS - 1)
            for i in range(TT - TB, TT):
                out_proj(i)
                h2_transpose(i)
                router(i)
                ranks(i)

            eng.wait_ge(dve_msum, TT)
            mm(M0[0:E, 0:1], MSUM[:, :], ones_b[:, 0:1], True, True).then_inc(pe_tab, 1)
            eng.wait_ge(chain_tab, 1)
            mm(M0[0:E, 8:9], upto[:, :], ctf[:, :], True, True)
            mm(M0[:, 384:384 + E], CTB, before[0:E, 0:E], True, True)
            mm(M0[0:1, 64:64 + E], cnt[:, :], identf[0:E, 0:E], True, True).then_inc(pe_tab, 1)
            eng.wait_ge(chain_tab, 2)
            CMP = A8[0:E, 0:NTAB]
            mm(M1[0:1, 0:NTAB], ones_f[:, :], CMP, True, True)
            mm(M1[0:1, 256:256 + NTAB], ctf[:, :], CMP, True, True)
            mm(M0[0:1, 256:256 + E], cum[:, :], identf[0:E, 0:E], True, True).then_inc(pe_tab, 1)

            def gate_up(o, xs, w, wlo):
                mm(o, xs(0), w(0), True, False)
                mm(o, xs(0), wlo(0), False, False)
                mm(o, xs(1), w(1), False, False)
                mm(o, xs(1), wlo(1), False, False)
                mm(o, xs(2), w(0), False, False)
                return mm(o, xs(3), w(1), False, True)

            def down(o, ht, w, wlo, first=True, last=True):
                mm(o, ht(0), w(0), first, False)
                mm(o, ht(0), wlo(0), False, False)
                mm(o, ht(1), w(1), False, False)
                mm(o, ht(1), wlo(1), False, False)
                mm(o, ht(2), w(0), False, False)
                return mm(o, ht(3), w(1), False, last)

            def h_transposes(j):
                for q in range(4):
                    x = eng.transpose(HTP[j][0:I2, P * q:P * (q + 1)],
                                      HHL[j][:, q // 2, I2 * (q % 2):I2 * (q % 2 + 1)], identb[:, :])
                return x

            def htv(j):
                return lambda q: HT[j][0:I2, P * q:P * (q + 1)]

            eng.wait_ge(w_split, N_SPLIT0)
            eng.wait_ge(dve_tab, 1)
            eng.wait_ge(dve_hl, TT)

            def sh_down(i):
                for s in range(2):
                    eng.wait_ge(sh_h, 2 * i + s + 1)
                    if i >= 1:
                        eng.wait_ge(sh_te, 2 * (i - 1) + s + 1)
                    h_transposes(s).then_inc(sh_t, 1)
                if i >= 1:
                    eng.wait_ge(sh_ye, i)
                for s in range(2):
                    eng.wait_ge(sh_te, 2 * i + s + 1)
                    w = SW[s]
                    x = down(YP[0], htv(s), lambda k: w[0:I2, DHI + D * k:DHI + D * (k + 1)],
                             lambda k: w[0:I2, DLO + D * k:DLO + D * (k + 1)], s == 0, s == 1)
                x.then_inc(sh_y, 1)

            for i in range(TT):
                for s in range(2):
                    if i >= 1:
                        eng.wait_ge(sh_h, 2 * (i - 1) + s + 1)
                    w = SW[s]
                    h2 = h2T_cols(i)
                    gate_up(GUP[s][:, 0:2 * IW], lambda q: h2[:, q, :], lambda k: w[:, 2 * IW * k:2 * IW * (k + 1)],
                            lambda k: w[:, WALL + 2 * IW * k:WALL + 2 * IW * (k + 1)]).then_inc(sh_gu, 1)
                if i >= 1:
                    sh_down(i - 1)
            sh_down(TT - 1)
            eng.wait_ge(sh_ye, TT)
            eng.transpose(HTP[0][0:I2, 0:P], HHL[0][:, 0, 0:I2], identb[:, :]).then_inc(tiles_done, 1)

            def t1(j, cnt_x):
                eng.wait_ge(xg_loaded[j], cnt_x)
                for q in range(4):
                    x = eng.transpose(XTP[j % 2][:, P * q:P * (q + 1)], XG[j][:, P * q:P * (q + 1)], identb[:, :])
                x.then_inc(e_t1, 1)

            def gu(t, j, e):
                w = (e % NSLOT) * WSPLIT
                eng.wait_ge(e_xt, t + 1)
                eng.wait_ge(w_split, e + (N_SPLIT0 + 1))
                x = XT[j]
                gate_up(GUP[j][:, 0:2 * IW], lambda q: x[:, P * q:P * (q + 1)], lambda k: wslot(w + 2 * IW * k, 2 * IW),
                        lambda k: wslot(w + (WALL + 2 * IW * k), 2 * IW)).then_inc(e_gu, 1)

            def t2(t, j):
                eng.wait_ge(e_h, t + 1)
                h_transposes(j).then_inc(e_t2, 1)

            def dn(t, j, e):
                w = (e % NSLOT) * WSPLIT
                eng.wait_ge(e_te, t + 1)
                down(YP[j], htv(j), lambda k: KT[0:I2, ds(w + (DHI + D * k), D)],
                     lambda k: KT[0:I2, ds(w + (DLO + D * k), D)]).then_inc(tiles_done, 1)

            n = eng.value_load(TAB[0:1, ET.stop - 1:ET.stop], min_val=T_MIN // U, max_val=STEPS_MAX)
            def expert_of(t):
                return eng.value_load(TAB[0:1, ds(t + ET.start, 1)], min_val=0, max_val=E - 1)

            def expert_at(words, k):
                return words[k // 4] // 64 ** (k % 4) % 64

            e0 = [expert_of(t) for t in range(3)]
            t1(0, 16)
            t1(1, 16)
            gu(0, 0, e0[0])
            eng.wait_ge(e_xt, 1)
            t1(2, 16)
            gu(1, 1, e0[1])
            t2(0, 0)
            eng.wait_ge(e_xt, 2)
            t1(3, 16)
            eng.wait_ge(e_h, 1)
            gu(2, 0, e0[2])
            with eng.Fori(0, n * U, U) as m:
                four = registers(eng, PACK[0:1, ds(m, 2)], 64 ** 4)
                for j in range(U):
                    t2(m + (1 + j), (1 + j) % 2)
                    dn(m + j, j % 2, expert_at(four, j))
                    t1(j, m * 4 + 32)
                    gu(m + (3 + j), (3 + j) % 2, expert_at(four, 3 + j))

        @block.vector
        def _(eng):
            links = [0]

            def link(x):
                links[0] += 1
                x.then_inc(chain, 1)
                eng.wait_ge(chain, links[0])

            def rsqrt(y, v, t, iv, n):
                link(eng.tensor_scalar(iv, v.bitcast(i32), 1, None, ALU.logical_shift_right))
                link(eng.tensor_scalar(y.bitcast(i32), iv, -1.0, float(0x5F3759DF), ALU.mult, ALU.add))
                for _ in range(4):
                    link(eng.tensor_tensor(t, y, y, ALU.mult))
                    link(eng.tensor_tensor(t, t, v, ALU.mult))
                    link(eng.tensor_scalar(t, t, -0.5, 1.5, ALU.mult, ALU.add))
                    link(eng.tensor_tensor(y, y, t, ALU.mult))

            eng.wait_ge(x_loaded, 16)
            for t in range(TT):
                link(eng.bn_stats(stats[:, :], ACC[:, t, :]))
                link(eng.bn_aggr(mv[:, t, :], stats[:, :]))
            link(eng.tensor_scalar(ve[:, :], mv[:, :, 1], EPS, None, ALU.add))
            rsqrt(rs[:, :], ve[:, :], rt[:, :], ri[:, :], TT)

            def kt_evac(c):
                r = KR[c]
                for g in range(2):
                    n = 2 * c + g
                    eng.wait_ge(pe_kt, n + 1)
                    bank = BANKS[2 + n % 2].bitcast(bf16).rearrange("p (h q) -> p h q", h=8)
                    eng.tensor_copy(KTv[0:AUG, 8 * g:8 * g + 8, c * P:c * P + r], bank[0:AUG, :, 0:r]).then_inc(dve_kt, 1)

            def key_residual(c):
                r = KR[c]
                ka = AUGT[c % 3][0:r]
                eng.wait_ge(act_v, 2 * c + 2)
                if c >= 2:
                    eng.wait_ge(dve_ka, c - 1)
                eng.tensor_tensor(R1[c % 2][0:r, :].rearrange("p (h d) -> p h d", h=NH),
                                  BANKS[c % 2][0:r, 0:D].rearrange("p (h d) -> p h d", h=NH),
                                  ka[:, :, DK:2 * DK], ALU.subtract).then_inc(dve_r1, 1)
                eng.tensor_reduce(KN[0:r, c, :], SQ[0:r, :].rearrange("p (h d) -> p h d", h=NH), AX.X,
                                  ALU.add).then_inc(dve_kn, 1)

            def key_third(c):
                r = KR[c]
                ka = AUGT[c % 3][0:r]
                eng.wait_ge(act_km, c + 1)
                eng.wait_ge(dve_r1, c + 1)
                eng.tensor_tensor(ka[:, :, 0:DK], R1[c % 2][0:r, :].rearrange("p (h d) -> p h d", h=NH),
                                  ka[:, :, 2 * DK:3 * DK], ALU.subtract).then_inc(dve_ka, 1)

            for c in range(KC):
                key_residual(c)
                if c >= 1:
                    key_third(c - 1)
                if c >= 2:
                    kt_evac(c - 2)
            key_third(KC - 1)
            eng.wait_ge(dve_kn, KC)
            eng.tensor_reduce(kmax[:, :], KN[:, :, :].rearrange("p c h -> p h c"), AX.X, ALU.max).then_inc(dve_kn, 1)
            kt_evac(KC - 2)
            kt_evac(KC - 1)

            def qt_evac(t):
                for g in range(2):
                    n = 2 * t + g
                    eng.wait_ge(pe_qt, n + 1)
                    bank = BANKS[2 + n % 2].bitcast(bf16).rearrange("p (h q) -> p h q", h=8)
                    eng.tensor_copy(QTv[0:AUG, t // TB, 8 * g:8 * g + 8, P * (t % TB):P * (t % TB + 1)],
                                    bank[0:AUG, :, :]).then_inc(dve_qt, 1)

            def xn(t):
                if t >= 1:
                    eng.wait_ge(pe_xt, t)
                eng.tensor_scalar(XN, ACC[:, t, :], mv[:, t, 0:1], rs[:, t:t + 1], ALU.subtract,
                                  ALU.mult).then_inc(dve_xn, 1)

            def xnt(t):
                eng.wait_ge(pe_xt, t + 1)
                if t >= 1:
                    eng.wait_ge(pe_q, t)
                eng.tensor_copy(XNT, PVB[0][:, 0:D]).then_inc(dve_xt, 1)

            xn(0)
            xnt(0)
            xn(1)
            xnt(1)
            xn(2)
            eng.wait_ge(pool_kmax, 1)
            link(eng.tensor_scalar(knall[:, :], knall[:, :], -0.5 / DK ** 0.5, None, ALU.mult))
            for t in range(TT):
                eng.wait_ge(act_v, 2 * KC + t + 1)
                eng.tensor_reduce(qn[:, :], SQ.rearrange("p (h d) -> p h d", h=NH), AX.X, ALU.add).then_inc(dve_qn, 1)
                eng.wait_ge(dve_qn, t + 1)
                link(eng.scalar_tensor_tensor(out=NM[:, t, :], in0=qn[:, :], scalar=-0.5 * DK ** 0.5, in1=knall[:, :],
                                              op0=ALU.mult, op1=ALU.add))
                if t == 0:
                    eng.wait_ge(pe_kt, 2 * KC)
                if t >= 3:
                    eng.wait_ge(pe_qt, 2 * (t - 2))
                qa = AUGT[t % 3]
                link(eng.tensor_copy(qa[:, :, NT * DK], NM[:, t, :]))
                eng.tensor_tensor(qa[:, :, NT * DK + 1], NM[:, t, :], qa[:, :, NT * DK], ALU.subtract).then_inc(dve_m, 1)
                if t + 2 < TT:
                    xnt(t + 2)
                if t + 3 < TT:
                    xn(t + 3)
                if t >= 1:
                    qt_evac(t - 1)
            qt_evac(TT - 1)
            link(eng.tensor_reduce(shmax[:, 1:2], NM[:, :, :].rearrange("p t h -> p (t h)"), AX.X, ALU.min))
            eng.tensor_scalar(shmax[:, 0:1], shmax[:, 1:2], -1.0, None, ALU.mult).then_inc(dve_top, 1)
            eng.wait_ge(pool_top, 1)
            eng.tensor_scalar(flag[:, :], shmax[:, 1:2], SHIFT_MAX, None, ALU.is_gt).then_inc(dve_flag, 1)
            eng.wait_ge(dve_flag, 1)
            general = eng.value_load(flag[0:1, 0:1], min_val=0, max_val=1)
            with eng.If(general > 0):
                with eng.Fori(0, NB) as b:
                    for j in range(TB):
                        for h in range(NH):
                            eng.wait_ge(gen_s, b * (TB * NH) + (j * NH + h + 1))
                            eng.tensor_reduce(MROW[:, h:h + 1], SP4[:, 0:KV], AX.X, ALU.max).then_inc(gen_m, 1)
                        eng.wait_ge(gen_m, b * (TB * NH) + (j + 1) * NH)
                        eng.tensor_scalar(MROW, MROW, -1.0, None, ALU.mult).then_inc(gen_chain, 1)
                        eng.wait_ge(gen_chain, b * (2 * TB) + (2 * j + 1))
                        eng.tensor_copy(MHL[:, :, 0], MROW).then_inc(gen_chain, 1)
                        eng.wait_ge(gen_chain, b * (2 * TB) + (2 * j + 2))
                        eng.tensor_tensor(MHL[:, :, 1], MROW, MHL[:, :, 0], ALU.subtract).then_inc(gen_split, 1)
                        eng.wait_ge(gen_t, b * TB + (j + 1))
                        for g in range(2):
                            bank = BANKS[6 + g].bitcast(bf16)
                            x = eng.tensor_copy(QT[NT * DK:AUG, ds(b * (NH * QB) + 8 * g * QB, 8 * QB)]
                                                .rearrange("p (h q) -> p h q", h=8)[:, :, P * j:P * (j + 1)],
                                                bank[NT * DK:AUG, :].rearrange("p (h q) -> p h q", h=8))
                        x.then_inc(gen_qt, 1)
            eng.nop()

            def normalise(q):
                b, g = q // NG, q % NG
                eng.wait_ge(pe_pv, KC * (q + 1))
                eng.wait_ge(dve_attn, q) if q else None
                eng.tensor_copy(OS, PVB[q % 2][:, :]).then_inc(dve_pv, 1)
                eng.wait_ge(dve_pv, q + 1)
                link(eng.stream_shuffle(RS, OS, [DK] * 32))
                link(eng.reciprocal(RS, RS))
                eng.tensor_tensor(attnT(b, g), OS, RS, ALU.mult).then_inc(dve_attn, 1)

            def residual(i):
                eng.wait_ge(pe_op, i + 1)
                link(eng.scalar_tensor_tensor(out=ACC[:, i, :], in0=M0[:, 0:D], scalar=tg[:, 0:1], in1=ACC[:, i, :],
                                              op0=ALU.mult, op1=ALU.add))
                link(eng.bn_stats(stats[:, :], ACC[:, i, :]))
                link(eng.bn_aggr(mv[:, 0, :], stats[:, :]))
                link(eng.tensor_scalar(ve[:, 0:1], mv[:, 0, 1:2], EPS, None, ALU.add))
                rsqrt(rs[:, 0:1], ve[:, 0:1], rt[:, 0:1], ri[:, 0:1], 1)
                if i >= 1:
                    eng.wait_ge(pool_xr, 2 * i)
                    eng.wait_ge(pe_h2t, i)
                eng.tensor_scalar(H2, ACC[:, i, :], mv[:, 0, 0:1], rs[:, 0:1], ALU.subtract, ALU.mult).then_inc(dve_h2, 1)
                eng.wait_ge(dve_h2, i + 1)

            def h2_parts(i):
                eng.wait_ge(pe_h2t, i + 1)
                if i >= 1:
                    eng.wait_ge(pe_lg, i)
                eng.tensor_copy(H2T, M0[:, D:2 * D]).then_inc(dve_h2t, 1)
                eng.wait_ge(dve_h2t, i + 1)
                h2 = h2T_cols(i)
                src = H2T.rearrange("p (c q) -> p c q", c=2)
                link(eng.tensor_copy(h2[:, 0:2, :], src))
                eng.tensor_tensor(h2[:, 2:4, :], src, h2[:, 0:2, :], ALU.subtract).then_inc(dve_hl, 1)
                eng.wait_ge(dve_hl, i + 1)

            A8v = A8.rearrange("p (k e) -> p k e", k=K8)
            PXv = PX.rearrange("p (k e) -> p k e", k=K8)

            def choose(i):
                eng.wait_ge(act_sig, i + 1)
                link(eng.tensor_scalar(CF[:, :], EX[:, :], 1.0, None, ALU.add))
                link(eng.reciprocal(SCO[:, :], CF[:, :]))
                link(eng.tensor_tensor(CF[:, :], SCO[:, :], bias[:, :], ALU.add))
                for g in range(8):
                    x = eng.max(G8[:, 8 * g:8 * g + 8], CF[:, 8 * g:8 * g + 8])
                link(x)
                g8 = G8[:, :].rearrange("p (g k) -> p g k", k=8)
                link(eng.tensor_tensor(GS[:, :], g8[:, :, 0], g8[:, :, 1], ALU.add))
                link(eng.max(T8[:, :], GS[:, :]))
                link(eng.max_index(I8[:, :], T8[:, :], GS[:, :]))
                link(eng.tensor_copy(F8[:, :], I8[:, :]))
                a4 = A8[:, 0:32].rearrange("p (g j) -> p g j", j=4)
                link(eng.tensor_tensor(a4, iota_e[:, 0:8].rearrange("p (g o) -> p g o", o=1).broadcast_to((P, 8, 4)),
                                       F8[:, 0:4].rearrange("p (o j) -> p o j", o=1).broadcast_to((P, 8, 4)), ALU.is_equal))
                link(eng.tensor_reduce(GM[:, :], a4, AX.X, ALU.add))
                cf = CF[:, :].rearrange("p (g k) -> p g k", k=8)
                link(eng.tensor_tensor(cf, cf, GM[:, :].rearrange("p (g o) -> p g o", o=1).broadcast_to((P, 8, 8)), ALU.mult))
                link(eng.tensor_scalar(CF[:, :], CF[:, :], 0.0, None, ALU.add))
                link(eng.max(T8[:, :], CF[:, :]))
                link(eng.max_index(I8[:, :], T8[:, :], CF[:, :]))
                link(eng.tensor_copy(F8[:, :], I8[:, :]))
                link(eng.tensor_copy(CHOSEN[:, i, :], F8[:, :]))
                link(eng.tensor_tensor(A8v, iota_e[:, :].rearrange("p (o e) -> p o e", o=1).broadcast_to((P, K8, E)),
                                       F8[:, :].rearrange("p (k o) -> p k o", o=1).broadcast_to((P, K8, E)), ALU.is_equal))
                if i >= 1:
                    eng.wait_ge(pe_rank, i)
                with nc.allow_low_precision("ones and zeros"):
                    eng.tensor_reduce(MK[:, :], A8v.rearrange("p k e -> p e k"), AX.X, ALU.add).then_inc(dve_mk, 1)
                eng.wait_ge(dve_mk, i + 1)

            def place(i):
                eng.wait_ge(pe_rank, i + 1)
                link(eng.tensor_tensor(POS[:, :], M1[:, E:2 * E], base_e[:, :], ALU.add))
                eng.tensor_tensor(MSUM[:, :], MSUM[:, :], MK[:, :], ALU.add).then_inc(dve_msum, 1)
                eng.wait_ge(dve_msum, i + 1)
                link(eng.tensor_tensor(PXv, A8v, POS[:, :].rearrange("p (o e) -> p o e", o=1).broadcast_to((P, K8, E)), ALU.mult))
                link(eng.tensor_reduce(W8[:, :], PXv, AX.X, ALU.add))
                eng.tensor_copy(IDX[:, i, :], W8[:, :]).then_inc(dve_idx, 1)
                eng.wait_ge(dve_idx, i + 1)
                link(eng.tensor_tensor(PXv, A8v, SCO[:, :].rearrange("p (o e) -> p o e", o=1).broadcast_to((P, K8, E)), ALU.mult))
                link(eng.tensor_reduce(W8[:, :], PXv, AX.X, ALU.add))
                link(eng.tensor_reduce(W1[:, 0:1], W8[:, :], AX.X, ALU.add))
                link(eng.tensor_scalar(W1[:, 0:1], W1[:, 0:1], 1e-20, None, ALU.add))
                link(eng.reciprocal(W1[:, 1:2], W1[:, 0:1]))
                link(eng.tensor_scalar(W8[:, :], W8[:, :], W1[:, 1:2], SCALE_OUT, ALU.mult, ALU.mult))
                link(eng.tensor_scalar(WK[:, i, :], W8[:, :], tg[:, 1:2], None, ALU.mult))

            eng.wait_ge(gates_done, 1)
            eng.wait_ge(pe_qt, 2 * TT)
            eng.wait_ge(pool_ql, TT)
            for b in range(NB):
                i = (b - 1) * TB
                if b >= 1:
                    residual(i)
                    h2_parts(i)
                    choose(i)
                    residual(i + 1)
                normalise(b * NG)
                if b >= 1:
                    place(i)
                    h2_parts(i + 1)
                    choose(i + 1)
                    residual(i + 2)
                    place(i + 1)
                    h2_parts(i + 2)
                    choose(i + 2)
                normalise(b * NG + 1)
                if b >= 1:
                    residual(i + 3)
                    place(i + 2)
                    h2_parts(i + 3)
                    choose(i + 3)
                normalise(b * NG + 2)
                if b >= 1:
                    place(i + 3)
                normalise(b * NG + 3)
            for i in range(TT - TB, TT):
                residual(i)
                h2_parts(i)
                choose(i)
                place(i)

            eng.wait_ge(pe_tab, 1)
            link(eng.tensor_copy(cnt[:, :], M0[0:E, 0:1]))
            link(eng.tensor_scalar(cti[:, :], cnt[:, :], float(P - 1), None, ALU.add))
            link(eng.tensor_scalar(cti[:, :], cti[:, :], 7, None, ALU.logical_shift_right))
            link(eng.tensor_copy(ctf[:, :], cti[:, :]))
            link(eng.tensor_scalar(ctf[:, :], ctf[:, :], 1.0, None, ALU.max))
            eng.tensor_scalar(CTB, ones_b[0:E, :], ctf[:, 0:1], None, ALU.mult).then_inc(chain_tab, 1)
            eng.wait_ge(pe_tab, 2)
            link(eng.tensor_copy(cum[:, :], M0[0:E, 8:9]))
            link(eng.scalar_tensor_tensor(out=DELTA, in0=M0[:, 384:384 + E], scalar=float(P), in1=base_e[:, :],
                                          op0=ALU.mult, op1=ALU.subtract))
            link(eng.tensor_tensor(TAB[0:1, PADR.start:PADR.start + E], M0[0:1, 64:64 + E], base_e[0:1, :], ALU.add))
            eng.tensor_scalar(A8[0:E, 0:NTAB], iota_t[:, :], cum[:, 0:1], None, ALU.is_ge).then_inc(chain_tab, 1)
            eng.wait_ge(pe_tab, 3)
            tf = TABF
            link(eng.tensor_copy(tf[0:1, ET], M1[0:1, 0:NTAB]))
            link(eng.scalar_tensor_tensor(out=tf[0:1, RT], in0=M1[0:1, 256:256 + NTAB], scalar=-1.0, in1=iota_t[0:1, :],
                                          op0=ALU.mult, op1=ALU.add))
            link(eng.tensor_scalar(tf[0:1, WB], tf[0:1, ET], float(REGION), None, ALU.mult))
            link(eng.scalar_tensor_tensor(out=TAB[0:1, RT], in0=tf[0:1, RT], scalar=float(P), in1=tf[0:1, WB],
                                          op0=ALU.mult, op1=ALU.add))
            link(eng.tensor_scalar(TAB[0:1, RT], TAB[0:1, RT], float(E * REGION), None, ALU.min))
            link(eng.tensor_scalar(TAB[0:1, ET], tf[0:1, ET], float(E - 1), None, ALU.min))
            by4 = TAB[0:1, ET].rearrange("o (i k) -> o i k", k=U)
            fours = tf[0:1, RT.start:RT.start + NTAB // U]
            link(eng.scalar_tensor_tensor(out=fours, in0=by4[:, :, 3], scalar=64.0, in1=by4[:, :, 2], op0=ALU.mult, op1=ALU.add))
            link(eng.scalar_tensor_tensor(out=fours, in0=fours, scalar=64.0, in1=by4[:, :, 1], op0=ALU.mult, op1=ALU.add))
            link(eng.scalar_tensor_tensor(out=fours, in0=fours, scalar=64.0, in1=by4[:, :, 0], op0=ALU.mult, op1=ALU.add))
            link(eng.memset(PACK, 0))
            pack = PACK.rearrange("o (i k) -> o i k", k=U)
            eng.tensor_copy(pack[:, :, 0], fours)
            link(eng.tensor_copy(pack[:, 0:NTAB // U - 1, 1], fours[:, 1:]))
            link(eng.tensor_scalar(tf[0:1, 0:1], M1[0:1, 255 + NTAB:256 + NTAB], float(U - 1), None, ALU.add))
            link(eng.tensor_copy(TAB[0:1, ET.stop - 1:ET.stop], tf[0:1, 0:1]))
            link(eng.tensor_scalar(TAB[0:1, ET.stop - 1:ET.stop], TAB[0:1, ET.stop - 1:ET.stop], U.bit_length() - 1, None,
                                   ALU.logical_shift_right))
            link(eng.memset(TAB[0:1, WAITC.start:WAITC.start + NSLOT], 1))
            eng.tensor_scalar(TAB[0:1, WAITC.start + NSLOT:WAITC.start + E], M0[0:1, 256:256 + E - NSLOT], 1.0, None,
                              ALU.add).then_inc(dve_tab, 1)
            eng.wait_ge(dve_tab, 1)

            def hidden(j):
                return eng.tensor_tensor(HF[j], SIL[j], GUP[j][:, IW:2 * IW], ALU.mult)

            def result_rows(i):
                link(eng.tensor_tensor(A8v, iota_e[:, :].rearrange("p (o e) -> p o e", o=1).broadcast_to((P, K8, E)),
                                       CHOSEN[:, i, :].rearrange("p (k o) -> p k o", o=1).broadcast_to((P, K8, E)), ALU.is_equal))
                link(eng.tensor_tensor(PXv, A8v, DELTA.rearrange("p (o e) -> p o e", o=1).broadcast_to((P, K8, E)), ALU.mult))
                link(eng.tensor_reduce(W8[:, :], PXv, AX.X, ALU.add))
                eng.tensor_tensor(IDX2[:, i, :], IDX[:, i, :], W8[:, :], ALU.add).then_inc(dve_idx2, 1)
                eng.wait_ge(dve_idx2, i + 1)

            for i in range(TT):
                result_rows(i)
                for s in range(2):
                    eng.wait_ge(sh_sil, 2 * i + s + 1)
                    link(hidden(s))
                    if i >= 1:
                        eng.wait_ge(sh_t, 2 * (i - 1) + s + 1)
                    link(eng.tensor_copy(HHL[s][:, 0, :], HF[s]))
                    eng.tensor_tensor(HHL[s][:, 1, :], HF[s], HHL[s][:, 0, :], ALU.subtract).then_inc(sh_h, 1)
                if i >= 1:
                    eng.wait_ge(sh_y, i)
                    eng.scalar_tensor_tensor(out=ACC[:, i - 1, :], in0=YP[0], scalar=tg[:, 1:2], in1=ACC[:, i - 1, :],
                                             op0=ALU.mult, op1=ALU.add).then_inc(sh_ye, 1)
            eng.wait_ge(sh_y, TT)
            eng.scalar_tensor_tensor(out=ACC[:, TT - 1, :], in0=YP[0], scalar=tg[:, 1:2], in1=ACC[:, TT - 1, :],
                                     op0=ALU.mult, op1=ALU.add).then_inc(sh_ye, 1)

            def xt_evac(t, j):
                eng.wait_ge(e_t1, t + 1)
                eng.tensor_copy(XT[j], XTP[j]).then_inc(e_xt, 1)

            def h_split(t, j, link_to):
                eng.wait_ge(e_sil, t + 1)
                hidden(j).then_inc(e_link, 1)
                eng.wait_ge(e_link, link_to)
                eng.tensor_copy(HHL[j][:, 0, :], HF[j]).then_inc(e_link, 1)
                eng.wait_ge(e_link, link_to + 1)
                eng.tensor_tensor(HHL[j][:, 1, :], HF[j], HHL[j][:, 0, :], ALU.subtract).then_inc(e_h, 1)

            n = eng.value_load(TAB[0:1, ET.stop - 1:ET.stop], min_val=T_MIN // U, max_val=STEPS_MAX)
            xt_evac(0, 0)
            xt_evac(1, 1)
            h_split(0, 0, 1)
            eng.wait_ge(e_gu, 1)
            xt_evac(2, 0)
            h_split(1, 1, 3)
            with eng.Fori(0, n * U, U) as m:
                for j in range(U):
                    eng.wait_ge(e_gu, m + (2 + j))
                    xt_evac(m + (3 + j), (3 + j) % 2)
                    eng.wait_ge(e_t2, m + (1 + j))
                    h_split(m + (2 + j), j % 2, m * 2 + (5 + 2 * j))

            for i in range(TT):
                for k in range(K8):
                    eng.wait_ge(gathered[k], 16 * (i + 1))
                    if k >= 1 or i >= 1:
                        eng.wait_ge(dve_comb, K8 * i + k)
                    eng.scalar_tensor_tensor(out=ACC[:, i, :], in0=RING[:, k, :], scalar=WK[:, i, k:k + 1],
                                             in1=ACC[:, i, :], op0=ALU.mult, op1=ALU.add).then_inc(dve_comb, 1)


def kernel(x, ctx_1024, g_xattn, g_ffn, L0_xattn_w_q, L0_xattn_w_k, L0_xattn_w_v, L0_xattn_w_o, L0_ffn_gate_w,
           L0_ffn_gate_bias, L0_ffn_Wg, L0_ffn_Wu, L0_ffn_Wd, L0_ffn_Sg, L0_ffn_Su, L0_ffn_Sd):
    import numpy as np
    import concourse.bacc as bacc
    from concourse.bass_utils import run_bass_kernel_spmd

    a = np.asarray
    S, D = x.shape[1], x.shape[2]
    E, IW = L0_ffn_Wg.shape[0], L0_ffn_Wg.shape[1]
    I2 = IW // 2

    def chunks(w):
        w = a(w)
        return w.reshape(w.shape[0] // 128, 128, w.shape[1]).transpose(1, 0, 2)

    wo = np.zeros((4, 4, 32, D), np.float32)
    wo[:, :, 0:16, :] = a(L0_xattn_w_o).T.reshape(4, 4, 16, D)
    gate = np.concatenate([a(L0_ffn_Wg), a(L0_ffn_Sg).reshape(2, IW, D)])
    up = np.concatenate([a(L0_ffn_Wu), a(L0_ffn_Su).reshape(2, IW, D)])
    gu = np.concatenate([gate, up], axis=1)
    wgu = gu.transpose(0, 2, 1).reshape(E + 2, 2, 128, 2 * IW).transpose(0, 2, 1, 3).reshape(E + 2, 128, 4 * IW)
    down = np.concatenate([a(L0_ffn_Wd), a(L0_ffn_Sd).reshape(D, 2, IW).transpose(1, 0, 2)])
    wd = down.transpose(0, 2, 1).reshape(E + 2, 2, I2, D).transpose(0, 2, 1, 3).reshape(E + 2, I2, 2 * D)
    w = np.zeros((E + 2, 128, 4 * IW + 2 * D), np.float32)
    w[:, :, 0:4 * IW] = wgu
    w[:, 0:I2, 4 * IW:] = wd
    arrays = {
        "x": a(x).reshape(S, D),
        "ctxT": chunks(a(ctx_1024)[0].T),
        "wq": chunks(a(L0_xattn_w_q).T),
        "wkv": chunks(np.concatenate([a(L0_xattn_w_k), a(L0_xattn_w_v)]).T),
        "wo": wo.reshape(4, 128, D).transpose(1, 0, 2),
        "router": chunks(a(L0_ffn_gate_w).T),
        "bias": a(L0_ffn_gate_bias).reshape(1, E),
        "gates": np.concatenate([a(g_xattn).reshape(1), a(g_ffn).reshape(1)]).reshape(1, 2),
        "w": w,
    }
    arrays = {"in_" + k: np.ascontiguousarray(v) for k, v in arrays.items()}
    nc = bacc.Bacc("TRN2", target_bir_lowering=False, num_devices=1)
    args = [nc.dram_tensor(k, v.shape, mybir.dt.from_np(v.dtype), kind="ExternalInput").ap() for k, v in arrays.items()]
    args.append(nc.dram_tensor("out", (S, D), mybir.dt.float32, kind="ExternalOutput").ap())
    flamingo_gated_block(nc, *args)
    r = run_bass_kernel_spmd(nc, [arrays], core_ids=[0])
    return r.results[0]["out"].reshape(x.shape)
```

```python
import concourse.bass as bass
from concourse import mybir
from contextlib import ExitStack


def flamingo_gated_block(
    nc: bass.Bass,
    x_in: bass.AP,
    ctxT_in: bass.AP,
    wq_in: bass.AP,
    wkv_in: bass.AP,
    wo_in: bass.AP,
    router_in: bass.AP,
    bias_in: bass.AP,
    gates_in: bass.AP,
    w_in: bass.AP,
    out: bass.AP,
):
    f32 = mybir.dt.float32
    bf16 = mybir.dt.bfloat16
    i32 = mybir.dt.int32
    u32 = mybir.dt.uint32
    ALU = mybir.AluOpType
    ACT = mybir.ActivationFunctionType
    AX = mybir.AxisListType
    RMAX = bass.bass_isa.ReduceOp.max
    ds = bass.ds

    P = 128
    S, D = x_in.shape
    KV = ctxT_in.shape[2]
    NH = 16
    DK = D // NH
    TT = S // P
    KC = -(-KV // P)
    KR = [min(P, KV - P * c) for c in range(KC)]
    QB = 512
    NB = S // QB
    TB = QB // P
    NG = NH // 4
    NT = 6
    AUG = NT * DK + 2
    EPS = 1e-5
    SHIFT_MAX = 40.0

    E = router_in.shape[2]
    K8 = 8
    WALL = w_in.shape[2]
    WGU = WALL - 2 * D
    IW = WGU // 4
    I2 = IW // 2
    WSPLIT = 2 * WALL
    DHI = WGU
    DLO = WALL + WGU
    NSTG = 4
    NSLOT = 8
    REGION = S + P
    T_MAX = K8 * S // P + E - 1
    NTAB = 200
    SCALE_OUT = 2.5

    dispatch = nc.dram_tensor("dispatch_rows", (E * REGION + P, 2 * D), bf16).ap()
    T_MIN = K8 * S // P
    U = 4
    STEPS_MAX = -(-T_MAX // U)
    expert_out = nc.dram_tensor("expert_rows", (U * STEPS_MAX * P, D), f32).ap()

    ctx = ExitStack()
    with ctx:
        def sb(name, shape, dt):
            return ctx.enter_context(nc.sbuf_tensor(name, shape, dt))

        def sem(name):
            return ctx.enter_context(nc.semaphore(name))

        KT = sb("KT", [P, NH * KV + 16], bf16)
        QT = sb("QT", [P, NB * NH * QB], bf16)
        VA = sb("VA", [P, KC * NH * 32], f32)
        PR = sb("PR", [P, 3 * 4 * QB], f32)
        ACC = sb("ACC", [P, TT, D], f32)
        SCR = sb("SCR", [P, 3584], f32)
        wo = sb("wo", [P, NG, D], f32)
        gw = sb("gw", [P, 2, E], f32)
        bias = sb("bias", [P, E], f32)
        gates = sb("gates", [P, 2], f32)
        tg = sb("tg", [P, 2], f32)
        identf = sb("identf", [P, P], f32)
        identb = sb("identb", [P, P], bf16)
        before = sb("before", [P, P], bf16)
        upto = sb("upto", [E, E], f32)
        ones_b = sb("ones_b", [P, P], bf16)
        ones_f = sb("ones_f", [E, 1], f32)
        zrow = sb("zrow", [P, 2 * D], bf16)
        iota_e = sb("iota_e", [P, E], f32)
        base_e = sb("base_e", [P, E], f32)
        iota_t = sb("iota_t", [E, NTAB], f32)
        turn = sb("turn", [P, 1 + NSLOT], f32)
        stats = sb("stats", [P, 6], f32)
        mv = sb("mv", [P, TT, 2], f32)
        rs = sb("rs", [P, TT], f32)
        rt = sb("rt", [P, TT], f32)
        ri = sb("ri", [P, TT], i32)
        ve = sb("ve", [P, TT], f32)
        kmax = sb("kmax", [P, NH], f32)
        knall = sb("knall", [P, NH], f32)
        NM = sb("NM", [P, TT, NH], f32)
        qn = sb("qn", [P, NH], f32)
        shmax = sb("shmax", [P, 2], f32)
        flag = sb("flag", [P, 1], i32)
        EX = sb("EX", [P, E], f32)
        SCO = sb("SCO", [P, E], f32)
        CF = sb("CF", [P, E], f32)
        G8 = sb("G8", [P, E], f32)
        GS = sb("GS", [P, 8], f32)
        T8 = sb("T8", [P, 8], f32)
        I8 = sb("I8", [P, 8], u32)
        F8 = sb("F8", [P, 8], f32)
        GM = sb("GM", [P, 8], f32)
        W8 = sb("W8", [P, 8], f32)
        W1 = sb("W1", [P, 2], f32)
        MK = sb("MK", [P, E], bf16)
        MSUM = sb("MSUM", [P, E], bf16)
        POS = sb("POS", [P, E], f32)
        IDX = sb("IDX", [P, TT, K8], u32)
        WK = sb("WK", [P, TT, K8], f32)
        cnt = sb("cnt", [E, 1], f32)
        cti = sb("cti", [E, 1], i32)
        ctf = sb("ctf", [E, 1], f32)
        cum = sb("cum", [E, 1], f32)

        SP4 = ctx.enter_context(nc.psum_tensor("SP4", [P, 4 * 512], f32))
        PVB = [ctx.enter_context(nc.psum_tensor(f"PVB{i}", [P, 512], f32)) for i in range(2)]
        M0 = ctx.enter_context(nc.psum_tensor("M0", [P, 512], f32))
        M1 = ctx.enter_context(nc.psum_tensor("M1", [P, 512], f32))
        BANKS = [SP4[:, 512 * i:512 * i + 512] for i in range(4)] + [PVB[0][:, :], PVB[1][:, :], M0[:, :], M1[:, :]]

        KTv = KT[:, 0:NH * KV].rearrange("p (h k) -> p h k", h=NH)
        QTv = QT[:, :].rearrange("p (b h q) -> p b h q", b=NB, h=NH)
        VAv = VA[:, :].rearrange("p (c h d) -> p c h d", c=KC, h=NH)
        PRv = PR[:, :].rearrange("p (s h q) -> p s h q", s=3, h=4)

        KN = QT[:, 0:2 * KC * NH].bitcast(f32).rearrange("p (c h) -> p c h", c=KC)

        def attnT(b, g):
            o = (b * NH + 4 * g) * QB
            return QT[:, o:o + 2 * QB].bitcast(f32)

        def h2T_cols(i):
            b, j = i // TB, i % TB
            o = b * NH * QB
            v = QT[:, o:o + NH * QB].rearrange("p (g r) -> p g r", g=4)
            return v[:, :, 2 * QB + P * j:2 * QB + P * (j + 1)]

        ctxT = PR[:, 0:2 * KV].rearrange("p (c k) -> p c k", c=2)
        wkv = PR[:, 2 * KV:2 * KV + 1024].rearrange("p (c n) -> p c n", c=2)
        wq = PR[:, 2 * KV + 1024:2 * KV + 1536].rearrange("p (c n) -> p c n", c=2)
        AW = NH * AUG
        AUGT = [SCR[:, j * (AW // 2):(j + 1) * (AW // 2)].bitcast(bf16).rearrange("p (h a) -> p h a", h=NH)
                for j in range(2)]
        o = 2 * KV + 1536
        AUGT.append(PR[:, o:o + AW // 2].bitcast(bf16).rearrange("p (h a) -> p h a", h=NH))
        SQ = SCR[:, AW:AW + D]
        R1 = [SCR[:, AW + D * (1 + j):AW + D * (2 + j)] for j in range(2)]
        QS = [SCR[:, AW + 3 * D:AW + 4 * D], PR[:, o + AW // 2:o + AW // 2 + D]]
        XN = SCR[:, AW + 4 * D:AW + 5 * D]
        XNT = SCR[:, AW + 5 * D:AW + 6 * D]
        CHOSEN = NM[:, 0:TT // 2, :].rearrange("p t (u k) -> p (t u) k", k=K8)
        IDX2 = NM[:, TT // 2:TT, :].bitcast(u32).rearrange("p t (u k) -> p (t u) k", k=K8)
        MROW = SCR[:, 0:NH]
        MHL = SCR[:, NH:2 * NH].bitcast(bf16).rearrange("p (h t) -> p h t", h=NH)

        OS = SCR[:, 0:512]
        RS = SCR[:, 512:1024]
        H2S = SCR[:, 1024:1280]
        H2T = SCR[:, 1280:1536]
        XR = [SCR[:, 1536 + D * j:1536 + D * (j + 1)].bitcast(bf16) for j in range(4)]
        TABF = SCR[0:1, 0:5 * NTAB]
        CTB = EX[0:E, :].bitcast(bf16)
        DELTA = POS[:, :]
        A8 = SCR[:, 2560:3072]
        PX = SCR[:, 3072:3584]

        H2L = [attnT(NB - 1, j // 2)[:, D * (j % 2):D * (j % 2 + 1)] for j in range(TB)]
        H2TL = [attnT(NB - 1, 2 + j // 2)[:, D * (j % 2):D * (j % 2 + 1)] for j in range(TB)]
        SCOL = [H2S[:, E * j:E * (j + 1)] for j in range(TB)]
        EXL = [H2T[:, E * j:E * (j + 1)] for j in range(TB)]
        OPL = [BANKS[6 if j % 2 == 0 else 1][:, D * (j // 2):D * (j // 2 + 1)] for j in range(TB)]

        STG = [KT[:, (NSLOT + j) * WSPLIT:(NSLOT + j + 1) * WSPLIT].bitcast(f32) for j in range(2)] \
            + [VA[:, 4224 + WALL * j:4224 + WALL * (j + 1)] for j in range(2)]
        SW = [PR[:, (WSPLIT // 2) * s:(WSPLIT // 2) * (s + 1)].bitcast(bf16) for s in range(2)]
        RING = QT[:, 0:2 * 2 * K8 * D].bitcast(f32).rearrange("p (k n) -> p k n", k=2 * K8)
        XG = [VA[:, D * j:D * (j + 1)].bitcast(bf16) for j in range(2)] \
            + [PR[:, 5280 + D * j:5280 + D * (j + 1)].bitcast(bf16) for j in range(2)]
        XT = [VA[:, 512 + 256 * j:512 + 256 * (j + 1)].bitcast(bf16) for j in range(2)]
        SIL = [VA[:, 1024 + IW * j:1024 + IW * (j + 1)] for j in range(2)]
        HF = [VA[:, 1376 + IW * j:1376 + IW * (j + 1)] for j in range(2)]
        HHL = [VA[:, 1728 + IW * j:1728 + IW * (j + 1)].bitcast(bf16).rearrange("p (t n) -> p t n", t=2) for j in range(2)]
        HT = [VA[:, 2080 + 256 * j:2080 + 256 * (j + 1)].bitcast(bf16) for j in range(2)]
        YB = [VA[:, 2592 + D * j:2592 + D * (j + 1)] for j in range(2)]
        TAB = VA[0:1, 3200:3200 + 5 * NTAB].bitcast(i32)
        PACK = PR[0:1, WSPLIT:WSPLIT + NTAB].bitcast(i32)
        XTP = [BANKS[j][:, 0:256].bitcast(bf16) for j in range(2)]
        GUP = [BANKS[2 + j] for j in range(2)]
        HTP = [BANKS[4 + j][:, 0:256].bitcast(bf16) for j in range(2)]
        YP = [BANKS[6 + j][:, 0:D] for j in range(2)]
        SHY = BANKS[0][:, 0:D]

        ctx_in = sem("ctx_in"); wkv_in_s = sem("wkv_loaded"); x_loaded = sem("x_loaded"); wq_loaded = sem("wq_loaded")
        small_loaded = sem("small_loaded"); consts = sem("consts"); gates_done = sem("gates_done")
        pe_kv = sem("pe_kv"); act_kh = sem("act_kh"); act_v = sem("act_v"); dve_r1 = sem("dve_r1"); act_km = sem("act_km")
        dve_ka = sem("dve_ka"); pe_kt = sem("pe_kt"); dve_kt = sem("dve_kt"); dve_kn = sem("dve_kn"); pool_kmax = sem("pool_kmax")
        dve_xn = sem("dve_xn"); pe_xt = sem("pe_xt"); dve_xt = sem("dve_xt"); pe_q = sem("pe_q"); act_qs = sem("act_qs")
        act_qh = sem("act_qh"); pool_r1 = sem("pool_r1"); act_qm = sem("act_qm"); pool_ql = sem("pool_ql"); dve_qn = sem("dve_qn")
        dve_m = sem("dve_m"); pe_qt = sem("pe_qt"); dve_qt = sem("dve_qt")
        dve_top = sem("dve_top"); pool_top = sem("pool_top"); dve_flag = sem("dve_flag")
        gen_s = sem("gen_s"); gen_m = sem("gen_m"); gen_split = sem("gen_split"); gen_t = sem("gen_t"); gen_qt = sem("gen_qt")
        gen_chain = sem("gen_chain")
        pe_qk = sem("pe_qk"); act_exp = sem("act_exp"); pe_pv = sem("pe_pv"); dve_pv = sem("dve_pv"); dve_attn = sem("dve_attn")
        pe_op = sem("pe_op"); dve_h2 = sem("dve_h2"); pool_xr = sem("pool_xr"); pe_h2t = sem("pe_h2t"); dve_h2t = sem("dve_h2t")
        dve_hl = sem("dve_hl"); pe_lg = sem("pe_lg"); act_sig = sem("act_sig"); dve_mk = sem("dve_mk"); pe_rank = sem("pe_rank")
        dve_msum = sem("dve_msum"); dve_idx = sem("dve_idx"); dve_idx2 = sem("dve_idx2")
        scattered = [sem(f"scattered{j}") for j in range(4)]
        dummy_zero = sem("dummy_zero"); rest_zero = sem("rest_zero"); padded = sem("padded")
        pe_tab = sem("pe_tab"); chain_tab = sem("dve_tab_parts"); dve_pad = sem("dve_pad"); dve_rows = sem("dve_rows")
        dve_tab = sem("dve_tab")
        w_loaded = [sem(f"w_loaded{j}") for j in range(NSTG)]
        w_first = [sem(f"w_first{j}") for j in range(2)]
        w_split = sem("w_split")
        sh_gu = sem("sh_gu"); sh_sil = sem("sh_sil"); sh_h = sem("sh_h"); sh_t = sem("sh_t"); sh_te = sem("sh_te")
        sh_y = sem("sh_y"); sh_ye = sem("sh_ye")
        xg_loaded = [sem(f"xg_loaded{j}") for j in range(U)]
        e_t1 = sem("e_t1"); e_xt = sem("e_xt"); e_gu = sem("e_gu"); e_sil = sem("e_sil"); e_link = sem("hidden_chain")
        e_h = sem("e_h"); e_t2 = sem("e_t2"); e_te = sem("e_te"); tiles_done = sem("tiles_done"); e_ye = sem("e_ye")
        y_stored = [sem(f"y_stored{j}") for j in range(2)]
        rows_done = sem("rows_done")
        gathered = [sem(f"gathered{k}") for k in range(2 * K8)]
        dve_comb = sem("dve_comb"); out_done = sem("out_done")
        chain = sem("vector_chain"); pchain = sem("pool_chain")

        AT_OUT, AT_TURN, AT_ROUTE, AT_RANK = (3, 11, 24, 35), (7, 18, 28, 39), (9, 21, 30, 42), (14, 25, 36, 47)
        N_SPLIT0 = 2
        ET, RT, SPARE, PADR, WAITC = (slice(NTAB * n, NTAB * (n + 1)) for n in range(5))
        def registers(eng, ap, most):
            return nc.values_load_multi_w_load_instructions(ap, engines=[eng.engine], min_val=0, max_val=most)[1]

        COUNT = slice(SPARE.start, SPARE.start + 1)

        block = ctx.enter_context(nc.Block())

        @block.sync
        def _(eng):
            eng.dma_start(ctxT, ctxT_in).then_inc(ctx_in, 16)
            eng.dma_start(wkv, wkv_in).then_inc(wkv_in_s, 16)
            eng.dma_start(wq, wq_in).then_inc(wq_loaded, 16)
            eng.dma_start(ACC[:, :, :], x_in.rearrange("(t p) n -> p t n", p=P)).then_inc(x_loaded, 16)
            eng.dma_start(gates[:, :], gates_in.broadcast_to((P, 2))).then_inc(small_loaded, 16)
            eng.dma_start(bias[:, :], bias_in.broadcast_to((P, E))).then_inc(small_loaded, 16)
            eng.dma_start(wo[:, :, :], wo_in).then_inc(small_loaded, 16)
            eng.dma_start(gw[:, :, :], router_in).then_inc(small_loaded, 16)
            eng.wait_ge(consts, 1)
            eng.wait_ge(pe_kt, 2 * KC)
            eng.dma_start(expert_out[T_MIN * P:, :].rearrange("(t p) n -> p t n", p=P),
                          zrow[:, :].bitcast(f32).rearrange("p (o n) -> p o n", o=1).broadcast_to((P, U * STEPS_MAX - T_MIN, D)))\
               .then_inc(rest_zero, 16)
            eng.dma_start(dispatch[E * REGION:E * REGION + P, :], zrow[:, :]).then_inc(dummy_zero, 16)

            def pad(e4):
                first = registers(eng, TAB[0:1, ds(e4 * U + PADR.start, U)], E * REGION - P)
                for j in range(U):
                    eng.dma_start(dispatch[ds(first[j], P), :], zrow[:, :]).then_inc(padded, 16)

            def load(t4, first_time=False):
                first = registers(eng, TAB[0:1, ds(t4 * U + RT.start, U)], E * REGION)
                for j in range(U):
                    if not first_time:
                        eng.wait_ge(e_t1, t4 * U + (j + 1 - U))
                    eng.dma_start(XG[j], dispatch[ds(first[j], P), :]).then_inc(xg_loaded[j], 16)

            eng.wait_ge(dve_pad, 1)
            pad(0)
            pad(1)
            eng.wait_ge(rest_zero, 16)
            eng.wait_ge(dummy_zero, 16)
            for j in range(4):
                eng.wait_ge(scattered[j], 16 * K8 * TT // 4)
            eng.wait_ge(padded, 16 * 2 * U)
            eng.wait_ge(dve_rows, 1)
            n = eng.value_load(TAB[0:1, COUNT], min_val=T_MIN // U, max_val=STEPS_MAX)
            load(0, first_time=True)
            with eng.Fori(0, E // U - 2) as i:
                eng.wait_ge(padded, i * (16 * U) + 32 * U)
                pad(i + 2)
                load(i + 1)
            eng.wait_ge(padded, 16 * E)
            with eng.Fori(E // U - 2, n) as i:
                load(i + 1)

            for i in range(TT):
                eng.wait_ge(dve_comb, K8 * (i + 1))
                eng.dma_start(out[i * P:(i + 1) * P, :], ACC[:, i, :]).then_inc(out_done, 16)
            eng.wait_ge(out_done, 16 * TT)

        @block.gpsimd
        def _(eng):
            eng.memset(zrow[:, :], 0.0).then_inc(consts, 1)
            eng.memset(identf[:, :], 0.0)
            eng.memset(before[:, :], 1.0)
            eng.memset(ones_b[:, :], 1.0)
            eng.memset(ones_f[:, :], 1.0)
            eng.memset(upto[:, :], 1.0)
            eng.memset(MSUM[:, :], 0.0)
            eng.memset(turn[:, :], 0.0)
            eng.iota(iota_e[:, :], [[1, E]], base=0, channel_multiplier=0, allow_small_or_imprecise_dtypes=True)
            eng.iota(iota_t[:, :], [[1, NTAB]], base=0, channel_multiplier=0,
                     allow_small_or_imprecise_dtypes=True).then_inc(pchain, 1)
            eng.wait_ge(pchain, 1)
            eng.affine_select(out=identf[:, :], in_=identf[:, :], compare_op=ALU.not_equal, fill=1.0, base=0,
                              pattern=[[-1, P]], channel_multiplier=1)
            eng.affine_select(out=before[:, :], in_=before[:, :], compare_op=ALU.is_gt, fill=0.0, base=0,
                              pattern=[[1, P]], channel_multiplier=-1)
            eng.affine_select(out=upto[:, :], in_=upto[:, :], compare_op=ALU.is_ge, fill=0.0, base=0,
                              pattern=[[1, E]], channel_multiplier=-1)
            eng.tensor_scalar(base_e[:, :], iota_e[:, :], float(REGION), None, ALU.mult).then_inc(pchain, 1)
            eng.wait_ge(pchain, 2)
            eng.tensor_scalar(identb[:, :], identf[:, :], 1.0, None, ALU.mult).then_inc(consts, 1)
            for j in range(3):
                eng.memset(AUGT[j][:, :, NT * DK:AUG], 1.0)
            eng.memset(KN[:, :, :], 0.0)
            eng.memset(VAv[:, :, :, DK:2 * DK], 1.0).then_inc(consts, 1)

            eng.wait_ge(dve_kn, KC + 1)
            eng.partition_all_reduce(knall[:, :], kmax[:, :], P, RMAX).then_inc(pool_kmax, 1)
            def second_split(t):
                eng.wait_ge(act_qh, t + 1)
                if t >= 2:
                    eng.wait_ge(act_qm, t - 1)
                    eng.wait_ge(pool_ql, t - 1)
                eng.tensor_tensor(R1[t % 2], QS[t % 2], AUGT[t % 3][:, :, 0:DK], ALU.subtract).then_inc(pool_r1, 1)

            def third_split(t):
                eng.wait_ge(act_qm, t + 1)
                eng.tensor_tensor(AUGT[t % 3][:, :, 5 * DK:6 * DK], R1[t % 2].rearrange("p (h d) -> p h d", h=NH),
                                  AUGT[t % 3][:, :, 3 * DK:4 * DK], ALU.subtract).then_inc(pool_ql, 1)

            second_split(0)
            for t in range(1, TT):
                second_split(t)
                third_split(t - 1)
            third_split(TT - 1)
            eng.wait_ge(dve_top, 1)
            eng.partition_all_reduce(shmax[:, 1:2], shmax[:, 0:1], P, RMAX).then_inc(pool_top, 1)

            def rows(i):
                H2 = H2S if i < TT - TB else H2L[i - (TT - TB)]
                eng.wait_ge(dve_h2, i + 1)
                if i >= 4:
                    eng.wait_ge(scattered[i % 4], 16 * K8 * (i // 4))
                eng.tensor_scalar(XR[i % 4][:, 0:D], H2, 1.0, None, ALU.mult).then_inc(pool_xr, 1)
                eng.wait_ge(pool_xr, 2 * i + 1)
                eng.tensor_tensor(XR[i % 4][:, D:2 * D], H2, XR[i % 4][:, 0:D], ALU.subtract).then_inc(pool_xr, 1)

            def scatter(i):
                eng.wait_ge(pool_xr, 2 * i + 2)
                eng.wait_ge(dve_idx, i + 1)
                for k in range(K8):
                    eng.indirect_dma_start(out=dispatch, out_offset=bass.IndirectOffsetOnAxis(ap=IDX[:, i, k:k + 1], axis=0),
                                           in_=XR[i % 4], in_offset=None).then_inc(scattered[i % 4], 16)

            for i in range(TT - TB):
                rows(i)
                if i < TT - TB - 1:
                    scatter(i)
            def load_w(e, st):
                eng.dma_start(STG[st], w_in[ds(e, 1), :, :].rearrange("o p n -> p (o n)")).then_inc(w_loaded[st], 16)

            def first_part(st, par, hi):
                eng.dma_start(hi, STG[st]).then_inc(w_first[par], 16)

            def second_part(st, hi, lo):
                eng.tensor_tensor(lo, STG[st], hi, ALU.subtract).then_inc(w_split, 1)

            eng.wait_ge(pe_qk, 2 * NB * NG * KC)
            for s in range(2):
                load_w(E + s, s)
            eng.wait_ge(pe_pv, NB * NG * KC)
            for s in range(2):
                load_w(s, 2 + s)
            for s in range(2):
                eng.wait_ge(w_loaded[s], 16)
                first_part(s, s, SW[s][:, 0:WALL])
            scatter(TT - TB - 1)
            for s in range(2):
                eng.wait_ge(w_first[s], 16)
                second_part(s, SW[s][:, 0:WALL], SW[s][:, WALL:2 * WALL])
            for s in range(2):
                eng.wait_ge(w_split, s + 1)
                load_w(2 + s, s)
            for i in range(TT - TB, TT):
                rows(i)

            def slot(j):
                return KT[:, j * WSPLIT:j * WSPLIT + WALL], KT[:, j * WSPLIT + WALL:(j + 1) * WSPLIT]

            def expert_first(i, j):
                w = eng.value_load(TAB[0:1, ds(i * NSLOT + (WAITC.start + j), 1)], min_val=1, max_val=T_MAX + 1)
                eng.wait_ge(w_loaded[(j + 2) % NSTG], i * (16 * NSLOT // NSTG) + 16 * ((j + 2) // NSTG + 1))
                eng.wait_ge(tiles_done, w)
                eng.tensor_tensor(turn[:, j + 1:j + 2], turn[:, 0:1], turn[:, 0:1], ALU.add)
                first_part((j + 2) % NSTG, j % 2, slot(j)[0])

            def expert_second(i, j, more):
                eng.wait_ge(w_first[j % 2], i * (16 * NSLOT // 2) + 16 * (j // 2 + 2))
                second_part((j + 2) % NSTG, *slot(j))
                if more:
                    eng.wait_ge(w_split, i * NSLOT + (N_SPLIT0 + j + 1))
                    load_w(i * NSLOT + (j + NSTG), (j + 2) % NSTG)

            def first_group_first(j):
                eng.wait_ge(w_loaded[(j + 2) % NSTG], 16 * ((j + 2) // NSTG + 1))
                first_part((j + 2) % NSTG, j % 2, slot(j)[0])

            first_group_first(0)
            for j in range(NSLOT):
                if j < NSLOT - 1:
                    first_group_first(j + 1)
                expert_second(0, j, True)
                if j >= NSLOT - TB:
                    scatter(TT - NSLOT + j)
            eng.wait_ge(dve_tab, 1)
            expert_first(1, 0)
            with eng.Fori(1, E // NSLOT - 1) as i:
                for j in range(NSLOT):
                    if j < NSLOT - 1:
                        expert_first(i, j + 1)
                    else:
                        expert_first(i + 1, 0)
                    expert_second(i, j, True)
            for j in range(NSLOT):
                if j < NSLOT - 1:
                    expert_first(E // NSLOT - 1, j + 1)
                expert_second(E // NSLOT - 1, j, j < NSLOT - NSTG)

            eng.wait_ge(rows_done, 1)
            for i in range(TT):
                eng.wait_ge(dve_idx2, i + 1)
                for k in range(K8):
                    r = i % 2 * K8 + k
                    if i >= 2:
                        eng.wait_ge(dve_comb, K8 * (i - 2) + k + 1)
                    eng.indirect_dma_start(out=RING[:, r, :], out_offset=None, in_=expert_out,
                                           in_offset=bass.IndirectOffsetOnAxis(ap=IDX2[:, i, k:k + 1], axis=0)).then_inc(gathered[r], 16)

        @block.scalar
        def _(eng):
            eng.wait_ge(small_loaded, 64)
            eng.activation(tg[:, :], gates[:, :], ACT.Tanh).then_inc(gates_done, 1)

            def heads3(t, lo, hi, step=1):
                return t.rearrange("p h (n d) -> p h n d", d=DK)[:, :, lo:hi:step, :]

            def key_first(c):
                r, kv = KR[c], BANKS[c % 2]
                eng.wait_ge(pe_kv, c + 1)
                if c >= 3:
                    eng.wait_ge(pe_kt, 2 * (c - 2))
                src = kv[0:r, 0:D].rearrange("p (h o d) -> p h o d", h=NH, o=1).broadcast_to((r, NH, 3, DK))
                eng.activation(heads3(AUGT[c % 3][0:r, :, 0:NT * DK], 1, NT, 2), src, ACT.Copy).then_inc(act_kh, 1)
                if c >= 1:
                    eng.wait_ge(dve_kn, c)
                eng.activation(SQ[0:r, :], kv[0:r, 0:D], ACT.Square).then_inc(act_v, 1)
                eng.activation(VAv[0:r, c, :, 0:DK], kv[0:r, D:2 * D].rearrange("p (h d) -> p h d", h=NH),
                               ACT.Copy).then_inc(act_v, 1)

            def key_second(c):
                r = KR[c]
                eng.wait_ge(dve_r1, c + 1)
                src = R1[c % 2][0:r, :].rearrange("p (h o d) -> p h o d", h=NH, o=1).broadcast_to((r, NH, 2, DK))
                eng.activation(heads3(AUGT[c % 3][0:r, :, 0:NT * DK], 2, 5, 2), src, ACT.Copy).then_inc(act_km, 1)

            eng.wait_ge(consts, 3)
            key_first(0)
            for c in range(1, KC):
                key_first(c)
                key_second(c - 1)
            key_second(KC - 1)

            eng.wait_ge(dve_ka, KC)

            def query_first(t):
                qa = AUGT[t % 3][:, :, 0:NT * DK]
                qs = QS[t % 2]
                eng.wait_ge(pe_q, t + 1)
                if t >= 2:
                    eng.wait_ge(pool_r1, t - 1)
                    eng.wait_ge(dve_qn, t - 1)
                eng.activation(qs, PVB[1][:, 0:D], ACT.Copy, scale=1.0 / DK ** 0.5).then_inc(act_qs, 1)
                eng.wait_ge(act_qs, t + 1)
                if t == 0:
                    eng.wait_ge(pe_kt, 2 * KC)
                if t >= 3:
                    eng.wait_ge(pe_qt, 2 * (t - 2))
                src = qs.rearrange("p (h o d) -> p h o d", h=NH, o=1).broadcast_to((P, NH, 3, DK))
                eng.activation(heads3(qa, 0, 3), src, ACT.Copy).then_inc(act_qh, 1)
                if t >= 1:
                    eng.wait_ge(dve_qn, t)
                eng.activation(SQ, qs, ACT.Square).then_inc(act_v, 1)

            def query_second(t):
                eng.wait_ge(pool_r1, t + 1)
                src = R1[t % 2].rearrange("p (h o d) -> p h o d", h=NH, o=1).broadcast_to((P, NH, 2, DK))
                eng.activation(heads3(AUGT[t % 3][:, :, 0:NT * DK], 3, 5), src, ACT.Copy).then_inc(act_qm, 1)

            query_first(0)
            for t in range(1, TT):
                query_first(t)
                query_second(t - 1)
            query_second(TT - 1)

            def sigmoid_exp(i):
                eng.wait_ge(pe_lg, i + 1)
                if i >= 1:
                    eng.wait_ge(dve_mk, i)
                eng.activation(EX[:, :], M1[:, 0:E], ACT.Exp, scale=-1.0).then_inc(act_sig, 1)

            for n in range(NB * NG * KC):
                b, c = n // (NG * KC), n % KC
                r = KR[c]
                for p in range(2):
                    eng.wait_ge(pe_qk, 2 * n + p + 1)
                    if n >= 3:
                        eng.wait_ge(pe_pv, n - 2)
                    eng.activation(PRv[0:r, n % 3, 2 * p:2 * p + 2, :],
                                   SP4[0:r, 1024 * p:1024 * p + 1024].rearrange("p (h q) -> p h q", h=2),
                                   ACT.Exp).then_inc(act_exp, 1)
                m = n % (NG * KC)
                if b >= 1 and m - 1 in AT_ROUTE:
                    sigmoid_exp((b - 1) * TB + AT_ROUTE.index(m - 1))
            def sh_silu(cnt_gu, s):
                eng.wait_ge(sh_gu, cnt_gu)
                eng.activation(SIL[s], GUP[s][:, 0:IW], ACT.Silu).then_inc(sh_sil, 1)

            def sh_evac(cnt_t, s):
                eng.wait_ge(sh_t, cnt_t)
                eng.activation(HT[s][0:I2, :], HTP[s][0:I2, :], ACT.Copy).then_inc(sh_te, 1)

            for i in range(TT):
                if i == 4:
                    eng.wait_ge(pe_lg, TT)
                    for j in range(TB):
                        eng.activation(EXL[j], M1[:, E * j:E * (j + 1)], ACT.Exp, scale=-1.0).then_inc(act_sig, 1)
                for s in range(2):
                    if i >= 1:
                        eng.wait_ge(sh_h, 2 * (i - 1) + s + 1)
                    sh_silu(2 * i + s + 1, s)
                if i >= 1:
                    if i >= 2:
                        eng.wait_ge(sh_y, i - 1)
                    for s in range(2):
                        sh_evac(2 * (i - 1) + s + 1, s)
            eng.wait_ge(sh_y, TT - 1)
            for s in range(2):
                sh_evac(2 * (TT - 1) + s + 1, s)

            def silu(t, j):
                eng.wait_ge(e_gu, t + 1)
                eng.activation(SIL[j], GUP[j][:, 0:IW], ACT.Silu).then_inc(e_sil, 1)

            def ht_evac(t, j):
                eng.wait_ge(e_t2, t + 1)
                eng.activation(HT[j][0:I2, :], HTP[j][0:I2, :], ACT.Copy).then_inc(e_te, 1)

            def y_out(t, j, first=False):
                eng.wait_ge(tiles_done, t + 2)
                if not first:
                    eng.wait_ge(y_stored[j], t * 8 - 8 * j)
                eng.activation(YB[j], YP[j], ACT.Copy).then_inc(e_ye, 1)
                eng.wait_ge(e_ye, t + 1)
                eng.dma_start(expert_out[ds(t * P, P), :], YB[j]).then_inc(y_stored[j], 16)

            eng.wait_ge(dve_tab, 1)
            eng.wait_ge(sh_y, TT)
            silu(0, 0)
            silu(1, 1)
            ht_evac(0, 0)
            n = eng.value_load(TAB[0:1, COUNT], min_val=T_MIN // U, max_val=STEPS_MAX)
            for t in range(U):
                eng.wait_ge(e_h, t + 1)
                silu(2 + t, t % 2)
                eng.wait_ge(tiles_done, t + 1)
                ht_evac(1 + t, (1 + t) % 2)
                y_out(t, t % 2, first=t < 2)
            with eng.Fori(1, n) as i:
                for j in range(U):
                    eng.wait_ge(e_h, i * U + (j + 1))
                    silu(i * U + (2 + j), j % 2)
                    eng.wait_ge(tiles_done, i * U + (j + 1))
                    ht_evac(i * U + (1 + j), (1 + j) % 2)
                    y_out(i * U + j, j % 2)
            for j in range(2):
                eng.wait_ge(y_stored[j], n * (16 * U // 2))
            eng.activation(tg[:, 0:1], tg[:, 0:1], ACT.Copy).then_inc(rows_done, 1)

        @block.tensor
        def _(eng):
            def mm(o, l, r, start, stop, **kw):
                return eng.matmul(o, l, r, start=start, stop=stop, **kw)

            def kv_rows(c):
                r = KR[c]
                if c >= 2:
                    eng.wait_ge(act_v, 2 * (c - 1))
                    eng.wait_ge(dve_r1, c - 1)
                for k in range(2):
                    i = mm(BANKS[c % 2][0:r, :], ctxT[:, k, c * P:c * P + r], wkv[:, k, :], k == 0, k == 1)
                i.then_inc(pe_kv, 1)

            def kv_transposes(c):
                r = KR[c]
                eng.wait_ge(dve_ka, c + 1)
                for g in range(2):
                    n = 2 * c + g
                    if n >= 2:
                        eng.wait_ge(dve_kt, n - 1)
                    bank = BANKS[2 + n % 2].bitcast(bf16).rearrange("p (h q) -> p h q", h=8)
                    for h in range(8):
                        i = eng.transpose(bank[0:AUG, h, 0:r], AUGT[c % 3][0:r, 8 * g + h, :], identb[0:r, 0:r])
                    i.then_inc(pe_kt, 1)

            def q_rows(t):
                eng.wait_ge(dve_xn, t + 1)
                if t >= 1:
                    eng.wait_ge(dve_xt, t)
                for k in range(2):
                    i = eng.transpose(PVB[0][:, P * k:P * (k + 1)], XN[:, P * k:P * (k + 1)], identf[:, :])
                i.then_inc(pe_xt, 1)
                eng.wait_ge(dve_xt, t + 1)
                if t >= 1:
                    eng.wait_ge(act_qs, t)
                for k in range(2):
                    i = mm(PVB[1][:, 0:D], XNT[:, P * k:P * (k + 1)], wq[:, k, :], k == 0, k == 1)
                i.then_inc(pe_q, 1)

            eng.wait_ge(consts, 3)
            eng.wait_ge(ctx_in, 16)
            eng.wait_ge(wkv_in_s, 16)
            eng.wait_ge(wq_loaded, 16)
            kv_rows(0)
            kv_rows(1)
            for c in range(KC):
                if c + 2 < KC:
                    kv_rows(c + 2)
                if c == KC - 1:
                    q_rows(0)
                kv_transposes(c)

            def q_transposes(t):
                eng.wait_ge(dve_m, t + 1)
                eng.wait_ge(pool_ql, t + 1)
                for g in range(2):
                    n = 2 * t + g
                    eng.wait_ge(dve_kt, 2 * KC)
                    if n >= 2:
                        eng.wait_ge(dve_qt, n - 1)
                    bank = BANKS[2 + n % 2].bitcast(bf16).rearrange("p (h q) -> p h q", h=8)
                    for h in range(8):
                        i = eng.transpose(bank[0:AUG, h, :], AUGT[t % 3][:, 8 * g + h, :], identb[:, :])
                    i.then_inc(pe_qt, 1)

            q_rows(1)
            for t in range(TT):
                if t + 2 < TT:
                    q_rows(t + 2)
                q_transposes(t)

            eng.wait_ge(dve_flag, 1)
            general = eng.value_load(flag[0:1, 0:1], min_val=0, max_val=1)
            with eng.If(general > 0):
                eng.wait_ge(dve_qt, 2 * TT)
                with eng.Fori(0, NB) as b:
                    for j in range(TB):
                        for h in range(NH):
                            if not (j == 0 and h == 0):
                                eng.wait_ge(gen_m, b * (TB * NH) + (j * NH + h))
                            for c in range(4):
                                w = min(512, KV - 512 * c)
                                i = mm(SP4[:, 512 * c:512 * c + w],
                                       QT[0:NT * DK, ds(b * (NH * QB) + (h * QB + j * P), P)],
                                       KTv[0:NT * DK, h, 512 * c:512 * c + w], True, True)
                            i.then_inc(gen_s, 1)
                        eng.wait_ge(gen_split, b * TB + (j + 1))
                        for h in range(NH):
                            bank = BANKS[6 + h // 8].bitcast(bf16)
                            i = eng.transpose(bank[NT * DK:AUG, P * (h % 8):P * (h % 8 + 1)], MHL[:, h, :], identb[:, :])
                        i.then_inc(gen_t, 1)
                        eng.wait_ge(gen_qt, b * TB + (j + 1))
                        eng.wait_ge(gen_m, b * (TB * NH) + (j + 1) * NH)
            eng.nop()

            def scores(n, p):
                b, g, c = n // (NG * KC), n // KC % NG, n % KC
                r = KR[c]
                if n >= 1:
                    eng.wait_ge(act_exp, 2 * (n - 1) + p + 1)
                for u in range(2):
                    h = 4 * g + 2 * p + u
                    i = mm(SP4[0:r, 512 * (2 * p + u):512 * (2 * p + u + 1)], KTv[0:AUG, h, c * P:c * P + r],
                           QTv[0:AUG, b, h, :], True, True)
                i.then_inc(pe_qk, 1)

            def attend(n):
                b, g, c = n // (NG * KC), n // KC % NG, n % KC
                q, r = n // KC, KR[c]
                eng.wait_ge(act_exp, 2 * n + 2)
                if c == 0 and q >= 2:
                    eng.wait_ge(dve_pv, q - 1)
                for u in range(4):
                    i = mm(PVB[q % 2][32 * u:32 * u + 32, :], VAv[0:r, c, 4 * g + u, :], PRv[0:r, n % 3, u, :],
                           c == 0, c == KC - 1)
                i.then_inc(pe_pv, 1)

            def out_proj(i):
                b, j = i // TB, i % TB
                eng.wait_ge(dve_attn, NG * (b + 1))
                if i >= 1:
                    eng.wait_ge(dve_h2t, i)
                for g in range(NG):
                    x = mm(M0[:, 0:D], attnT(b, g)[:, P * j:P * (j + 1)], wo[:, g, :], g == 0, g == NG - 1)
                x.then_inc(pe_op, 1)

            def h2_transpose(i):
                eng.wait_ge(dve_h2, i + 1)
                for k in range(2):
                    x = eng.transpose(M0[:, D + P * k:D + P * (k + 1)], H2S[:, P * k:P * (k + 1)], identf[:, :])
                x.then_inc(pe_h2t, 1)

            def router(i):
                eng.wait_ge(dve_h2t, i + 1)
                if i >= 1:
                    eng.wait_ge(dve_idx, i)
                for k in range(2):
                    x = mm(M1[:, 0:E], H2T[:, P * k:P * (k + 1)], gw[:, k, :], k == 0, k == 1)
                x.then_inc(pe_lg, 1)

            def ranks(i):
                eng.wait_ge(dve_mk, i + 1)
                if i >= 1:
                    eng.wait_ge(dve_msum, i)
                mm(M1[:, E:2 * E], before[:, :], MK[:, :], True, False)
                mm(M1[:, E:2 * E], ones_b[:, :], MSUM[:, :], False, True).then_inc(pe_rank, 1)

            eng.wait_ge(dve_qt, 2 * TT)
            scores(0, 0)
            scores(0, 1)
            STEPS = NB * NG * KC
            for n in range(STEPS):
                if n + 1 < STEPS:
                    scores(n + 1, 0)
                if n >= 1:
                    attend(n - 1)
                if n + 1 < STEPS:
                    scores(n + 1, 1)
                b, m = n // (NG * KC), n % (NG * KC)
                if b >= 1:
                    for j in range(TB):
                        i = (b - 1) * TB + j
                        if m == AT_OUT[j]:
                            out_proj(i)
                        if m == AT_TURN[j]:
                            h2_transpose(i)
                        if m == AT_ROUTE[j]:
                            router(i)
                        if m == AT_RANK[j]:
                            ranks(i)
            attend(STEPS - 1)
            def gate_up(o, xs, w, wlo):
                mm(o, xs(0), w(0), True, False)
                mm(o, xs(0), wlo(0), False, False)
                mm(o, xs(1), w(1), False, False)
                mm(o, xs(1), wlo(1), False, False)
                mm(o, xs(2), w(0), False, False)
                return mm(o, xs(3), w(1), False, True)

            def down(o, ht, w, wlo, first=True, last=True):
                mm(o, ht(0), w(0), first, False)
                mm(o, ht(0), wlo(0), False, False)
                mm(o, ht(1), w(1), False, False)
                mm(o, ht(1), wlo(1), False, False)
                mm(o, ht(2), w(0), False, False)
                return mm(o, ht(3), w(1), False, last)

            def h_transposes(j):
                for q in range(4):
                    x = eng.transpose(HTP[j][0:I2, P * q:P * (q + 1)],
                                      HHL[j][:, q // 2, I2 * (q % 2):I2 * (q % 2 + 1)], identb[:, :])
                return x

            def htv(j):
                return lambda q: HT[j][0:I2, P * q:P * (q + 1)]

            def sh_down(i):
                for s in range(2):
                    eng.wait_ge(sh_h, 2 * i + s + 1)
                    if i >= 1:
                        eng.wait_ge(sh_te, 2 * (i - 1) + s + 1)
                    h_transposes(s).then_inc(sh_t, 1)
                if i >= 1:
                    eng.wait_ge(sh_ye, i)
                for s in range(2):
                    eng.wait_ge(sh_te, 2 * i + s + 1)
                    w = SW[s]
                    x = down(SHY, htv(s), lambda k: w[0:I2, DHI + D * k:DHI + D * (k + 1)],
                             lambda k: w[0:I2, DLO + D * k:DLO + D * (k + 1)], s == 0, s == 1)
                x.then_inc(sh_y, 1)

            def shared(i):
                for s in range(2):
                    if i == 0:
                        eng.wait_ge(w_split, s + 1)
                        eng.wait_ge(act_exp, 2 * STEPS)
                    if i >= 1:
                        eng.wait_ge(sh_h, 2 * (i - 1) + s + 1)
                    w = SW[s]
                    h2 = h2T_cols(i)
                    gate_up(GUP[s][:, 0:2 * IW], lambda q: h2[:, q, :], lambda k: w[:, 2 * IW * k:2 * IW * (k + 1)],
                            lambda k: w[:, WALL + 2 * IW * k:WALL + 2 * IW * (k + 1)]).then_inc(sh_gu, 1)
                if i >= 1:
                    sh_down(i - 1)

            LAST = range(TT - TB, TT)
            eng.wait_ge(dve_attn, NG * NB)
            eng.wait_ge(dve_h2t, TT - TB)
            eng.wait_ge(act_exp, 2 * STEPS)
            for j, i in enumerate(LAST):
                for g in range(NG):
                    x = mm(OPL[j], attnT(NB - 1, g)[:, P * j:P * (j + 1)], wo[:, g, :], g == 0, g == NG - 1)
                x.then_inc(pe_op, 1)
            shared(0)
            shared(1)
            for j, i in enumerate(LAST):
                eng.wait_ge(dve_h2, i + 1)
                for k in range(2):
                    x = eng.transpose(OPL[j][:, P * k:P * (k + 1)], H2L[j][:, P * k:P * (k + 1)], identf[:, :])
                x.then_inc(pe_h2t, 1)
            shared(2)
            shared(3)
            eng.wait_ge(dve_idx, TT - TB)
            for j, i in enumerate(LAST):
                eng.wait_ge(dve_h2t, i + 1)
                for k in range(2):
                    x = mm(M1[:, E * j:E * (j + 1)], H2TL[j][:, P * k:P * (k + 1)], gw[:, k, :], k == 0, k == 1)
                x.then_inc(pe_lg, 1)
            for j, i in enumerate(LAST):
                shared(4 + 2 * j)
                eng.wait_ge(dve_mk, i + 1)
                eng.wait_ge(dve_msum, i)
                eng.wait_ge(dve_h2t, TT)
                mm(OPL[j][:, 0:E], before[:, :], MK[:, :], True, False)
                mm(OPL[j][:, 0:E], ones_b[:, :], MSUM[:, :], False, True).then_inc(pe_rank, 1)
                shared(5 + 2 * j)

            eng.wait_ge(dve_msum, TT)
            eng.wait_ge(act_sig, TT)
            mm(M0[0:E, 0:1], MSUM[:, :], ones_b[:, 0:1], True, True).then_inc(pe_tab, 1)
            shared(12)
            shared(13)
            eng.wait_ge(chain_tab, 1)
            mm(M0[0:E, 8:9], upto[:, :], ctf[:, :], True, True)
            mm(M0[:, 384:384 + E], CTB, before[0:E, 0:E], True, True)
            mm(M0[0:1, 64:64 + E], cnt[:, :], identf[0:E, 0:E], True, True).then_inc(pe_tab, 1)
            shared(14)
            eng.wait_ge(chain_tab, 2)
            CMP = A8[0:E, 0:NTAB]
            mm(M1[0:1, 0:NTAB], ones_f[:, :], CMP, True, True)
            mm(M1[0:1, 256:256 + NTAB], ctf[:, :], CMP, True, True)
            mm(M0[0:1, 256:256 + E], cum[:, :], identf[0:E, 0:E], True, True).then_inc(pe_tab, 1)
            shared(15)
            sh_down(TT - 1)
            eng.wait_ge(dve_tab, 1)
            eng.wait_ge(sh_ye, TT)
            eng.transpose(HTP[0][0:I2, 0:P], HHL[0][:, 0, 0:I2], identb[:, :]).then_inc(tiles_done, 1)

            def t1(j, cnt_x):
                eng.wait_ge(xg_loaded[j], cnt_x)
                for q in range(4):
                    x = eng.transpose(XTP[j % 2][:, P * q:P * (q + 1)], XG[j][:, P * q:P * (q + 1)], identb[:, :])
                x.then_inc(e_t1, 1)

            def slot_of(e):
                return KT[:, ds((e % NSLOT) * WSPLIT, WSPLIT)]

            def gu(t, j, e):
                slot = slot_of(e)
                eng.wait_ge(e_xt, t + 1)
                eng.wait_ge(w_split, e + (N_SPLIT0 + 1))
                x = XT[j]
                gate_up(GUP[j][:, 0:2 * IW], lambda q: x[:, P * q:P * (q + 1)], lambda k: slot[:, 2 * IW * k:2 * IW * (k + 1)],
                        lambda k: slot[:, WALL + 2 * IW * k:WALL + 2 * IW * (k + 1)]).then_inc(e_gu, 1)

            def t2(t, j):
                eng.wait_ge(e_h, t + 1)
                h_transposes(j).then_inc(e_t2, 1)

            def dn(t, j, slot):
                eng.wait_ge(e_te, t + 1)
                down(YP[j], htv(j), lambda k: slot[0:I2, DHI + D * k:DHI + D * (k + 1)],
                     lambda k: slot[0:I2, DLO + D * k:DLO + D * (k + 1)]).then_inc(tiles_done, 1)

            n = eng.value_load(TAB[0:1, COUNT], min_val=T_MIN // U, max_val=STEPS_MAX)
            def expert_of(t):
                return eng.value_load(TAB[0:1, ds(t + ET.start, 1)], min_val=0, max_val=E - 1)

            def expert_at(word, k):
                e = word % 64
                return e if k == 0 else e + word // (8 * 8 ** k) % 8

            e0 = [expert_of(t) for t in range(3)]
            t1(0, 16)
            t1(1, 16)
            gu(0, 0, e0[0])
            eng.wait_ge(e_xt, 1)
            t1(2, 16)
            gu(1, 1, e0[1])
            t2(0, 0)
            eng.wait_ge(e_xt, 2)
            t1(3, 16)
            eng.wait_ge(e_h, 1)
            gu(2, 0, e0[2])
            with eng.Fori(0, n * U, U) as m:
                word = eng.value_load(PACK[0:1, ds(m, 1)], min_val=0, max_val=2 ** 24 - 1)
                for j in range(U):
                    t2(m + (1 + j), (1 + j) % 2)
                    dn(m + j, j % 2, slot_of(expert_at(word, j)))
                    t1(j, m * 4 + 32)
                    e = eng.snap(expert_at(word, 3 + j))
                    gu(m + (3 + j), (3 + j) % 2, e)

        @block.vector
        def _(eng):
            links = [0]

            def link(x):
                links[0] += 1
                x.then_inc(chain, 1)
                eng.wait_ge(chain, links[0])

            def rsqrt(y, v, t, iv, n):
                link(eng.tensor_scalar(iv, v.bitcast(i32), 1, None, ALU.logical_shift_right))
                link(eng.tensor_scalar(y.bitcast(i32), iv, -1.0, float(0x5F3759DF), ALU.mult, ALU.add))
                for _ in range(4):
                    link(eng.tensor_tensor(t, y, y, ALU.mult))
                    link(eng.tensor_tensor(t, t, v, ALU.mult))
                    link(eng.tensor_scalar(t, t, -0.5, 1.5, ALU.mult, ALU.add))
                    link(eng.tensor_tensor(y, y, t, ALU.mult))

            def kt_evac(c):
                r = KR[c]
                for g in range(2):
                    n = 2 * c + g
                    eng.wait_ge(pe_kt, n + 1)
                    bank = BANKS[2 + n % 2].bitcast(bf16).rearrange("p (h q) -> p h q", h=8)
                    eng.tensor_copy(KTv[0:AUG, 8 * g:8 * g + 8, c * P:c * P + r], bank[0:AUG, :, 0:r]).then_inc(dve_kt, 1)

            def xn(t):
                if t >= 1:
                    eng.wait_ge(pe_xt, t)
                eng.tensor_scalar(XN, ACC[:, t, :], mv[:, t, 0:1], rs[:, t:t + 1], ALU.subtract,
                                  ALU.mult).then_inc(dve_xn, 1)

            def xnt(t):
                eng.wait_ge(pe_xt, t + 1)
                if t >= 1:
                    eng.wait_ge(pe_q, t)
                eng.tensor_copy(XNT, PVB[0][:, 0:D]).then_inc(dve_xt, 1)

            def key_residual(c):
                r = KR[c]
                ka = AUGT[c % 3][0:r]
                eng.wait_ge(act_v, 2 * c + 2)
                if c >= 2:
                    eng.wait_ge(dve_ka, c - 1)
                eng.tensor_tensor(R1[c % 2][0:r, :].rearrange("p (h d) -> p h d", h=NH),
                                  BANKS[c % 2][0:r, 0:D].rearrange("p (h d) -> p h d", h=NH),
                                  ka[:, :, DK:2 * DK], ALU.subtract).then_inc(dve_r1, 1)
                eng.tensor_reduce(KN[0:r, c, :], SQ[0:r, :].rearrange("p (h d) -> p h d", h=NH), AX.X,
                                  ALU.add).then_inc(dve_kn, 1)

            def key_third(c):
                r = KR[c]
                ka = AUGT[c % 3][0:r]
                eng.wait_ge(act_km, c + 1)
                eng.wait_ge(dve_r1, c + 1)
                eng.tensor_tensor(ka[:, :, 0:DK], R1[c % 2][0:r, :].rearrange("p (h d) -> p h d", h=NH),
                                  ka[:, :, 2 * DK:3 * DK], ALU.subtract).then_inc(dve_ka, 1)

            for c in range(KC):
                key_residual(c)
                if c >= 1:
                    key_third(c - 1)
                if c >= 2:
                    kt_evac(c - 2)
                if 1 <= c <= TT // 2:
                    eng.wait_ge(x_loaded, 16)
                    for t in (2 * c - 2, 2 * c - 1):
                        link(eng.bn_stats(stats[:, :], ACC[:, t, :]))
                        link(eng.bn_aggr(mv[:, t, :], stats[:, :]))
                if c == TT // 2 + 1:
                    link(eng.tensor_scalar(ve[:, :], mv[:, :, 1], EPS, None, ALU.add))
                    rsqrt(rs[:, :], ve[:, :], rt[:, :], ri[:, :], TT)
            xn(0)
            key_third(KC - 1)
            eng.wait_ge(dve_kn, KC)
            eng.tensor_reduce(kmax[:, :], KN[:, :, :].rearrange("p c h -> p h c"), AX.X, ALU.max).then_inc(dve_kn, 1)
            xnt(0)
            xn(1)
            kt_evac(KC - 2)
            kt_evac(KC - 1)

            def qt_evac(t):
                for g in range(2):
                    n = 2 * t + g
                    eng.wait_ge(pe_qt, n + 1)
                    bank = BANKS[2 + n % 2].bitcast(bf16).rearrange("p (h q) -> p h q", h=8)
                    eng.tensor_copy(QTv[0:AUG, t // TB, 8 * g:8 * g + 8, P * (t % TB):P * (t % TB + 1)],
                                    bank[0:AUG, :, :]).then_inc(dve_qt, 1)

            xnt(1)
            xn(2)
            eng.wait_ge(pool_kmax, 1)
            link(eng.tensor_scalar(knall[:, :], knall[:, :], -0.5 / DK ** 0.5, None, ALU.mult))
            for t in range(TT):
                eng.wait_ge(act_v, 2 * KC + t + 1)
                eng.tensor_reduce(qn[:, :], SQ.rearrange("p (h d) -> p h d", h=NH), AX.X, ALU.add).then_inc(dve_qn, 1)
                eng.wait_ge(dve_qn, t + 1)
                link(eng.scalar_tensor_tensor(out=NM[:, t, :], in0=qn[:, :], scalar=-0.5 * DK ** 0.5, in1=knall[:, :],
                                              op0=ALU.mult, op1=ALU.add))
                if t == 0:
                    eng.wait_ge(pe_kt, 2 * KC)
                if t >= 3:
                    eng.wait_ge(pe_qt, 2 * (t - 2))
                qa = AUGT[t % 3]
                link(eng.tensor_copy(qa[:, :, NT * DK], NM[:, t, :]))
                eng.tensor_tensor(qa[:, :, NT * DK + 1], NM[:, t, :], qa[:, :, NT * DK], ALU.subtract).then_inc(dve_m, 1)
                if t + 2 < TT:
                    xnt(t + 2)
                if t + 3 < TT:
                    xn(t + 3)
                if t >= 1:
                    qt_evac(t - 1)
            qt_evac(TT - 1)
            link(eng.tensor_reduce(shmax[:, 1:2], NM[:, :, :].rearrange("p t h -> p (t h)"), AX.X, ALU.min))
            eng.tensor_scalar(shmax[:, 0:1], shmax[:, 1:2], -1.0, None, ALU.mult).then_inc(dve_top, 1)
            eng.wait_ge(pool_top, 1)
            eng.tensor_scalar(flag[:, :], shmax[:, 1:2], SHIFT_MAX, None, ALU.is_gt).then_inc(dve_flag, 1)
            eng.wait_ge(dve_flag, 1)
            general = eng.value_load(flag[0:1, 0:1], min_val=0, max_val=1)
            with eng.If(general > 0):
                with eng.Fori(0, NB) as b:
                    for j in range(TB):
                        for h in range(NH):
                            eng.wait_ge(gen_s, b * (TB * NH) + (j * NH + h + 1))
                            eng.tensor_reduce(MROW[:, h:h + 1], SP4[:, 0:KV], AX.X, ALU.max).then_inc(gen_m, 1)
                        eng.wait_ge(gen_m, b * (TB * NH) + (j + 1) * NH)
                        eng.tensor_scalar(MROW, MROW, -1.0, None, ALU.mult).then_inc(gen_chain, 1)
                        eng.wait_ge(gen_chain, b * (2 * TB) + (2 * j + 1))
                        eng.tensor_copy(MHL[:, :, 0], MROW).then_inc(gen_chain, 1)
                        eng.wait_ge(gen_chain, b * (2 * TB) + (2 * j + 2))
                        eng.tensor_tensor(MHL[:, :, 1], MROW, MHL[:, :, 0], ALU.subtract).then_inc(gen_split, 1)
                        eng.wait_ge(gen_t, b * TB + (j + 1))
                        for g in range(2):
                            bank = BANKS[6 + g].bitcast(bf16)
                            x = eng.tensor_copy(QT[NT * DK:AUG, ds(b * (NH * QB) + 8 * g * QB, 8 * QB)]
                                                .rearrange("p (h q) -> p h q", h=8)[:, :, P * j:P * (j + 1)],
                                                bank[NT * DK:AUG, :].rearrange("p (h q) -> p h q", h=8))
                        x.then_inc(gen_qt, 1)
            eng.nop()

            def normalise(q):
                b, g = q // NG, q % NG
                eng.wait_ge(pe_pv, KC * (q + 1))
                if q >= 1:
                    eng.wait_ge(dve_attn, q)
                eng.tensor_copy(OS, PVB[q % 2][:, :]).then_inc(dve_pv, 1)
                eng.wait_ge(dve_pv, q + 1)
                link(eng.stream_shuffle(RS, OS, [DK] * 32))
                link(eng.reciprocal(RS, RS))
                eng.tensor_tensor(attnT(b, g), OS, RS, ALU.mult).then_inc(dve_attn, 1)

            def residual(i):
                eng.wait_ge(pe_op, i + 1)
                link(eng.scalar_tensor_tensor(out=ACC[:, i, :], in0=M0[:, 0:D], scalar=tg[:, 0:1], in1=ACC[:, i, :],
                                              op0=ALU.mult, op1=ALU.add))
                link(eng.bn_stats(stats[:, :], ACC[:, i, :]))
                link(eng.bn_aggr(mv[:, 0, :], stats[:, :]))
                link(eng.tensor_scalar(ve[:, 0:1], mv[:, 0, 1:2], EPS, None, ALU.add))
                rsqrt(rs[:, 0:1], ve[:, 0:1], rt[:, 0:1], ri[:, 0:1], 1)
                if i >= 1:
                    eng.wait_ge(pool_xr, 2 * i)
                    eng.wait_ge(pe_h2t, i)
                eng.tensor_scalar(H2S, ACC[:, i, :], mv[:, 0, 0:1], rs[:, 0:1], ALU.subtract, ALU.mult).then_inc(dve_h2, 1)
                eng.wait_ge(dve_h2, i + 1)

            def h2_parts(i):
                eng.wait_ge(pe_h2t, i + 1)
                if i >= 1:
                    eng.wait_ge(pe_lg, i)
                eng.tensor_copy(H2T, M0[:, D:2 * D]).then_inc(dve_h2t, 1)
                eng.wait_ge(dve_h2t, i + 1)
                h2 = h2T_cols(i)
                src = H2T.rearrange("p (c q) -> p c q", c=2)
                link(eng.tensor_copy(h2[:, 0:2, :], src))
                eng.tensor_tensor(h2[:, 2:4, :], src, h2[:, 0:2, :], ALU.subtract).then_inc(dve_hl, 1)
                eng.wait_ge(dve_hl, i + 1)

            A8v = A8.rearrange("p (k e) -> p k e", k=K8)
            PXv = PX.rearrange("p (k e) -> p k e", k=K8)

            def choose(i, ex=EX[:, :], sco=SCO[:, :]):
                eng.wait_ge(act_sig, i + 1)
                link(eng.tensor_scalar(CF[:, :], ex, 1.0, None, ALU.add))
                link(eng.reciprocal(sco, CF[:, :]))
                link(eng.tensor_tensor(CF[:, :], sco, bias[:, :], ALU.add))
                for g in range(8):
                    x = eng.max(G8[:, 8 * g:8 * g + 8], CF[:, 8 * g:8 * g + 8])
                link(x)
                g8 = G8[:, :].rearrange("p (g k) -> p g k", k=8)
                link(eng.tensor_tensor(GS[:, :], g8[:, :, 0], g8[:, :, 1], ALU.add))
                link(eng.max(T8[:, :], GS[:, :]))
                link(eng.max_index(I8[:, :], T8[:, :], GS[:, :]))
                link(eng.tensor_copy(F8[:, :], I8[:, :]))
                a4 = A8[:, 0:32].rearrange("p (g j) -> p g j", j=4)
                link(eng.tensor_tensor(a4, iota_e[:, 0:8].rearrange("p (g o) -> p g o", o=1).broadcast_to((P, 8, 4)),
                                       F8[:, 0:4].rearrange("p (o j) -> p o j", o=1).broadcast_to((P, 8, 4)), ALU.is_equal))
                link(eng.tensor_reduce(GM[:, :], a4, AX.X, ALU.add))
                cf = CF[:, :].rearrange("p (g k) -> p g k", k=8)
                link(eng.tensor_tensor(cf, cf, GM[:, :].rearrange("p (g o) -> p g o", o=1).broadcast_to((P, 8, 8)), ALU.mult))
                link(eng.tensor_scalar(CF[:, :], CF[:, :], 0.0, None, ALU.add))
                link(eng.max(T8[:, :], CF[:, :]))
                link(eng.max_index(I8[:, :], T8[:, :], CF[:, :]))
                link(eng.tensor_copy(F8[:, :], I8[:, :]))
                link(eng.tensor_copy(CHOSEN[:, i, :], F8[:, :]))
                link(eng.tensor_tensor(A8v, iota_e[:, :].rearrange("p (o e) -> p o e", o=1).broadcast_to((P, K8, E)),
                                       F8[:, :].rearrange("p (k o) -> p k o", o=1).broadcast_to((P, K8, E)), ALU.is_equal))
                if i >= 1:
                    eng.wait_ge(pe_rank, i)
                with nc.allow_low_precision("ones and zeros"):
                    eng.tensor_reduce(MK[:, :], A8v.rearrange("p k e -> p e k"), AX.X, ALU.add).then_inc(dve_mk, 1)
                eng.wait_ge(dve_mk, i + 1)

            def place(i, rank=M1[:, E:2 * E]):
                eng.wait_ge(pe_rank, i + 1)
                link(eng.tensor_tensor(POS[:, :], rank, base_e[:, :], ALU.add))
                eng.tensor_tensor(MSUM[:, :], MSUM[:, :], MK[:, :], ALU.add).then_inc(dve_msum, 1)
                eng.wait_ge(dve_msum, i + 1)
                link(eng.tensor_tensor(PXv, A8v, POS[:, :].rearrange("p (o e) -> p o e", o=1).broadcast_to((P, K8, E)), ALU.mult))
                link(eng.tensor_reduce(W8[:, :], PXv, AX.X, ALU.add))
                eng.tensor_copy(IDX[:, i, :], W8[:, :]).then_inc(dve_idx, 1)
                eng.wait_ge(dve_idx, i + 1)

            def weigh(i, sco=SCO[:, :]):
                link(eng.tensor_tensor(PXv, A8v, sco.rearrange("p (o e) -> p o e", o=1).broadcast_to((P, K8, E)), ALU.mult))
                link(eng.tensor_reduce(W8[:, :], PXv, AX.X, ALU.add))
                link(eng.tensor_reduce(W1[:, 0:1], W8[:, :], AX.X, ALU.add))
                link(eng.tensor_scalar(W1[:, 0:1], W1[:, 0:1], 1e-20, None, ALU.add))
                link(eng.reciprocal(W1[:, 1:2], W1[:, 0:1]))
                link(eng.tensor_scalar(W8[:, :], W8[:, :], W1[:, 1:2], SCALE_OUT, ALU.mult, ALU.mult))
                link(eng.tensor_scalar(WK[:, i, :], W8[:, :], tg[:, 1:2], None, ALU.mult))

            eng.wait_ge(gates_done, 1)
            eng.wait_ge(pe_qt, 2 * TT)
            eng.wait_ge(pool_ql, TT)
            for b in range(NB):
                i = (b - 1) * TB
                if b >= 1:
                    residual(i)
                    h2_parts(i)
                    choose(i)
                    residual(i + 1)
                normalise(b * NG)
                if b >= 1:
                    place(i)
                    weigh(i)
                    h2_parts(i + 1)
                    choose(i + 1)
                    residual(i + 2)
                    place(i + 1)
                    weigh(i + 1)
                    h2_parts(i + 2)
                    choose(i + 2)
                normalise(b * NG + 1)
                if b >= 1:
                    residual(i + 3)
                    place(i + 2)
                    weigh(i + 2)
                    h2_parts(i + 3)
                    choose(i + 3)
                normalise(b * NG + 2)
                if b >= 1:
                    place(i + 3)
                    weigh(i + 3)
                normalise(b * NG + 3)
            def hidden(j):
                return eng.tensor_tensor(HF[j], SIL[j], GUP[j][:, IW:2 * IW], ALU.mult)

            def shared_sum(i):
                eng.wait_ge(sh_y, i + 1)
                eng.scalar_tensor_tensor(out=ACC[:, i, :], in0=SHY, scalar=tg[:, 1:2], in1=ACC[:, i, :],
                                         op0=ALU.mult, op1=ALU.add).then_inc(sh_ye, 1)

            def shared(i):
                for s in range(2):
                    eng.wait_ge(sh_sil, 2 * i + s + 1)
                    link(hidden(s))
                    if i >= 1:
                        eng.wait_ge(sh_t, 2 * (i - 1) + s + 1)
                    link(eng.tensor_copy(HHL[s][:, 0, :], HF[s]))
                    eng.tensor_tensor(HHL[s][:, 1, :], HF[s], HHL[s][:, 0, :], ALU.subtract).then_inc(sh_h, 1)
                if i >= 1:
                    shared_sum(i - 1)

            eng.wait_ge(pool_xr, 2 * (TT - TB))
            eng.wait_ge(pe_h2t, TT - TB)
            LAST = range(TT - TB, TT)
            eng.wait_ge(pe_op, TT)
            for j, i in enumerate(LAST):
                link(eng.scalar_tensor_tensor(out=ACC[:, i, :], in0=OPL[j], scalar=tg[:, 0:1], in1=ACC[:, i, :],
                                              op0=ALU.mult, op1=ALU.add))
                link(eng.bn_stats(stats[:, :], ACC[:, i, :]))
                link(eng.bn_aggr(mv[:, j, :], stats[:, :]))
            link(eng.tensor_scalar(ve[:, 0:TB], mv[:, 0:TB, 1], EPS, None, ALU.add))
            rsqrt(rs[:, 0:TB], ve[:, 0:TB], rt[:, 0:TB], ri[:, 0:TB], TB)
            for j, i in enumerate(LAST):
                eng.tensor_scalar(H2L[j], ACC[:, i, :], mv[:, j, 0:1], rs[:, j:j + 1], ALU.subtract,
                                  ALU.mult).then_inc(dve_h2, 1)
            shared(0)
            shared(1)
            eng.wait_ge(pe_h2t, TT)
            for j, i in enumerate(LAST):
                eng.tensor_copy(H2TL[j], OPL[j]).then_inc(dve_h2t, 1)
                eng.wait_ge(dve_h2t, i + 1)
                h2 = h2T_cols(i)
                src = H2TL[j].rearrange("p (c q) -> p c q", c=2)
                link(eng.tensor_copy(h2[:, 0:2, :], src))
                eng.tensor_tensor(h2[:, 2:4, :], src, h2[:, 0:2, :], ALU.subtract).then_inc(dve_hl, 1)
            shared(2)
            shared(3)
            for j, i in enumerate(LAST):
                choose(i, EXL[j], SCOL[j])
                shared(4 + 2 * j)
                place(i, OPL[j][:, 0:E])
                shared(5 + 2 * j)

            eng.wait_ge(pe_tab, 1)
            link(eng.tensor_copy(cnt[:, :], M0[0:E, 0:1]))
            link(eng.tensor_scalar(cti[:, :], cnt[:, :], float(P - 1), None, ALU.add))
            link(eng.tensor_scalar(cti[:, :], cti[:, :], 7, None, ALU.logical_shift_right))
            link(eng.tensor_copy(ctf[:, :], cti[:, :]))
            link(eng.tensor_scalar(ctf[:, :], ctf[:, :], 1.0, None, ALU.max))
            eng.tensor_scalar(CTB, ones_b[0:E, :], ctf[:, 0:1], None, ALU.mult).then_inc(chain_tab, 1)
            shared(12)
            shared(13)
            eng.wait_ge(pe_tab, 2)
            link(eng.tensor_copy(cum[:, :], M0[0:E, 8:9]))
            link(eng.scalar_tensor_tensor(out=DELTA, in0=M0[:, 384:384 + E], scalar=float(P), in1=base_e[:, :],
                                          op0=ALU.mult, op1=ALU.subtract))
            eng.tensor_tensor(TAB[0:1, PADR.start:PADR.start + E], M0[0:1, 64:64 + E], base_e[0:1, :], ALU.add)\
               .then_inc(dve_pad, 1)
            eng.tensor_scalar(A8[0:E, 0:NTAB], iota_t[:, :], cum[:, 0:1], None, ALU.is_ge).then_inc(chain_tab, 1)
            shared(14)
            eng.wait_ge(pe_tab, 3)
            tf = TABF
            link(eng.tensor_copy(tf[0:1, ET], M1[0:1, 0:NTAB]))
            link(eng.scalar_tensor_tensor(out=tf[0:1, RT], in0=M1[0:1, 256:256 + NTAB], scalar=-1.0, in1=iota_t[0:1, :],
                                          op0=ALU.mult, op1=ALU.add))
            link(eng.tensor_scalar(tf[0:1, SPARE], tf[0:1, ET], float(REGION), None, ALU.mult))
            link(eng.scalar_tensor_tensor(out=TAB[0:1, RT], in0=tf[0:1, RT], scalar=float(P), in1=tf[0:1, SPARE],
                                          op0=ALU.mult, op1=ALU.add))
            link(eng.tensor_scalar(TAB[0:1, RT], TAB[0:1, RT], float(E * REGION), None, ALU.min))
            link(eng.tensor_scalar(TAB[0:1, COUNT], M1[0:1, 255 + NTAB:256 + NTAB], float(U - 1), None, ALU.add))
            eng.tensor_scalar(TAB[0:1, COUNT], TAB[0:1, COUNT], U.bit_length() - 1, None,
                              ALU.logical_shift_right).then_inc(dve_rows, 1)
            shared(15)
            link(eng.tensor_scalar(TAB[0:1, ET], tf[0:1, ET], float(E - 1), None, ALU.min))
            by4 = TAB[0:1, ET].rearrange("o (i k) -> o i k", k=U)
            m = NTAB // U - 1
            gap = TABF[:, 3 * NTAB:3 * NTAB + 6 * m].rearrange("o (k i) -> o k i", k=6)
            for k in range(1, 7):
                x = eng.tensor_tensor(gap[:, k - 1, :], by4[:, k // U:m + k // U, k % U], by4[:, 0:m, 0], ALU.subtract)
            link(x)
            for k in range(5, 0, -1):
                link(eng.scalar_tensor_tensor(out=gap[:, k - 1, :], in0=gap[:, k, :], scalar=8.0, in1=gap[:, k - 1, :],
                                              op0=ALU.mult, op1=ALU.add))
            link(eng.memset(PACK, 0))
            link(eng.scalar_tensor_tensor(out=PACK.rearrange("o (i k) -> o i k", k=U)[:, 0:m, 0], in0=gap[:, 0, :], scalar=64.0,
                                          in1=by4[:, 0:m, 0], op0=ALU.mult, op1=ALU.add))
            link(eng.memset(TAB[0:1, WAITC.start:WAITC.start + NSLOT], 1))
            eng.tensor_scalar(TAB[0:1, WAITC.start + NSLOT:WAITC.start + E], M0[0:1, 256:256 + E - NSLOT], 1.0, None,
                              ALU.add).then_inc(dve_tab, 1)
            eng.wait_ge(dve_tab, 1)
            shared_sum(TT - 1)

            def result_rows(i):
                link(eng.tensor_tensor(A8v, iota_e[:, :].rearrange("p (o e) -> p o e", o=1).broadcast_to((P, K8, E)),
                                       CHOSEN[:, i, :].rearrange("p (k o) -> p k o", o=1).broadcast_to((P, K8, E)), ALU.is_equal))
                link(eng.tensor_tensor(PXv, A8v, DELTA.rearrange("p (o e) -> p o e", o=1).broadcast_to((P, K8, E)), ALU.mult))
                link(eng.tensor_reduce(W8[:, :], PXv, AX.X, ALU.add))
                eng.tensor_tensor(IDX2[:, i, :], IDX[:, i, :], W8[:, :], ALU.add).then_inc(dve_idx2, 1)
                eng.wait_ge(dve_idx2, i + 1)
                if i >= TT - TB:
                    weigh(i, SCOL[i - (TT - TB)])

            def xt_evac(t, j):
                eng.wait_ge(e_t1, t + 1)
                eng.tensor_copy(XT[j], XTP[j]).then_inc(e_xt, 1)

            def h_split(t, j, link_to):
                eng.wait_ge(e_sil, t + 1)
                hidden(j).then_inc(e_link, 1)
                eng.wait_ge(e_link, link_to)
                eng.tensor_copy(HHL[j][:, 0, :], HF[j]).then_inc(e_link, 1)
                eng.wait_ge(e_link, link_to + 1)
                eng.tensor_tensor(HHL[j][:, 1, :], HF[j], HHL[j][:, 0, :], ALU.subtract).then_inc(e_h, 1)

            n = eng.value_load(TAB[0:1, COUNT], min_val=T_MIN // U, max_val=STEPS_MAX)
            xt_evac(0, 0)
            xt_evac(1, 1)
            h_split(0, 0, 1)
            eng.wait_ge(e_gu, 1)
            xt_evac(2, 0)
            h_split(1, 1, 3)
            with eng.Fori(0, n * U, U) as m:
                for j in range(U):
                    eng.wait_ge(e_gu, m + (2 + j))
                    xt_evac(m + (3 + j), (3 + j) % 2)
                    eng.wait_ge(e_t2, m + (1 + j))
                    h_split(m + (2 + j), j % 2, m * 2 + (5 + 2 * j))

            result_rows(0)
            result_rows(1)
            for i in range(TT):
                if i + 2 < TT:
                    result_rows(i + 2)
                for k in range(K8):
                    r = i % 2 * K8 + k
                    eng.wait_ge(gathered[r], 16 * (i // 2 + 1))
                    if k >= 1 or i >= 1:
                        eng.wait_ge(dve_comb, K8 * i + k)
                    eng.scalar_tensor_tensor(out=ACC[:, i, :], in0=RING[:, r, :], scalar=WK[:, i, k:k + 1],
                                             in1=ACC[:, i, :], op0=ALU.mult, op1=ALU.add).then_inc(dve_comb, 1)


def kernel(x, ctx_1024, g_xattn, g_ffn, L0_xattn_w_q, L0_xattn_w_k, L0_xattn_w_v, L0_xattn_w_o, L0_ffn_gate_w,
           L0_ffn_gate_bias, L0_ffn_Wg, L0_ffn_Wu, L0_ffn_Wd, L0_ffn_Sg, L0_ffn_Su, L0_ffn_Sd):
    import numpy as np
    import concourse.bacc as bacc
    from concourse.bass_utils import run_bass_kernel_spmd

    a = np.asarray
    S, D = x.shape[1], x.shape[2]
    E, IW = L0_ffn_Wg.shape[0], L0_ffn_Wg.shape[1]
    I2 = IW // 2

    def chunks(w):
        w = a(w)
        return w.reshape(w.shape[0] // 128, 128, w.shape[1]).transpose(1, 0, 2)

    wo = np.zeros((4, 4, 32, D), np.float32)
    wo[:, :, 0:16, :] = a(L0_xattn_w_o).T.reshape(4, 4, 16, D)
    gate = np.concatenate([a(L0_ffn_Wg), a(L0_ffn_Sg).reshape(2, IW, D)])
    up = np.concatenate([a(L0_ffn_Wu), a(L0_ffn_Su).reshape(2, IW, D)])
    gu = np.concatenate([gate, up], axis=1)
    wgu = gu.transpose(0, 2, 1).reshape(E + 2, 2, 128, 2 * IW).transpose(0, 2, 1, 3).reshape(E + 2, 128, 4 * IW)
    down = np.concatenate([a(L0_ffn_Wd), a(L0_ffn_Sd).reshape(D, 2, IW).transpose(1, 0, 2)])
    wd = down.transpose(0, 2, 1).reshape(E + 2, 2, I2, D).transpose(0, 2, 1, 3).reshape(E + 2, I2, 2 * D)
    w = np.zeros((E + 2, 128, 4 * IW + 2 * D), np.float32)
    w[:, :, 0:4 * IW] = wgu
    w[:, 0:I2, 4 * IW:] = wd
    arrays = {
        "x": a(x).reshape(S, D),
        "ctxT": chunks(a(ctx_1024)[0].T),
        "wq": chunks(a(L0_xattn_w_q).T),
        "wkv": chunks(np.concatenate([a(L0_xattn_w_k), a(L0_xattn_w_v)]).T),
        "wo": wo.reshape(4, 128, D).transpose(1, 0, 2),
        "router": chunks(a(L0_ffn_gate_w).T),
        "bias": a(L0_ffn_gate_bias).reshape(1, E),
        "gates": np.concatenate([a(g_xattn).reshape(1), a(g_ffn).reshape(1)]).reshape(1, 2),
        "w": w,
    }
    arrays = {"in_" + k: np.ascontiguousarray(v) for k, v in arrays.items()}
    nc = bacc.Bacc("TRN2", target_bir_lowering=False, num_devices=1)
    args = [nc.dram_tensor(k, v.shape, mybir.dt.from_np(v.dtype), kind="ExternalInput").ap() for k, v in arrays.items()]
    args.append(nc.dram_tensor("out", (S, D), mybir.dt.float32, kind="ExternalOutput").ap())
    flamingo_gated_block(nc, *args)
    r = run_bass_kernel_spmd(nc, [arrays], core_ids=[0])
    return r.results[0]["out"].reshape(x.shape)
```
